# Optimizing a Trainium2 kernel written in Bass

```python
import numpy as np
import jax
import jax.numpy as jnp

def _softmax(x, axis=-1):
    return jax.nn.softmax(x, axis=axis)

def _gelu(x):
    return jax.nn.gelu(x, approximate=True)

def _silu(x):
    return jax.nn.silu(x)

def _sigmoid(x):
    return jax.nn.sigmoid(x)

def _layernorm(x, axis=-1, eps=1e-05):
    m = jnp.mean(x, axis=axis, keepdims=True)
    v = jnp.var(x, axis=axis, keepdims=True)
    return (x - m) / jnp.sqrt(v + eps)

def _scatter_add(tgt, idx, src, axis=0):
    return tgt.at[idx].add(src)

def _segment_sum(src, seg, n):
    return jax.ops.segment_sum(src, seg, n)
kernel_name = 'mk_flamingo_gated_d2_seqx_r4_7173f2'

def setup_inputs(seed: int=0):
    np.random.seed(seed)
    _w = jnp.asarray

    def _rec_inputs():
        import jax
        import jax.numpy as jnp
        _rk = jax.random.key(seed)
        x = -0.000125 + 0.9999 * jax.random.normal(jax.random.fold_in(_rk, 1), (16, 128, 256), jnp.float32)
        _lenS = 128 - jax.random.randint(jax.random.fold_in(_rk, 7), (16,), 0, max(1, 128 // 4) + 1, jnp.int32)
        _lenS2 = 128 - jax.random.randint(jax.random.fold_in(_rk, 8), (16,), 0, max(1, 128 // 4) + 1, jnp.int32)
        _ctx_1024P = jax.random.normal(jax.random.fold_in(_rk, 11), (16, 16, 256), jnp.float32)
        _ctx_1024c = jax.random.dirichlet(jax.random.fold_in(_rk, 511), 0.3 * jnp.ones((16,), jnp.float32), (16, 128))
        _ctx_1024t = jnp.einsum('bsk,bkd->bsd', _ctx_1024c, _ctx_1024P)
        _ctx_1024t = _ctx_1024t * jax.lax.rsqrt(jnp.mean(jnp.square(_ctx_1024t)) + 1e-12) * 0.953939
        ctx_1024 = -1.52775e-05 + 0.999936 * (_ctx_1024t + 0.3 * jax.random.normal(jax.random.fold_in(_rk, 611), (16, 128, 256), jnp.float32))
        _validS = jnp.arange(128)[None, :] < _lenS[:, None]
        _validS2 = jnp.arange(128)[None, :] < _lenS2[:, None]
        _causal = jnp.tril(jnp.ones((128, 128), dtype=bool))
        mask_Bx1xS2_bk0 = jnp.logical_not(jnp.broadcast_to(_validS2[:, None, :], (16, 1, 128)))
        _g = jax.random.normal(jax.random.fold_in(_rk, 9001), (2, 2), jnp.float32)
        _g = jnp.sign(_g) * jnp.maximum(jnp.abs(_g), 1.0) + (_g == 0) * 1.0
        g_xattn = _g[0]
        g_ffn = _g[1]
        return (x, ctx_1024, mask_Bx1xS2_bk0, g_xattn, g_ffn)
    x, ctx_1024, mask_Bx1xS2_bk0, g_xattn, g_ffn = _rec_inputs()

    def _L0_xattn_setup():
        import jax, jax.numpy as jnp
        import numpy as np
        DECAY = 0.9
        key = jax.random.key(seed)
        k1, k2, k3 = jax.random.split(key, 3)
        B, S, D = (8, 1024, 256)
        q = jax.random.normal(k1, (B, S, D), dtype=jnp.float32)
        k = jax.random.normal(k2, (B, S, D), dtype=jnp.float32)
        v = jax.random.normal(k3, (B, S, D), dtype=jnp.float32)
        return {'q': q, 'k': k, 'v': v}
    _L0_xattn_all = _L0_xattn_setup()
    _L0_xattn_in = {k: v for k, v in _L0_xattn_all.items() if k in ()}
    del _L0_xattn_all

    def _L0_ffn_setup():
        import math
        import jax, jax.numpy as jnp
        import numpy as np
        B, T, H = (4, 512, 256)
        E, K, F = (8, 2, 512)
        CAP_FACTOR = 1.25

        def _moe_forward(x, Wg, W_in, W_out):
            b, t, h = x.shape
            xf = x.reshape(-1, h)
            S = xf.shape[0]
            C = int(math.ceil(K * S / E * CAP_FACTOR))
            logits = xf @ Wg
            probs = jax.nn.softmax(logits, axis=-1)
            top_vals, top_idx = jax.lax.top_k(probs, K)
            flat_idx = top_idx.T.reshape(-1)
            onehot = jax.nn.one_hot(flat_idx, E, dtype=jnp.int32)
            cum = jnp.cumsum(onehot, axis=0) - 1
            loc = jnp.take_along_axis(cum, flat_idx[:, None], axis=1)[:, 0]
            loc = loc.reshape(K, S).T
            keep = loc < C
            gates = top_vals * keep.astype(top_vals.dtype)
            denom = jnp.maximum(gates.sum(-1, keepdims=True), 1e-09)
            gates = gates / denom
            loc_c = jnp.where(keep, loc, C)
            e_flat = top_idx.reshape(-1)
            l_flat = loc_c.reshape(-1)
            xk = jnp.broadcast_to(xf[:, None, :], (S, K, h)).reshape(-1, h)
            xk = jnp.where(keep.reshape(-1, 1), xk, 0.0)
            buf = jnp.zeros((E, C + 1, h), x.dtype).at[e_flat, l_flat].set(xk)
            inp = buf[:, :C]
            hid = jnp.einsum('ech,ehf->ecf', inp, W_in)
            a, g = jnp.split(hid, 2, axis=-1)
            hid = jax.nn.gelu(a, approximate=False) * g
            out_e = jnp.einsum('ecf,efh->ech', hid, W_out)
            out_pad = jnp.concatenate([out_e, jnp.zeros((E, 1, h), out_e.dtype)], axis=1)
            gathered = out_pad[e_flat, l_flat].reshape(S, K, h)
            y = (gathered * gates[..., None]).sum(axis=1)
            return y.reshape(b, t, h)
        key = jax.random.key(seed)
        k1, k2, k3, k4 = jax.random.split(key, 4)
        x = jax.random.normal(k1, (B, T, H), dtype=jnp.float32)
        Wg = jax.random.normal(k2, (H, E), dtype=jnp.float32) * 0.02
        W_in = jax.random.normal(k3, (E, H, 2 * F), dtype=jnp.float32) * (1.0 / math.sqrt(H))
        W_out = jax.random.normal(k4, (E, F, H), dtype=jnp.float32) * (1.0 / math.sqrt(F))
        return {'x': x, 'Wg': Wg, 'W_in': W_in, 'W_out': W_out}
    _L0_ffn_all = _L0_ffn_setup()
    _L0_ffn_in = {k: v for k, v in _L0_ffn_all.items() if k in ('Wg', 'W_in', 'W_out')}
    del _L0_ffn_all

    def _L1_xattn_setup():
        import jax, jax.numpy as jnp
        import numpy as np
        B, S, E, D = (4, 512, 256, 256)
        NEG_INF = float('-inf')
        key = jax.random.key(seed)
        ks = jax.random.split(key, 10)
        query = jax.random.normal(ks[0], (B, S, E), dtype=jnp.float32)
        key_t = jax.random.normal(ks[1], (B, S, E), dtype=jnp.float32)
        value = jax.random.normal(ks[2], (B, S, E), dtype=jnp.float32)
        sc = 1.0 / np.sqrt(E)
        Wq = jax.random.uniform(ks[3], (D, E), jnp.float32, -sc, sc)
        bq = jax.random.uniform(ks[4], (D,), jnp.float32, -sc, sc)
        Wk = jax.random.uniform(ks[5], (D, E), jnp.float32, -sc, sc)
        bk = jax.random.uniform(ks[6], (D,), jnp.float32, -sc, sc)
        Wv = jax.random.uniform(ks[7], (D, E), jnp.float32, -sc, sc)
        bv = jax.random.uniform(ks[8], (D,), jnp.float32, -sc, sc)
        lengths = jax.random.randint(ks[9], (B, 1, 1), 1, S + 1)
        pos = jnp.arange(S)[None, None, :]
        padding_mask = pos >= lengths
        return {'query': query, 'key': key_t, 'value': value, 'Wq': Wq, 'bq': bq, 'Wk': Wk, 'bk': bk, 'Wv': Wv, 'bv': bv, 'padding_mask': padding_mask, 'look_ahead_mask': 1}
    _L1_xattn_all = _L1_xattn_setup()
    _L1_xattn_in = {k: v for k, v in _L1_xattn_all.items() if k in ('Wq', 'bq', 'Wk', 'bk', 'Wv', 'bv')}
    del _L1_xattn_all

    def _L1_ffn_setup():
        import jax, jax.numpy as jnp
        import numpy as np
        K = 2
        key = jax.random.key(seed)
        k1, k2, k3, k4 = jax.random.split(key, 4)
        B, S, D, E, F = (2, 256, 256, 8, 1024)
        x = jax.random.normal(k1, (B, S, D), dtype=jnp.float32)
        gate_w = jax.random.normal(k2, (E, D), dtype=jnp.float32) * (1.0 / np.sqrt(D))
        w1 = jax.random.normal(k3, (E, D, F), dtype=jnp.float32) * (1.0 / np.sqrt(D))
        w2 = jax.random.normal(k4, (E, F, D), dtype=jnp.float32) * (1.0 / np.sqrt(F))
        return {'x': x, 'gate_w': gate_w, 'w1': w1, 'w2': w2}
    _L1_ffn_all = _L1_ffn_setup()
    _L1_ffn_in = {k: v for k, v in _L1_ffn_all.items() if k in ('gate_w', 'w1', 'w2')}
    del _L1_ffn_all
    return {'x': x, 'ctx_1024': ctx_1024, 'mask_Bx1xS2_bk0': mask_Bx1xS2_bk0, 'g_xattn': g_xattn, 'g_ffn': g_ffn, 'L0_ffn_Wg': _L0_ffn_in['Wg'], 'L0_ffn_W_in': _L0_ffn_in['W_in'], 'L0_ffn_W_out': _L0_ffn_in['W_out'], 'L1_xattn_Wq': _L1_xattn_in['Wq'], 'L1_xattn_bq': _L1_xattn_in['bq'], 'L1_xattn_Wk': _L1_xattn_in['Wk'], 'L1_xattn_bk': _L1_xattn_in['bk'], 'L1_xattn_Wv': _L1_xattn_in['Wv'], 'L1_xattn_bv': _L1_xattn_in['bv'], 'L1_ffn_gate_w': _L1_ffn_in['gate_w'], 'L1_ffn_w1': _L1_ffn_in['w1'], 'L1_ffn_w2': _L1_ffn_in['w2']}

def reference(x, ctx_1024, mask_Bx1xS2_bk0, g_xattn, g_ffn, L0_ffn_Wg, L0_ffn_W_in, L0_ffn_W_out, L1_xattn_Wq, L1_xattn_bq, L1_xattn_Wk, L1_xattn_bk, L1_xattn_Wv, L1_xattn_bv, L1_ffn_gate_w, L1_ffn_w1, L1_ffn_w2):
    import jax
    import jax.numpy as jnp

    def _L0_xattn_ref(q, k, v):
        import jax, jax.numpy as jnp
        import numpy as np
        DECAY = 0.9
        kv = jnp.swapaxes(k * v, 0, 1)

        def step(r, kv_t):
            r = DECAY * r + kv_t
            return (r, r)
        r0 = jnp.zeros(q.shape[:1] + q.shape[2:], dtype=q.dtype)
        _, rs = jax.lax.scan(step, r0, kv)
        return q * jnp.swapaxes(rs, 0, 1)

    def _L0_ffn_ref(x, Wg, W_in, W_out):
        import math
        import jax, jax.numpy as jnp
        import numpy as np
        B, T, H = (4, 512, 256)
        E, K, F = (8, 2, 512)
        CAP_FACTOR = 1.25

        def _moe_forward(x, Wg, W_in, W_out):
            b, t, h = x.shape
            xf = x.reshape(-1, h)
            S = xf.shape[0]
            C = int(math.ceil(K * S / E * CAP_FACTOR))
            logits = xf @ Wg
            probs = jax.nn.softmax(logits, axis=-1)
            top_vals, top_idx = jax.lax.top_k(probs, K)
            flat_idx = top_idx.T.reshape(-1)
            onehot = jax.nn.one_hot(flat_idx, E, dtype=jnp.int32)
            cum = jnp.cumsum(onehot, axis=0) - 1
            loc = jnp.take_along_axis(cum, flat_idx[:, None], axis=1)[:, 0]
            loc = loc.reshape(K, S).T
            keep = loc < C
            gates = top_vals * keep.astype(top_vals.dtype)
            denom = jnp.maximum(gates.sum(-1, keepdims=True), 1e-09)
            gates = gates / denom
            loc_c = jnp.where(keep, loc, C)
            e_flat = top_idx.reshape(-1)
            l_flat = loc_c.reshape(-1)
            xk = jnp.broadcast_to(xf[:, None, :], (S, K, h)).reshape(-1, h)
            xk = jnp.where(keep.reshape(-1, 1), xk, 0.0)
            buf = jnp.zeros((E, C + 1, h), x.dtype).at[e_flat, l_flat].set(xk)
            inp = buf[:, :C]
            hid = jnp.einsum('ech,ehf->ecf', inp, W_in)
            a, g = jnp.split(hid, 2, axis=-1)
            hid = jax.nn.gelu(a, approximate=False) * g
            out_e = jnp.einsum('ecf,efh->ech', hid, W_out)
            out_pad = jnp.concatenate([out_e, jnp.zeros((E, 1, h), out_e.dtype)], axis=1)
            gathered = out_pad[e_flat, l_flat].reshape(S, K, h)
            y = (gathered * gates[..., None]).sum(axis=1)
            return y.reshape(b, t, h)
        return _moe_forward(x, Wg, W_in, W_out)

    def _L1_xattn_ref(query, key, value, Wq, bq, Wk, bk, Wv, bv, padding_mask, look_ahead_mask):
        import jax, jax.numpy as jnp
        import numpy as np
        B, S, E, D = (4, 512, 256, 256)
        NEG_INF = float('-inf')
        q = query @ Wq.T + bq
        k = key @ Wk.T + bk
        v = value @ Wv.T + bv
        scale = jnp.sqrt(jnp.asarray(q.shape[-1], q.dtype))
        qk = jnp.einsum('bqd,bkd->bqk', q, k) / scale
        if padding_mask is not None:
            qk = jnp.where(padding_mask, NEG_INF, qk)
        if look_ahead_mask:
            causal = jnp.where(jnp.tril(jnp.ones((q.shape[1], k.shape[1]), dtype=bool)), jnp.asarray(0.0, qk.dtype), jnp.asarray(NEG_INF, qk.dtype))
            qk = qk + causal
        attn = jax.nn.softmax(qk, axis=-1)
        return jnp.einsum('bqk,bkd->bqd', attn, v)

    def _L1_ffn_ref(x, gate_w, w1, w2):
        import jax, jax.numpy as jnp
        import numpy as np
        K = 2
        D = x.shape[-1]
        xt = x.reshape(-1, D)
        T = xt.shape[0]
        E = gate_w.shape[0]
        logits = jnp.einsum('td,ed->te', xt, gate_w)
        w_topk, sel = jax.lax.top_k(logits, K)
        w_topk = jax.nn.softmax(w_topk.astype(jnp.float32), axis=-1).astype(x.dtype)
        combine = jnp.zeros((T, E), dtype=x.dtype)
        combine = combine.at[jnp.arange(T)[:, None], sel].add(w_topk)
        h = jax.nn.silu(jnp.einsum('td,edf->tef', xt, w1))
        y = jnp.einsum('tef,efd->ted', h, w2)
        out = jnp.einsum('ted,te->td', y, combine)
        return out.reshape(x.shape)
    x = x + jnp.tanh(g_xattn[0]) * _L0_xattn_ref(_layernorm(x, axis=-1), ctx_1024, ctx_1024)
    x = x + jnp.tanh(g_ffn[0]) * _L0_ffn_ref(_layernorm(x, axis=-1), L0_ffn_Wg, L0_ffn_W_in, L0_ffn_W_out)
    x = x + jnp.tanh(g_xattn[1]) * _L1_xattn_ref(_layernorm(x, axis=-1), ctx_1024, ctx_1024, L1_xattn_Wq, L1_xattn_bq, L1_xattn_Wk, L1_xattn_bk, L1_xattn_Wv, L1_xattn_bv, mask_Bx1xS2_bk0, 1)
    x = x + jnp.tanh(g_ffn[1]) * _L1_ffn_ref(_layernorm(x, axis=-1), L1_ffn_gate_w, L1_ffn_w1, L1_ffn_w2)
    return x

_drawn_inputs = setup_inputs


def setup_inputs(seed=0):
    import zlib

    import numpy as np

    out = dict(_drawn_inputs(seed))
    spreads = {'g_ffn': (-1.0, 0.6)}
    factors = {'L1_xattn_Wq': 8.0,
     'L1_xattn_bq': 38.606,
     'L1_xattn_Wk': 8.0,
     'L1_xattn_bk': 64.0,
     'L1_xattn_bv': 8.0}
    for name, (base, spread) in spreads.items():
        noise = np.random.default_rng([zlib.crc32(name.encode()), seed]).standard_normal(out[name].shape)
        drawn = base * np.exp(spread * noise) if base else spread * noise
        out[name] = jnp.asarray(drawn.astype(out[name].dtype))
    for name, factor in factors.items():
        out[name] = (out[name] * factor).astype(out[name].dtype)
    return out
```

```python
import math
from contextlib import ExitStack

import numpy as np

import concourse.bass as bass
from concourse import mybir

ALU = mybir.AluOpType
ACT = mybir.ActivationFunctionType
AX = mybir.AxisListType
F32 = mybir.dt.float32
BF16 = mybir.dt.bfloat16
I32 = mybir.dt.int32
U32 = mybir.dt.uint32
U8 = mybir.dt.uint8

P = 128
NB, S, D = 16, 128, 256
T = NB * S
DC = D // P
E, K = 8, 2
QB = 4
NQ = NB // QB
QN = QB * P
NG = K * NB
F0 = 512
F1 = 1024
CAP = math.ceil(K * T / E * 1.25)
CT = CAP // P
TILES0 = E * CT
TILES1 = K * T // P + E - 1
NA = max(TILES0, TILES1 + 1)
HALF = CAP // 2
FB0 = F0 // P
FB1 = F1 // P
STEPS0 = 2 * FB0
LN_EPS = 1e-5
NEG = -1.0e30
WSET = 4096
WIN0 = DC * 2 * F0
WIN1 = DC * F1
SCALE = 1.0 / math.sqrt(D)

_at, CF = 0, {}
for _n, _w in (("ident", P), ("decay", P), ("causal", P), ("reset", E * NG), ("iota_e", E), ("iota_a", NA),
               ("trash", NA), ("part", 1), ("eps", 1), ("group1", NG),
               ("before", P), ("ones", P), ("iota", P)):
    CF[_n] = (_at, _at + _w)
    _at += _w
CF_W = _at
CB = {"before": (0, P), "ones": (P, 2 * P), "iota": (2 * P, 3 * P)}


def constants():
    f = np.zeros((P, CF_W), np.float32)
    r = np.arange(P)

    def put(name, value):
        f[:, slice(*CF[name])] = value

    put("ident", np.eye(P))
    lag = r[None, :] - r[:, None]
    put("decay", np.where(lag >= 0, np.float64(np.float32(0.9)) ** np.maximum(lag, 0), 0.0))
    put("causal", np.where(r[None, :] <= r[:, None], 0.0, NEG))
    put("reset", np.tile(np.arange(NG) > 0, E)[None, :])
    put("iota_e", np.arange(E)[None, :])
    put("iota_a", np.arange(NA)[None, :])
    put("trash", K * T + P * np.arange(NA)[None, :] + r[:, None])
    put("part", r[:, None])
    put("eps", LN_EPS)
    put("group1", np.arange(1, NG + 1)[None, :])
    put("ones", 1.0)
    put("before", r[:, None] < r[None, :])
    put("iota", r[None, :])
    return f


def build(nc, x, ctxt, mask, g_xattn, g_ffn, wg0, w_in, w_out, wqT, bq, wkT, bk, wvT, bv, wg1T, w1, w2, cf_d, out):
    with ExitStack() as ctx:
        def sb(name, shape, dt=F32):
            return ctx.enter_context(nc.sbuf_tensor(name, shape, dt))

        def sem(name):
            return ctx.enter_context(nc.semaphore(name))

        xn_rows = [nc.dram_tensor(f"xn_rows{layer}", [T, D], F32) for layer in (0, 1)]
        y_rows = [nc.dram_tensor(f"y_rows{layer}", [K * T + NA * P, D], F32) for layer in (0, 1)]

        cf = sb("cf", [P, CF_W])
        cb = sb("cb", [P, 3 * P], BF16)
        xs = sb("xs", [P, NB, D])
        cx = sb("cx", [P, NB, D])
        cx2 = sb("cx2", [P, 2, QB, D])
        kT = sb("kT", [P, DC, T])
        vv = sb("vv", [P, NB, D])
        xn = sb("xn", [P, 2, QB, D])
        xT = sb("xT", [P, DC, QN])
        cT = sb("cT", [P, DC, QN])
        wts = sb("wts", [P, 2 * WSET])
        xg = sb("xg", [P, 2 * CT, D])
        ys = sb("ys", [P, 2 * CT, D])
        xgT = sb("xgT", [P, DC, CAP])
        ga = sb("ga", [P, 2, HALF])
        hT = sb("hT", [P, FB0, CAP])
        h1 = xgT.ap().rearrange("p c n -> p (c n)")[:, 0:F1]
        maskb = sb("maskb", [P, NB, S])
        mask8 = sb("mask8", [P, NB * S], U8)
        wqkv = sb("wqkv", [P, 3, DC, D])
        bqk = sb("bqk", [P, 2, DC])
        bvb = sb("bvb", [P, D])
        wg = sb("wg", [P, 2, DC, E])
        gts = sb("gts", [P, 4])
        tg = sb("tg", [P, 4])
        stats = sb("stats", [P, QB, 6])
        mv = sb("mv", [P, 4, QB, 2])
        sd = sb("sd", [P, 4, QB])
        rstd = sb("rstd", [P, 4, QB])
        lg = sb("lg", [P, NB, E])
        pr = sb("pr", [P, NB, E])
        top = sb("top", [P, NB, 8])
        topi = sb("topi", [P, NB, 8], U32)
        eidx = sb("eidx", [P, NG])
        oh = sb("oh", [P, E, NG], BF16)
        incl = sb("incl", [P, E, NG])
        loc = sb("loc", [P, E, NG])
        sm = sb("sm", [P, 8, NG])
        smi = sb("smi", [P, 4, NG], I32)
        rr = sb("rr", [P, 4, NB])
        oha = hT[:, :, :].rearrange("p a b -> p (a b)")[:, 0:NG * NA].rearrange("p (g a) -> p g a", g=NG)
        rhs_a = sb("rhs_a", [P, NG, 2 * NA], BF16)
        ohb = sb("ohb", [P, NG, P], BF16)
        inv = sb("inv", [P, 4, NA])
        row_y = sb("row_y", [P, NA], I32)
        row_x = sb("row_x", [P, NA], I32)
        gates = [sb(f"gates{layer}", [P, NG]) for layer in (0, 1)]
        te = sb("te", [P, 4, E])
        tei = sb("tei", [P, 4, E], I32)
        tab = sb("tab", [P, NA, E])
        tabf = sb("tabf", [P, 3, NA])
        tabi = sb("tabi", [P, 3, NA], I32)
        hflat = hT[:, :, :].rearrange("p a b -> p (a b)")
        qT = hflat[:, 0:DC * QN].rearrange("p (c n) -> p c n", c=DC)
        sc, prb, pT = (hflat[:, DC * QN + n * QN:DC * QN + (n + 1) * QN].rearrange("p (b s) -> p b s", b=QB)
                       for n in range(3))
        att = sb("att", [P, 4, QB])

        def psum(name):
            return ctx.enter_context(nc.psum_tensor(name, [P, 2, 512], F32))

        PA, PB, PC, PD = psum("PA"), psum("PB"), psum("PC"), psum("PD")

        def c(name):
            return cf[:, CF[name][0]:CF[name][1]]

        ident, decay = c("ident"), c("decay")
        before, ones_b, iota_b = (cb[:, a:b] for a, b in (CB["before"], CB["ones"], CB["iota"]))

        def yk(q, k):
            return cx[:, (2 * (q % 2) + k) * QB:(2 * (q % 2) + k + 1) * QB, :]

        cf_in, cb_ready, g_in, small_in, mask_in = (sem(n) for n in ("cf_in", "cb_ready", "g_in", "small_in", "mask_in"))
        x_in = [sem(f"x_in{q}") for q in range(NQ)]
        ctx_in = [sem(f"ctx_in{q}") for q in range(NQ)]
        zero_ready, zero_out = sem("zero_ready"), sem("zero_out")
        sq_ready, ret_done, ret_used = sem("sq_ready"), sem("ret_done"), sem("ret_used")
        evac_ready, evac_done = sem("evac_ready"), sem("evac_done")
        v_ready = sem("v_ready")
        var_ready, sd_ready = sem("var_ready"), sem("sd_ready")
        xn_ready, xn_read, lg_done, tanh_ready = sem("xn_ready"), sem("xn_read"), sem("lg_done"), sem("tanh_ready")
        xn_out0 = [sem("xn_out0a"), sem("xn_out0b")]
        xn_out1 = sem("xn_out1")
        chain = sem("dve_chain")
        e_arg, e_ready = sem("e_arg"), sem("e_ready")
        oh_ready, rank_done, map_ready, map_done = (sem(n) for n in ("oh_ready", "rank_done", "map_ready", "map_done"))
        rows_ready = sem("rows_ready")
        w_in_in = [sem(f"w_in_in{p}") for p in range(2)]
        w_out_in = [sem(f"w_out_in{p}") for p in range(2)]
        g0_in = [sem(f"g0_in{s}") for s in range(2 * CT)]
        s0_out = [sem(f"s0_out{s}") for s in range(2 * CT)]
        xt0_done, xt0_evac, hid0_done, gelu_done, h0_ready = (sem(n) for n in (
            "xt0_done", "xt0_evac", "hid0_done", "gelu_done", "h0_ready"))
        y0_done, y0_evac, ys0_free = sem("y0_done"), sem("y0_evac"), sem("ys0_free")
        y_in = [sem(f"y_in{q}") for q in range(2)]
        yk_used = sem("yk_used")
        evac2_ready, evac2_done = sem("evac2_ready"), sem("evac2_done")
        sc_done, sc_ready, exp_done, pv_done, pv_used = (sem(n) for n in (
            "sc_done", "sc_ready", "exp_done", "pv_done", "pv_used"))
        tab_ready, wts1_in, wts1_ready = sem("tab_ready"), sem("wts1_in"), sem("wts1_ready")
        g1_in = [sem(f"g1_in{p}") for p in range(2)]
        s1_out = [sem(f"s1_out{p}") for p in range(2)]
        xt1_done, xt1_evac, hid1_done, silu_done = (sem(n) for n in ("xt1_done", "xt1_evac", "hid1_done", "silu_done"))
        ht1_done, ht1_act, ht1_dve, y1_done, y1_evac, ys1_free = (sem(n) for n in (
            "ht1_done", "ht1_act", "ht1_dve", "y1_done", "y1_evac", "ys1_free"))
        fin_ready, fin_out = sem("fin_ready"), sem("fin_out")

        EV1 = {}
        for t in range(NQ + 2):
            if 0 <= t - 1 < NQ:
                for n in ("ctxT", "kT", "v"):
                    EV1[n, t - 1] = len(EV1) + 1
            if 0 <= t - 2 < NQ:
                EV1["xT", t - 2] = len(EV1) + 1
        EV2 = {}
        for t in range(NQ + 4):
            for n, lag in (("xT4", 4), ("pT", 3), ("xT3", 1), ("qT", 1)):
                if 0 <= t - lag < NQ:
                    EV2[n, t - lag] = len(EV2) + 1
        SD = {}
        for t in range(NQ + 1):
            for n, lag in ((1, 1), (0, 0)):
                if 0 <= t - lag < NQ:
                    SD[n, t - lag] = len(SD) + 1
        for t in range(NQ + 3):
            for n, lag in ((3, 3), (2, 0)):
                if 0 <= t - lag < NQ:
                    SD[n, t - lag] = len(SD) + 1

        def tiles(dram, row0, n):
            return dram[row0:row0 + n * P, :].rearrange("(b p) d -> p b d", p=P)

        w_in_v = w_in.rearrange("e (c p) f -> e p c f", p=P)
        w_out_v = w_out.rearrange("e (c p) d -> e p c d", p=P)
        w1_v = w1.rearrange("e (c p) f -> e p c f", p=P)
        w2_v = w2.rearrange("e (c p) d -> e p c d", p=P)

        block = ctx.enter_context(nc.Block())

        @block.sync
        def _(sp):
            sp.dma_start(cf[:, :], cf_d).then_inc(cf_in, 16)
            for q in range(NQ):
                sp.dma_start(cx[:, q * QB:(q + 1) * QB, :],
                             ctxt[q * QB:(q + 1) * QB].rearrange("b p d -> p b d")).then_inc(ctx_in[q], 16)
                sp.dma_start(xs[:, q * QB:(q + 1) * QB, :],
                             x[q * QB:(q + 1) * QB].rearrange("b p d -> p b d")).then_inc(x_in[q], 16)
                if q == 0:
                    sp.dma_start(gts[:, 0:2], g_xattn.partition_broadcast(P)).then_inc(g_in, 16)
                    sp.dma_start(gts[:, 2:4], g_ffn.partition_broadcast(P)).then_inc(g_in, 16)
                    for n, w in enumerate((wqT, wkT, wvT)):
                        sp.dma_start(wqkv[:, n, :, :], w.rearrange("(c p) d -> p c d", p=P)).then_inc(small_in, 16)
                    for n, b in enumerate((bq, bk)):
                        sp.dma_start(bqk[:, n, :], b).then_inc(small_in, 16)
                    sp.dma_start(bvb[:, :], bv.partition_broadcast(P)).then_inc(small_in, 16)
                    for n, w in enumerate((wg0, wg1T)):
                        sp.dma_start(wg[:, n, :, :], w.rearrange("(c p) e -> p c e", p=P)).then_inc(small_in, 16)
            sp.dma_start(mask8[:, :], mask.rearrange("b o s -> (b o s)").partition_broadcast(P)).then_inc(mask_in, 16)

            def load0(e):
                at = (e % 2) * WSET
                sp.dma_start(wts[:, at:at + WIN0].rearrange("p (c f) -> p c f", c=DC), w_in_v[e])\
                    .then_inc(w_in_in[e % 2], 16)
                sp.dma_start(wts[:, at + WIN0:at + WIN0 + FB0 * D].rearrange("p (c d) -> p c d", c=FB0), w_out_v[e])\
                    .then_inc(w_out_in[e % 2], 16)

            load0(0)
            load0(1)
            sp.wait_ge(zero_ready, 1)
            for n in range(K * NQ):
                sp.dma_start(tiles(y_rows[0], n * QN, QB), ys[:, 0:QB, :]).then_inc(zero_out, 16)
            for q in range(NQ):
                sp.wait_ge(xn_ready, q + 1)
                sp.dma_start(tiles(xn_rows[0], q * QN, QB), xn[:, q % 2]).then_inc(xn_out0[q % 2], 16)
            for e in range(2, E):
                sp.wait_ge(y0_done, CT * (e - 1))
                load0(e)

            def load1(e):
                at = (e % 2) * WSET
                sp.dma_start(wts[:, at:at + WIN1].rearrange("p (c f) -> p c f", c=DC), w1_v[e]).then_inc(wts1_in, 16)
                sp.dma_start(wts[:, at + WIN1:at + WSET].rearrange("p (c d) -> p c d", c=FB1), w2_v[e])\
                    .then_inc(wts1_in, 16)

            def fetch(layer, q):
                for k in range(K):
                    sp.dma_start(yk(q, k), tiles(y_rows[layer], k * T + q * QN, QB)).then_inc(y_in[q % 2], 16)

            for s in range(2 * CT):
                sp.wait_ge(s0_out[s], 16 * E // 2)
            sp.wait_ge(evac_done, EV1["ctxT", NQ - 1])
            for t in range(NQ + 4):
                if 0 <= t - 4 < NQ:
                    sp.wait_ge(xn_ready, NQ + SDX[3, t - 4])
                    sp.dma_start(tiles(xn_rows[1], (t - 4) * QN, QB), xn[:, 1]).then_inc(xn_out1, 16)
                if t < NQ:
                    if t >= 2:
                        sp.wait_ge(yk_used, t - 1)
                    fetch(0, t)
                if t == 1:
                    sp.wait_ge(y0_done, TILES0)
                    load1(0)
                    load1(1)
            sp.wait_ge(tab_ready, 1)
            for e in range(E):
                if e >= 2:
                    end = sp.value_load(tei[0:1, 2, e - 2:e - 1], min_val=1, max_val=TILES1 + 1)
                    sp.wait_ge(y1_done, end)
                    load1(e)
                sp.wait_ge(wts1_in, 32 * max(2, e + 1))
                sp.sem_inc(wts1_ready, 1)
            for p in range(2):
                sp.wait_ge(s1_out[p], 16 * ((TILES1 + 1 - p) // 2))
            for q in range(NQ):
                if q >= 2:
                    sp.wait_ge(yk_used, NQ + q - 1)
                fetch(1, q)
            for q in range(NQ):
                sp.wait_ge(fin_ready, q + 1)
                sp.dma_start(out[q * QB:(q + 1) * QB].rearrange("b p d -> p b d"),
                             xs[:, q * QB:(q + 1) * QB, :]).then_inc(fin_out, 16)
            sp.wait_ge(fin_out, 16 * NQ)

        @block.gpsimd
        def _(pool):
            pool.memset(ys[:, 0:QB, :], 0.0).then_inc(zero_ready, 1)
            for t in range(NQ + 1):
                if t < NQ:
                    pool.wait_ge(ctx_in[t], 16)
                    if t >= 2:
                        pool.wait_ge(ret_done, t - 1)
                    pool.tensor_tensor(cx2[:, t % 2], cx[:, t * QB:(t + 1) * QB, :], cx[:, t * QB:(t + 1) * QB, :],
                                       ALU.mult).then_inc(sq_ready, 1)
                if t >= 1:
                    q = t - 1
                    pool.wait_ge(small_in, 16 * 8)
                    pool.wait_ge(evac_done, EV1["v", q])
                    v = vv[:, q * QB:(q + 1) * QB, :]
                    pool.tensor_tensor(v, v, bvb[:, :].unsqueeze(1).broadcast_to([P, QB, D]), ALU.add)\
                        .then_inc(v_ready, 1)

            def gather0(e):
                for t in range(CT):
                    s = (e % 2) * CT + t
                    pool.indirect_dma_start(xg[:, s, :], None, xn_rows[0].ap(), bass.IndirectOffsetOnAxis(
                        ap=row_x[:, e * CT + t:e * CT + t + 1], axis=0)).then_inc(g0_in[s], 16)

            def scatter0(e):
                for t in range(CT):
                    s = (e % 2) * CT + t
                    pool.wait_ge(y0_evac, 2 + e * CT + t + 1)
                    pool.indirect_dma_start(y_rows[0].ap(), bass.IndirectOffsetOnAxis(
                        ap=row_y[:, e * CT + t:e * CT + t + 1], axis=0), ys[:, s, :], None).then_inc(s0_out[s], 16)
                    if e >= 1:
                        pool.wait_ge(s0_out[s - CT if s >= CT else s + CT], 16 * ((e + 1) // 2))
                        pool.sem_inc(ys0_free, 1)

            pool.wait_ge(rows_ready, 1)
            for n in range(2):
                pool.wait_ge(xn_out0[n], 16 * NQ // 2)
            pool.wait_ge(zero_out, 16 * K * NQ)
            gather0(0)
            gather0(1)
            for e in range(E):
                if e + 2 < E:
                    pool.wait_ge(xt0_done, (e + 1) * CT)
                    gather0(e + 2)
                scatter0(e)

            def gather1(j):
                pool.indirect_dma_start(xg[:, j % 2, :], None, xn_rows[1].ap(), bass.IndirectOffsetOnAxis(
                    ap=row_x[:, j:j + 1], axis=0)).then_inc(g1_in[j % 2], 16)

            pool.wait_ge(rows_ready, 2)
            pool.wait_ge(xn_out1, 16 * NQ)
            gather1(0)
            gather1(1)
            for j in range(TILES1):
                if j + 2 < TILES1:
                    pool.wait_ge(xt1_done, j + 1)
                    gather1(j + 2)
                pool.wait_ge(y1_evac, 2 + j + 1)
                pool.indirect_dma_start(y_rows[1].ap(), bass.IndirectOffsetOnAxis(ap=row_y[:, j:j + 1], axis=0),
                                        ys[:, j % 2, :], None).then_inc(s1_out[j % 2], 16)
                if j >= 1:
                    pool.wait_ge(s1_out[(j - 1) % 2], 16 * ((j + 1) // 2))
                    pool.sem_inc(ys1_free, 1)

        @block.scalar
        def _(act):
            act.wait_ge(g_in, 32)
            act.activation(tg[:, :], gts[:, :], ACT.Tanh).then_inc(tanh_ready, 1)
            act.wait_ge(cf_in, 16)

            def root(n, q):
                act.wait_ge(var_ready, SD[n, q])
                act.activation(sd[:, n, :], mv[:, n, :, 1], ACT.Sqrt, bias=c("eps")).then_inc(sd_ready, 1)

            for t in range(NQ + 2):
                if 0 <= t - 1 < NQ:
                    root(1, t - 1)
                if t < NQ:
                    root(0, t)
                if 0 <= t - 1 < NQ:
                    q = t - 1
                    act.wait_ge(evac_ready, EV1["ctxT", q])
                    act.activation(cT[:, :, :], PB[:, :, :], ACT.Copy).then_inc(evac_done, 1)
                    act.wait_ge(small_in, 16 * 8)
                    act.wait_ge(evac_ready, EV1["kT", q])
                    act.activation(kT[:, 0, q * QN:(q + 1) * QN], PC[:, 0, :], ACT.Identity, bias=bqk[:, 1, 0:1])
                    act.activation(kT[:, 1, q * QN:(q + 1) * QN], PC[:, 1, :], ACT.Identity, bias=bqk[:, 1, 1:2])\
                        .then_inc(evac_done, 1)
                    act.wait_ge(evac_ready, EV1["v", q])
                    act.activation(vv[:, q * QB:(q + 1) * QB, :].rearrange("p b d -> p (b d)"),
                                   PC[:, :, :].rearrange("p b d -> p (b d)"), ACT.Copy).then_inc(evac_done, 1)
                if 0 <= t - 2 < NQ:
                    act.wait_ge(evac_ready, EV1["xT", t - 2])
                    act.activation(xT[:, :, :], PB[:, :, :], ACT.Copy).then_inc(evac_done, 1)
            act.wait_ge(e_arg, 1)
            act.activation(pr[:, :, :], lg[:, :, :], ACT.Exp).then_inc(e_ready, 1)

            act.sem_inc(xt0_evac, 2)

            def xt0(i, par, e):
                for t in range(CT):
                    act.wait_ge(xt0_done, e * CT + t + 1)
                    act.activation(xgT[:, :, t * P:(t + 1) * P],
                                   PB[:, (par * CT + t) % 2, 0:D].rearrange("p (c n) -> p c n", c=DC),
                                   ACT.Copy).then_inc(xt0_evac, 1)

            def gelu0(i, par, e):
                for s in range(STEPS0):
                    act.wait_ge(hid0_done, e * STEPS0 + s + 1)
                    act.wait_ge(h0_ready, e * STEPS0 + s + 1)
                    act.activation(ga[:, s % 2, :], (PA, PC)[s % 2][:, 0, 0:HALF], ACT.Gelu).then_inc(gelu_done, 1)

            xt0(0, 0, 0)
            with act.Fori(0, E // 2 - 1) as i:
                for par in range(2):
                    gelu0(i, par, i * 2 + par)
                    xt0(i, 1 - par, i * 2 + par + 1)
            gelu0(E // 2 - 1, 0, E - 2)
            xt0(E // 2 - 1, 1, E - 1)
            gelu0(E // 2 - 1, 1, E - 1)

            for t in range(NQ + 4):
                if 0 <= t - 4 < NQ:
                    act.wait_ge(evac2_ready, EV2["xT4", t - 4])
                    act.activation(xT[:, :, :], PB[:, :, :], ACT.Copy).then_inc(evac2_done, 1)
                if 0 <= t - 3 < NQ:
                    act.wait_ge(evac2_ready, EV2["pT", t - 3])
                    act.activation(pT[:, :, :], PA[:, 1, :].rearrange("p (b s) -> p b s", b=QB), ACT.Copy)\
                        .then_inc(evac2_done, 1)
                    root(3, t - 3)
                if 0 <= t - 2 < NQ:
                    q = t - 2
                    act.wait_ge(sc_ready, q + 1)
                    if q >= 1:
                        act.wait_ge(evac2_ready, EV2["pT", q - 1])
                        act.wait_ge(pv_used, q)
                    for b in range(QB):
                        ins = act.activation(prb[:, b, :], sc[:, b, :], ACT.Exp, bias=att[:, 1, b:b + 1], scale=SCALE,
                                             accum_out=att[:, 2, b:b + 1])
                    ins.then_inc(exp_done, 1)
                if 0 <= t - 1 < NQ:
                    q = t - 1
                    act.wait_ge(evac2_ready, EV2["xT3", q])
                    act.activation(xT[:, :, :], PB[:, :, :], ACT.Copy).then_inc(evac2_done, 1)
                    act.wait_ge(evac2_ready, EV2["qT", q])
                    for k in range(DC):
                        ins = act.activation(qT[:, k, :], PC[:, k, :], ACT.Identity, bias=bqk[:, 0, k:k + 1])
                    ins.then_inc(evac2_done, 1)
                if t < NQ:
                    root(2, t)
            act.wait_ge(e_arg, 2)
            act.activation(rr[:, 1, :], rr[:, 0, :], ACT.Exp).then_inc(e_ready, 1)

            act.sem_inc(xt1_evac, 2)
            act.sem_inc(silu_done, 2)
            act.sem_inc(ht1_act, 1)

            def xt1(par, j):
                act.wait_ge(xt1_done, j + 1)
                act.activation(cT[:, par, 0:D], PB[:, par, 0:D], ACT.Copy).then_inc(xt1_evac, 1)

            def silu1(j):
                for f in range(2):
                    act.wait_ge(hid1_done, j * 2 + f + 1)
                    act.activation(h1[:, f * 512:(f + 1) * 512], PA[:, f, :], ACT.Silu).then_inc(silu_done, 1)

            def turn1(j):
                act.wait_ge(ht1_done, j * 2 + 1)
                act.activation(hT[:, 0, 0:512], PC[:, 0, :], ACT.Copy).then_inc(ht1_act, 1)

            xt1(0, 0)
            xt1(1, 1)
            silu1(0)
            with act.Fori(0, (TILES1 - 3) // 2) as i:
                for par in range(2):
                    turn1(i * 2 + par)
                    silu1(i * 2 + par + 1)
                    xt1(par, i * 2 + par + 2)
            for j in range(TILES1 - 3, TILES1):
                turn1(j)
                if j + 1 < TILES1:
                    silu1(j + 1)
                if j + 2 < TILES1:
                    xt1(j % 2, j + 2)

        @block.vector
        def _(dve):
            links = [0]

            def link(ins):
                links[0] += 1
                ins.then_inc(chain, 1)
                dve.wait_ge(chain, links[0])

            def norm_stats(n, q):
                for b in range(QB):
                    ins = dve.bn_stats(stats[:, b, :], xs[:, q * QB + b, :])
                link(ins)
                for b in range(QB):
                    ins = dve.bn_aggr(mv[:, n, b, :], stats[:, b, :])
                link(ins)
                dve.sem_inc(var_ready, 1)

            def normalise(n, q, dst):
                dve.wait_ge(sd_ready, SD[n, q])
                link(dve.reciprocal(rstd[:, n, :], sd[:, n, :]))
                for b in range(QB):
                    ins = dve.tensor_scalar(dst[:, b, :], xs[:, q * QB + b, :], mv[:, n, b, 0:1], rstd[:, n, b:b + 1],
                                            ALU.subtract, ALU.mult)
                return ins

            dve.wait_ge(tanh_ready, 1)
            for t in range(NQ + 2):
                if 0 <= t - 2 < NQ:
                    q = t - 2
                    if q >= 2:
                        dve.wait_ge(xn_out0[q % 2], 16 * (q // 2))
                        dve.wait_ge(xn_read, q - 1)
                    link(normalise(1, q, xn[:, q % 2]))
                    dve.sem_inc(xn_ready, 1)
                if 0 <= t - 1 < NQ:
                    q = t - 1
                    link(normalise(0, q, qT_rows(qT)))
                    dve.wait_ge(ret_done, q + 1)
                    link(dve.scalar_tensor_tensor(qT_flat(qT), qT_flat(qT), tg[:, 0:1], flat(PA[:, :, :]),
                                                  ALU.mult, ALU.mult))
                    dve.sem_inc(ret_used, 1)
                    xq = flat(xs[:, q * QB:(q + 1) * QB, :])
                    link(dve.tensor_tensor(xq, xq, qT_flat(qT), ALU.add))
                    norm_stats(1, q)
                if t < NQ:
                    dve.wait_ge(x_in[t], 16)
                    norm_stats(0, t)

            link(dve.tensor_copy(cb[:, :], cf[:, CF["before"][0]:CF["iota"][1]]))
            dve.sem_inc(cb_ready, 1)
            dve.wait_ge(mask_in, 16)
            link(dve.tensor_scalar(maskb[:, :, :].rearrange("p b s -> p (b s)"), mask8[:, :], NEG, None, ALU.mult))
            link(dve.tensor_tensor(maskb[:, :, :], maskb[:, :, :], c("causal").unsqueeze(1).broadcast_to([P, NB, S]),
                                   ALU.add))

            def best_two(src):
                for b in range(NB):
                    ins = dve.max(top[:, b, :], src[:, b, :])
                link(ins)
                for b in range(NB):
                    ins = dve.max_index(topi[:, b, :], top[:, b, :], src[:, b, :])
                link(ins)
                link(dve.tensor_copy(eidx[:, :].rearrange("p (k b) -> p k b", k=K),
                                     topi[:, :, 0:K].rearrange("p b k -> p k b")))
                link(dve.tensor_tensor(oh[:, :, :], eidx[:, :].unsqueeze(1).broadcast_to([P, E, NG]),
                                       c("iota_e").unsqueeze(2).broadcast_to([P, E, NG]), ALU.is_equal))
                dve.sem_inc(oh_ready, 1)

            def ranks(layer):
                dve.wait_ge(rank_done, layer + 1)
                totals = PD[:, 1, E * NG:2 * E * NG]
                link(dve.tensor_tensor_scan(flat(incl[:, :, :]), c("reset"), totals, 0.0, ALU.mult, ALU.add))
                link(dve.tensor_tensor(flat(loc[:, :, :]), flat(incl[:, :, :]), totals, ALU.subtract))
                link(dve.tensor_tensor(flat(loc[:, :, :]), flat(loc[:, :, :]), PD[:, 1, 0:E * NG], ALU.add))

            def pick(dst):
                link(dve.tensor_tensor(flat(loc[:, :, :]), flat(loc[:, :, :]), flat(oh[:, :, :]), ALU.mult))
                link(dve.tensor_reduce(dst, loc[:, :, :].rearrange("p e g -> p g e"), AX.X, ALU.add))

            def invert(layer, slot):
                link(dve.tensor_copy(smi[:, 0, :], slot))
                link(dve.tensor_scalar(smi[:, 1, :], smi[:, 0, :], P - 1, None, ALU.bitwise_and))
                link(dve.tensor_scalar(smi[:, 2, :], smi[:, 0, :], 7, None, ALU.arith_shift_right))
                link(dve.tensor_copy(sm[:, 6, :], smi[:, 1, :]))
                link(dve.tensor_copy(sm[:, 7, :], smi[:, 2, :]))
                link(dve.tensor_tensor(oha[:, :, :], sm[:, 7, :].unsqueeze(2).broadcast_to([P, NG, NA]),
                                       c("iota_a").unsqueeze(1).broadcast_to([P, NG, NA]), ALU.is_equal))
                dve.tensor_scalar(rhs_a[:, :, 0:NA], oha[:, :, :], c("part"), None, ALU.mult)
                dve.tensor_tensor(rhs_a[:, :, NA:2 * NA], oha[:, :, :],
                                  c("group1").unsqueeze(2).broadcast_to([P, NG, NA]), ALU.mult)
                for g in range(NG):
                    ins = dve.tensor_scalar(ohb[:, g, :], iota_b, sm[:, 6, g:g + 1], None, ALU.is_equal)
                link(ins)
                dve.sem_inc(map_ready, 1)
                dve.wait_ge(map_done, layer + 1)
                part, group = PD[:, 0, 128:128 + NA], PD[:, 0, 128 + NA:128 + 2 * NA]
                link(dve.tensor_copy(inv[:, 0, :], group))
                link(dve.scalar_tensor_tensor(inv[:, 1, :], inv[:, 0, :], float(P), part, ALU.mult, ALU.add))
                link(dve.scalar_tensor_tensor(inv[:, 2, :], inv[:, 1, :], float(-P), c("trash"), ALU.add,
                                              ALU.subtract))
                link(dve.scalar_tensor_tensor(inv[:, 3, :], inv[:, 0, :], 1.0, inv[:, 2, :], ALU.min, ALU.mult))
                link(dve.tensor_tensor(row_y[:, :], inv[:, 3, :], c("trash"), ALU.add))
                link(dve.tensor_scalar(row_x[:, :], row_y[:, :], T - 1, None, ALU.bitwise_and))
                dve.sem_inc(rows_ready, 1)

            def over_e(ap):
                return ap.unsqueeze(2).broadcast_to([P, NB, E])

            dve.wait_ge(lg_done, 1)
            logits = PD[:, 0, 0:NB * E].rearrange("p (b e) -> p b e", e=E)
            link(dve.tensor_reduce(rr[:, 0, :], logits, AX.X, ALU.max))
            link(dve.tensor_tensor(lg[:, :, :], logits, over_e(rr[:, 0, :]), ALU.subtract))
            dve.sem_inc(e_arg, 1)
            dve.wait_ge(e_ready, 1)
            link(dve.tensor_reduce(rr[:, 2, :], pr[:, :, :], AX.X, ALU.add))
            link(dve.reciprocal(rr[:, 3, :], rr[:, 2, :]))
            link(dve.tensor_tensor(pr[:, :, :], pr[:, :, :], over_e(rr[:, 3, :]), ALU.mult))
            best_two(pr)
            ranks(0)
            pick(sm[:, 0, :])
            link(dve.tensor_scalar(sm[:, 1, :], sm[:, 0, :], float(CAP), float(64 * P), ALU.is_ge, ALU.mult))
            link(dve.tensor_tensor(sm[:, 2, :], sm[:, 1, :], sm[:, 0, :], ALU.add))
            link(dve.scalar_tensor_tensor(sm[:, 3, :], eidx[:, :], float(CAP), sm[:, 2, :], ALU.mult, ALU.add))
            invert(0, sm[:, 3, :])
            link(dve.tensor_scalar(sm[:, 4, :], sm[:, 0, :], float(CAP), None, ALU.is_lt))
            link(dve.tensor_tensor(sm[:, 5, :].rearrange("p (k b) -> p k b", k=K),
                                   top[:, :, 0:K].rearrange("p b k -> p k b"),
                                   sm[:, 4, :].rearrange("p (k b) -> p k b", k=K), ALU.mult))
            link(dve.tensor_tensor(rr[:, 0, :], sm[:, 5, 0:NB], sm[:, 5, NB:NG], ALU.add))
            link(dve.tensor_scalar(rr[:, 2, :], rr[:, 0, :], 1e-9, None, ALU.max))
            link(dve.reciprocal(rr[:, 3, :], rr[:, 2, :]))
            for k in range(K):
                ins = dve.tensor_tensor(gates[0][:, k * NB:(k + 1) * NB], sm[:, 5, k * NB:(k + 1) * NB], rr[:, 3, :],
                                        ALU.mult)
            link(ins)

            dve.sem_inc(h0_ready, 2)
            dve.sem_inc(y0_evac, 2)
            dve.wait_ge(zero_out, 16 * K * NQ)
            dve.sem_inc(ys0_free, 2 * CT)

            def hid0(i, par, e):
                for s in range(STEPS0):
                    half, fb = divmod(s, FB0)
                    dve.wait_ge(gelu_done, e * STEPS0 + s + 1)
                    dve.tensor_tensor(hT[:, fb, half * HALF:(half + 1) * HALF], ga[:, s % 2, :],
                                      (PA, PC)[s % 2][:, 1, 0:HALF], ALU.mult).then_inc(h0_ready, 1)

            def out0(i, par, e):
                for t in range(CT):
                    dve.wait_ge(y0_done, e * CT + t + 1)
                    dve.wait_ge(ys0_free, e * CT + t + 1)
                    dve.tensor_copy(ys[:, par * CT + t, :], PD[:, (par * CT + t) % 2, 0:D]).then_inc(y0_evac, 1)

            with dve.Fori(0, E // 2) as i:
                for par in range(2):
                    hid0(i, par, i * 2 + par)
                    out0(i, par, i * 2 + par)

            def combine(layer, q):
                dve.wait_ge(y_in[q % 2], 32 * (2 * layer + q // 2 + 1))
                for b in range(QB):
                    n = q * QB + b
                    ins = dve.tensor_scalar(yk(q, 0)[:, b, :], yk(q, 0)[:, b, :], gates[layer][:, n:n + 1], None,
                                            ALU.mult)
                link(ins)
                for b in range(QB):
                    n = q * QB + b
                    ins = dve.scalar_tensor_tensor(yk(q, 0)[:, b, :], yk(q, 1)[:, b, :],
                                                   gates[layer][:, NB + n:NB + n + 1], yk(q, 0)[:, b, :], ALU.mult,
                                                   ALU.add)
                link(ins)
                xq = flat(xs[:, q * QB:(q + 1) * QB, :])
                ins = dve.scalar_tensor_tensor(xq, flat(yk(q, 0)), tg[:, 2 + layer:3 + layer], xq, ALU.mult, ALU.add)
                link(ins)
                dve.sem_inc(yk_used, 1)

            for t in range(NQ + 4):
                if 0 <= t - 4 < NQ:
                    q = t - 4
                    if q >= 1:
                        dve.wait_ge(xn_out1, 16 * q)
                        dve.wait_ge(xn_read, NQ + SDX[3, q - 1])
                    link(normalise(3, q, xn[:, 1]))
                    dve.sem_inc(xn_ready, 1)
                if 0 <= t - 3 < NQ:
                    q = t - 3
                    dve.wait_ge(exp_done, q + 1)
                    link(dve.reciprocal(att[:, 3, :], att[:, 2, :]))
                    link(dve.tensor_scalar(att[:, 3, :], att[:, 3, :], tg[:, 1:2], None, ALU.mult))
                    dve.wait_ge(pv_done, q + 1)
                    for b in range(QB):
                        xb = xs[:, q * QB + b, :]
                        ins = dve.scalar_tensor_tensor(xb, PC[:, b // 2, (b % 2) * D:(b % 2 + 1) * D],
                                                       att[:, 3, b:b + 1], xb, ALU.mult, ALU.add)
                    link(ins)
                    dve.sem_inc(pv_used, 1)
                    norm_stats(3, q)
                if 0 <= t - 2 < NQ:
                    q = t - 2
                    dve.wait_ge(sc_done, q + 1)
                    if q >= 1:
                        dve.wait_ge(exp_done, q)
                    link(dve.tensor_tensor(sc[:, :, :], PA[:, 0, :].rearrange("p (b s) -> p b s", b=QB),
                                           maskb[:, q * QB:(q + 1) * QB, :], ALU.add))
                    link(dve.tensor_reduce(att[:, 0, :], sc[:, :, :], AX.X, ALU.max))
                    link(dve.tensor_scalar(att[:, 1, :], att[:, 0, :], -SCALE, None, ALU.mult))
                    dve.sem_inc(sc_ready, 1)
                if 0 <= t - 1 < NQ:
                    q = t - 1
                    if q >= 1:
                        dve.wait_ge(xn_read, NQ + SDX[2, q - 1])
                    link(normalise(2, q, xn[:, 0]))
                    dve.sem_inc(xn_ready, 1)
                if t < NQ:
                    combine(0, t)
                    norm_stats(2, t)

            dve.wait_ge(lg_done, 2)
            link(dve.tensor_copy(lg[:, :, :], logits))
            best_two(lg)
            ranks(1)
            link(dve.tensor_scalar(tei[:, 0, :], incl[:, :, NG - 1], float(P - 1), None, ALU.add))
            link(dve.tensor_scalar(tei[:, 1, :], tei[:, 0, :], 7, None, ALU.arith_shift_right))
            link(dve.tensor_copy(te[:, 0, :], tei[:, 1, :]))
            link(dve.tensor_tensor_scan(te[:, 1, :], c("ones")[:, 0:E], te[:, 0, :], 0.0, ALU.mult, ALU.add))
            link(dve.tensor_tensor(te[:, 2, :], te[:, 1, :], te[:, 0, :], ALU.subtract))
            link(dve.tensor_scalar(te[:, 3, :], te[:, 2, :], float(P), None, ALU.mult))
            link(dve.tensor_tensor(loc[:, :, :], loc[:, :, :], te[:, 3, :].unsqueeze(2).broadcast_to([P, E, NG]),
                                   ALU.add))
            pick(sm[:, 0, :])
            invert(1, sm[:, 0, :])
            link(dve.tensor_scalar(tei[:, 2, :], te[:, 1, :], 1.0, None, ALU.add))
            link(dve.tensor_tensor(tab[:, :, :], c("iota_a").unsqueeze(2).broadcast_to([P, NA, E]),
                                   te[:, 1, :].unsqueeze(1).broadcast_to([P, NA, E]), ALU.is_ge))
            link(dve.tensor_reduce(tabf[:, 0, :], tab[:, :, :], AX.X, ALU.add))
            link(dve.tensor_scalar(tabf[:, 1, :], tabf[:, 0, :], float(E - 1), 1.0, ALU.min, ALU.add))
            link(dve.tensor_copy(tabi[:, 0, :], tabf[:, 1, :]))
            link(dve.tensor_scalar(tabf[:, 2, :], tabf[:, 0, :], float(E - 1), None, ALU.min))
            link(dve.tensor_copy(tabi[:, 2, :], tabf[:, 2, :]))
            link(dve.tensor_scalar(tabi[:, 1, :], tabi[:, 2, :], 1, None, ALU.bitwise_and))
            dve.sem_inc(tab_ready, 1)
            link(dve.tensor_tensor(rr[:, 0, :], top[:, :, 1], top[:, :, 0], ALU.subtract))
            dve.sem_inc(e_arg, 1)
            dve.wait_ge(e_ready, 2)
            link(dve.tensor_scalar(rr[:, 2, :], rr[:, 1, :], 1.0, None, ALU.add))
            link(dve.reciprocal(gates[1][:, 0:NB], rr[:, 2, :]))
            link(dve.tensor_tensor(gates[1][:, NB:NG], gates[1][:, 0:NB], rr[:, 1, :], ALU.mult))

            dve.sem_inc(ht1_dve, 1)
            dve.sem_inc(y1_evac, 2)
            dve.sem_inc(ys1_free, 2)

            def tile1(i, par, j):
                dve.wait_ge(ht1_done, j * 2 + 2)
                dve.tensor_copy(hT[:, 1, 0:512], PC[:, 1, :]).then_inc(ht1_dve, 1)
                dve.wait_ge(y1_done, j + 2)
                dve.wait_ge(ys1_free, j + 1)
                dve.tensor_copy(ys[:, par, :], PD[:, par, 0:D]).then_inc(y1_evac, 1)

            with dve.Fori(0, (TILES1 - 1) // 2) as i:
                for par in range(2):
                    tile1(i, par, i * 2 + par)
            tile1((TILES1 - 1) // 2, 0, TILES1 - 1)

            for q in range(NQ):
                combine(1, q)
                dve.sem_inc(fin_ready, 1)

        @block.tensor
        def _(pe):
            def turn(src):
                for k in range(DC):
                    for b in range(QB):
                        mm = pe.transpose(PB[:, k, b * P:(b + 1) * P], src[:, b, k * P:(k + 1) * P], ident)
                return mm

            def product(dst, lhs, rhs):
                for k, (a, b) in enumerate(zip(lhs, rhs)):
                    mm = pe.matmul(dst, a, b, start=(k == 0), stop=(k == len(lhs) - 1))
                return mm

            def router(layer, q):
                for b in range(QB):
                    mm = product(PD[:, 0, (q * QB + b) * E:(q * QB + b + 1) * E],
                                 [xT[:, k, b * P:(b + 1) * P] for k in range(DC)],
                                 [wg[:, layer, k, :] for k in range(DC)])
                if q == NQ - 1:
                    mm.then_inc(lg_done, 1)

            pe.wait_ge(cf_in, 16)
            for t in range(NQ + 2):
                if t < NQ:
                    pe.wait_ge(sq_ready, t + 1)
                    if t >= 1:
                        pe.wait_ge(ret_used, t)
                    for n in range(2):
                        mm = pe.matmul(PA[:, n, :], decay, flat(cx2[:, t % 2, 2 * n:2 * n + 2, :]),
                                       start=True, stop=True)
                    mm.then_inc(ret_done, 1)
                if 0 <= t - 1 < NQ:
                    q = t - 1
                    pe.wait_ge(ctx_in[q], 16)
                    if EV1["ctxT", q] > 1:
                        pe.wait_ge(evac_done, EV1["ctxT", q] - 1)
                    turn(cx[:, q * QB:(q + 1) * QB, :]).then_inc(evac_ready, 1)
                    pe.wait_ge(small_in, 16 * 8)
                    pe.wait_ge(evac_done, EV1["ctxT", q])
                    for m in range(DC):
                        mm = product(PC[:, m, :], [wqkv[:, 1, k, m * P:(m + 1) * P] for k in range(DC)],
                                     [cT[:, k, :] for k in range(DC)])
                    mm.then_inc(evac_ready, 1)
                    pe.wait_ge(evac_done, EV1["kT", q])
                    for b in range(QB):
                        mm = product(PC[:, b // 2, (b % 2) * D:(b % 2 + 1) * D],
                                     [cT[:, k, b * P:(b + 1) * P] for k in range(DC)],
                                     [wqkv[:, 2, k, :] for k in range(DC)])
                    mm.then_inc(evac_ready, 1)
                if 0 <= t - 2 < NQ:
                    q = t - 2
                    pe.wait_ge(xn_ready, q + 1)
                    pe.wait_ge(evac_done, EV1["xT", q] - 1)
                    mm = turn(xn[:, q % 2])
                    mm.then_inc(evac_ready, 1)
                    pe.wait_ge(evac_done, EV1["xT", q])
                    pe.sem_inc(xn_read, 1)
                    router(0, q)

            def ranks(layer):
                pe.wait_ge(oh_ready, layer + 1)
                pe.matmul(PD[:, 1, 0:E * NG], before, flat(oh[:, :, :]), start=True, stop=True)
                pe.matmul(PD[:, 1, E * NG:2 * E * NG], ones_b, flat(oh[:, :, :]), start=True, stop=True)\
                    .then_inc(rank_done, 1)

            def invert(layer):
                pe.wait_ge(map_ready, layer + 1)
                for g in range(NG):
                    mm = pe.matmul(PD[:, 0, 128:128 + 2 * NA], ohb[:, g, :], rhs_a[:, g, :], start=(g == 0),
                                   stop=(g == NG - 1))
                mm.then_inc(map_done, 1)

            pe.wait_ge(cb_ready, 1)
            ranks(0)
            invert(0)

            def xt0(i, par, e):
                for t in range(CT):
                    s = par * CT + t
                    pe.wait_ge(g0_in[s], i * 16 + 16)
                    pe.wait_ge(xt0_evac, e * CT + t + 1)
                    for k in range(DC):
                        mm = pe.transpose(PB[:, s % 2, k * P:(k + 1) * P], xg[:, s, k * P:(k + 1) * P], ident)
                    mm.then_inc(xt0_done, 1)

            def hid0(i, par, e):
                pe.wait_ge(w_in_in[par], i * 16 + 16)
                pe.wait_ge(xt0_evac, e * CT + CT + 2)
                for s in range(STEPS0):
                    half, fb = divmod(s, FB0)
                    pe.wait_ge(h0_ready, e * STEPS0 + s + 1)
                    for n in range(2):
                        col = par * WSET + n * F0 + fb * P
                        mm = product((PA, PC)[s % 2][:, n, 0:HALF],
                                     [wts[:, col + k * 2 * F0:col + k * 2 * F0 + P] for k in range(DC)],
                                     [xgT[:, k, half * HALF:(half + 1) * HALF] for k in range(DC)])
                    mm.then_inc(hid0_done, 1)

            def out0(i, par, e):
                pe.wait_ge(w_out_in[par], i * 16 + 16)
                pe.wait_ge(h0_ready, e * STEPS0 + STEPS0 + 2)
                for t in range(CT):
                    pe.wait_ge(y0_evac, e * CT + t + 1)
                    col = par * WSET + WIN0
                    product(PD[:, (par * CT + t) % 2, 0:D], [hT[:, f, t * P:(t + 1) * P] for f in range(FB0)],
                            [wts[:, col + f * D:col + (f + 1) * D] for f in range(FB0)]).then_inc(y0_done, 1)

            xt0(0, 0, 0)
            with pe.Fori(0, E // 2 - 1) as i:
                for par in range(2):
                    e = i * 2 + par
                    hid0(i, par, e)
                    xt0(i + par, 1 - par, e + 1)
                    out0(i, par, e)
            i = E // 2 - 1
            hid0(i, 0, E - 2)
            xt0(i, 1, E - 1)
            out0(i, 0, E - 2)
            hid0(i, 1, E - 1)
            out0(i, 1, E - 1)

            for t in range(NQ + 4):
                if 0 <= t - 4 < NQ:
                    q = t - 4
                    pe.wait_ge(xn_ready, NQ + SDX[3, q])
                    pe.wait_ge(evac2_done, EV2["xT4", q] - 1)
                    turn(xn[:, 1]).then_inc(evac2_ready, 1)
                    pe.wait_ge(evac2_done, EV2["xT4", q])
                    pe.sem_inc(xn_read, 1)
                    router(1, q)
                if 0 <= t - 3 < NQ:
                    q = t - 3
                    pe.wait_ge(exp_done, q + 1)
                    pe.wait_ge(evac2_done, EV2["pT", q] - 1)
                    for b in range(QB):
                        mm = pe.transpose(PA[:, 1, b * S:(b + 1) * S], prb[:, b, :], ident)
                    mm.then_inc(evac2_ready, 1)
                    pe.wait_ge(evac2_done, EV2["pT", q])
                    pe.wait_ge(v_ready, NQ)
                    for b in range(QB):
                        mm = pe.matmul(PC[:, b // 2, (b % 2) * D:(b % 2 + 1) * D], pT[:, b, :], vv[:, q * QB + b, :],
                                       start=True, stop=True)
                    mm.then_inc(pv_done, 1)
                if 0 <= t - 2 < NQ:
                    q = t - 2
                    pe.wait_ge(evac2_done, EV2["qT", q])
                    if q >= 1:
                        pe.wait_ge(sc_ready, q)
                    for b in range(QB):
                        n = (q * QB + b) * S
                        mm = product(PA[:, 0, b * S:(b + 1) * S], [qT[:, k, b * P:(b + 1) * P] for k in range(DC)],
                                     [kT[:, k, n:n + S] for k in range(DC)])
                    mm.then_inc(sc_done, 1)
                if 0 <= t - 1 < NQ:
                    q = t - 1
                    pe.wait_ge(xn_ready, NQ + SDX[2, q])
                    if EV2["xT3", q] > 1:
                        pe.wait_ge(evac2_done, EV2["xT3", q] - 1)
                    turn(xn[:, 0]).then_inc(evac2_ready, 1)
                    pe.wait_ge(evac2_done, EV2["xT3", q])
                    pe.sem_inc(xn_read, 1)
                    if q >= 2:
                        pe.wait_ge(pv_used, q - 1)
                    for m in range(DC):
                        mm = product(PC[:, m, :], [wqkv[:, 0, k, m * P:(m + 1) * P] for k in range(DC)],
                                     [xT[:, k, :] for k in range(DC)])
                    mm.then_inc(evac2_ready, 1)
            ranks(1)
            invert(1)

            def xt1(i, par, j):
                pe.wait_ge(g1_in[par], i * 16 + 16)
                pe.wait_ge(xt1_evac, j + 1)
                for k in range(DC):
                    mm = pe.transpose(PB[:, par, k * P:(k + 1) * P], xg[:, par, k * P:(k + 1) * P], ident)
                mm.then_inc(xt1_done, 1)

            def hid1(par, j):
                need = pe.value_load(tabi[0:1, 0, bass.ds(j, 1)], min_val=1, max_val=E)
                half = pe.value_load(tabi[0:1, 1, bass.ds(j, 1)], min_val=0, max_val=1)
                pe.wait_ge(wts1_ready, need)
                pe.wait_ge(xt1_evac, j + 3)
                for f in range(2):
                    pe.wait_ge(silu_done, j * 2 + f + 1)
                    product(PA[:, f, :], [cT[:, par, k * P:(k + 1) * P] for k in range(DC)],
                            [wts[:, bass.ds(half * WSET + (k * F1 + f * 512), 512)] for k in range(DC)])\
                        .then_inc(hid1_done, 1)

            def turn1(j):
                for n, free in enumerate((ht1_act, ht1_dve)):
                    pe.wait_ge(silu_done, j * 2 + n + 3)
                    pe.wait_ge(free, j + 1)
                    for b in range(4):
                        f = n * 4 + b
                        mm = pe.transpose(PC[:, n, b * P:(b + 1) * P], h1[:, f * P:(f + 1) * P], ident)
                    mm.then_inc(ht1_done, 1)

            def out1(par, j):
                half = pe.value_load(tabi[0:1, 1, bass.ds(j, 1)], min_val=0, max_val=1)
                pe.wait_ge(ht1_act, j + 2)
                pe.wait_ge(ht1_dve, j + 2)
                pe.wait_ge(y1_evac, j + 1)
                product(PD[:, par, 0:D], [hT[:, f // 4, (f % 4) * P:(f % 4 + 1) * P] for f in range(FB1)],
                        [wts[:, bass.ds(half * WSET + (WIN1 + f * D), D)] for f in range(FB1)]).then_inc(y1_done, 1)

            pe.sem_inc(y1_done, 1)
            pe.wait_ge(tab_ready, 1)
            xt1(0, 0, 0)
            xt1(0, 1, 1)
            hid1(0, 0)
            with pe.Fori(0, (TILES1 - 3) // 2) as i:
                for par in range(2):
                    j = i * 2 + par
                    turn1(j)
                    hid1(1 - par, j + 1)
                    xt1(i + 1, par, j + 2)
                    out1(par, j)
            for j in range(TILES1 - 3, TILES1):
                turn1(j)
                if j + 1 < TILES1:
                    hid1((j + 1) % 2, j + 1)
                if j + 2 < TILES1:
                    xt1(j // 2 + 1, j % 2, j + 2)
                out1(j % 2, j)


def flat(ap):
    return ap.rearrange("p a b -> p (a b)")


def qT_flat(t):
    return flat(t[:, :, :])


def qT_rows(t):
    return qT_flat(t).rearrange("p (b d) -> p b d", d=D)


SDX = {}
for _t in range(NQ + 4):
    for _n, _lag in ((3, 4), (2, 1)):
        if 0 <= _t - _lag < NQ:
            SDX[_n, _t - _lag] = len(SDX) + 1


def kernel(**inputs):
    import concourse.bacc as bacc
    from concourse.bass_utils import run_bass_kernel_spmd

    nc = bacc.Bacc("TRN2", target_bir_lowering=False, num_devices=1)
    arrays, args = {}, []

    def give(name, a):
        a = np.ascontiguousarray(a)
        arrays[name] = a
        args.append(nc.dram_tensor(name, a.shape, mybir.dt.from_np(a.dtype), kind="ExternalInput").ap())

    for name in ("x", "ctx_1024", "mask_Bx1xS2_bk0", "g_xattn", "g_ffn", "L0_ffn_Wg", "L0_ffn_W_in", "L0_ffn_W_out"):
        give(name, inputs[name])
    for m in "qkv":
        give(f"w{m}T", np.asarray(inputs[f"L1_xattn_W{m}"]).T)
        b = np.asarray(inputs[f"L1_xattn_b{m}"])
        give(f"b{m}", b if m == "v" else b.reshape(DC, P).T)
    give("gate_wT", np.asarray(inputs["L1_ffn_gate_w"]).T)
    give("w1", inputs["L1_ffn_w1"])
    give("w2", inputs["L1_ffn_w2"])
    give("tables", constants())
    out = nc.dram_tensor("out", (NB, S, D), F32, kind="ExternalOutput").ap()
    build(nc, *args, out)
    r = run_bass_kernel_spmd(nc, [arrays], core_ids=[0])
    return r.results[0]["out"]
```

```python
import math
from contextlib import ExitStack

import numpy as np

import concourse.bass as bass
from concourse import mybir

ALU = mybir.AluOpType
ACT = mybir.ActivationFunctionType
AX = mybir.AxisListType
F32 = mybir.dt.float32
F32R = mybir.dt.float32r
BF16 = mybir.dt.bfloat16
I32 = mybir.dt.int32
U32 = mybir.dt.uint32
U8 = mybir.dt.uint8

P = 128
NB, S, D = 16, 128, 256
T = NB * S
DC = D // P
E, K = 8, 2
QB = 4
NQ = NB // QB
QN = QB * P
NG = K * NB
F0 = 512
F1 = 1024
CAP = math.ceil(K * T / E * 1.25)
CT = CAP // P
TILES0 = E * CT
TILES1 = K * T // P + E - 1
NA = max(TILES0, TILES1 + 1)
HALF = CAP // 2
FB0 = F0 // P
FB1 = F1 // P
PIECES = 4
STEPS0 = 2 * FB0
LN_EPS = 1e-5
NEG = -1.0e30
WIN = DC * 2 * F0
WOUT0 = F0 // P * D
WOUT1 = F1 // P * D
SCALE = 1.0 / math.sqrt(D)

_at, CF = 0, {}
for _n, _w in (("ident", P), ("decay", P), ("causal", P), ("reset", E * NG), ("iota_e", E), ("iota_a", NA),
               ("trash", NA), ("part", 1), ("eps", 1), ("group1", NG),
               ("before", P), ("ones", P), ("iota", P)):
    CF[_n] = (_at, _at + _w)
    _at += _w
CF_W = _at
CB = {"before": (0, P), "ones": (P, 2 * P), "iota": (2 * P, 3 * P)}


def constants():
    f = np.zeros((P, CF_W), np.float32)
    r = np.arange(P)

    def put(name, value):
        f[:, slice(*CF[name])] = value

    put("ident", np.eye(P))
    lag = r[None, :] - r[:, None]
    put("decay", np.where(lag >= 0, np.float64(np.float32(0.9)) ** np.maximum(lag, 0), 0.0))
    put("causal", np.where(r[None, :] <= r[:, None], 0.0, NEG))
    put("reset", np.tile(np.arange(NG) > 0, E)[None, :])
    put("iota_e", np.arange(E)[None, :])
    put("iota_a", np.arange(NA)[None, :])
    put("trash", K * T + P * np.arange(NA)[None, :] + r[:, None])
    put("part", r[:, None])
    put("eps", LN_EPS)
    put("group1", np.arange(1, NG + 1)[None, :])
    put("ones", 1.0)
    put("before", r[:, None] < r[None, :])
    put("iota", r[None, :])
    return f


def build(nc, x, ctxt, mask, g_xattn, g_ffn, wg0, w_in, w_out, wqT, bq, wkT, bk, wvT, bv, wg1T, w1, w2, cf_d, out):
    with ExitStack() as ctx:
        def sb(name, shape, dt=F32):
            return ctx.enter_context(nc.sbuf_tensor(name, shape, dt))

        def sem(name):
            return ctx.enter_context(nc.semaphore(name))

        xn_rows = [nc.dram_tensor(f"xn_rows{layer}", [T, D], F32) for layer in (0, 1)]
        y_rows = [nc.dram_tensor(f"y_rows{layer}", [K * T + NA * P, D], F32) for layer in (0, 1)]

        cf = sb("cf", [P, CF_W])
        cb = sb("cb", [P, 3 * P], BF16)
        xs = sb("xs", [P, NB, D])
        cx = sb("cx", [P, NB, D])
        kT = sb("kT", [P, DC, T])
        vv = sb("vv", [P, NB, D])
        xn = sb("xn", [P, 2, QB, D])
        xT = sb("xT", [P, DC, QN])
        h1 = flat(xT[:, :, :])
        raw = sb("raw", [P, WIN + WOUT1])
        cx2 = raw[:, 0:2 * QB * D].rearrange("p (n b d) -> p n b d", n=2, b=QB)
        whi, wlo = (sb(n, [P, WIN + WOUT1], F32R) for n in ("whi", "wlo"))
        xhi, xlo = (sb(n, [P, DC, CAP], F32R) for n in ("xhi", "xlo"))
        hhi, hlo = (sb(n, [P, FB0 * CAP], F32R) for n in ("hhi", "hlo"))
        xg = sb("xg", [P, 2 * CT, D])
        ys = sb("ys", [P, 2 * CT, D])
        mask8 = sb("mask8", [P, NB * S], U8)
        wqkv = sb("wqkv", [P, 3, DC, D])
        bqk = sb("bqk", [P, 2, DC])
        bvb = sb("bvb", [P, D])
        wg = sb("wg", [P, 2, DC, E])
        gts = sb("gts", [P, 4])
        tg = sb("tg", [P, 4])
        stats = sb("stats", [P, QB, 6])
        mv = sb("mv", [P, 4, QB, 2])
        sd = sb("sd", [P, 4, QB])
        rstd = sb("rstd", [P, 4, QB])
        lg = sb("lg", [P, NB, E])
        pr = sb("pr", [P, NB, E])
        top = sb("top", [P, NB, 8])
        topi = sb("topi", [P, NB, 8], U32)
        eidx = sb("eidx", [P, NG])
        oh = sb("oh", [P, E, NG], BF16)
        incl = sb("incl", [P, E, NG])
        loc = sb("loc", [P, E, NG])
        sm = sb("sm", [P, 8, NG])
        smi = sb("smi", [P, 4, NG], I32)
        rr = sb("rr", [P, 4, NB])
        xflat = flat(xg[:, :, :])
        oha = xflat[:, 0:NG * NA].rearrange("p (g a) -> p g a", g=NG)
        ring = sb("ring", [P, NG * NA])
        rhs_a = ring[:, :].bitcast(BF16).rearrange("p (g a) -> p g a", g=NG)
        ga = ring[:, 0:4 * HALF].rearrange("p (n c) -> p n c", n=4)
        ohb = flat(ys[:, :, :])[:, 0:NG * P // 2].bitcast(BF16).rearrange("p (g n) -> p g n", g=NG)
        inv = sb("inv", [P, 4, NA])
        row_y = sb("row_y", [P, NA], I32)
        row_x = sb("row_x", [P, NA], I32)
        gates = [sb(f"gates{layer}", [P, NG]) for layer in (0, 1)]
        te = sb("te", [P, 4, E])
        tei = sb("tei", [P, 4, E], I32)
        tab = ring[:, 0:NA * E].rearrange("p (a e) -> p a e", e=E)
        tabf = sb("tabf", [P, 6, NA])
        tabi = sb("tabi", [P, 3, NA], I32)
        qT = xflat[:, 0:DC * QN].rearrange("p (c n) -> p c n", c=DC)
        sc, prb, pT = (xflat[:, DC * QN + n * QN:DC * QN + (n + 1) * QN].rearrange("p (b s) -> p b s", b=QB)
                       for n in range(3))
        att = sb("att", [P, 4, QB])

        def psum(name):
            return ctx.enter_context(nc.psum_tensor(name, [P, 2, 512], F32))

        PA, PB, PC, PD = psum("PA"), psum("PB"), psum("PC"), psum("PD")

        def c(name):
            return cf[:, CF[name][0]:CF[name][1]]

        ident, decay = c("ident"), c("decay")
        before, ones_b, iota_b = (cb[:, a:b] for a, b in (CB["before"], CB["ones"], CB["iota"]))

        def bank0(par, t):
            return PB[:, (par * CT + t) % 2, 0:D].rearrange("p (c n) -> p c n", c=DC)

        def hid_at(h, s):
            half, fb = divmod(s, FB0)
            return h[:, fb * CAP + half * HALF:fb * CAP + (half + 1) * HALF]

        def yk(q, k):
            return cx[:, (2 * (q % 2) + k) * QB:(2 * (q % 2) + k + 1) * QB, :]

        cf_in, cb_ready, g_in, small_in, mask_in = (sem(n) for n in ("cf_in", "cb_ready", "g_in", "small_in", "mask_in"))
        x_in = [sem(f"x_in{q}") for q in range(NQ)]
        ctx_in = [sem(f"ctx_in{q}") for q in range(NQ)]
        zero_ready, zero_out = sem("zero_ready"), sem("zero_out")
        sq_ready, ret_done, ret_used = sem("sq_ready"), sem("ret_done"), sem("ret_used")
        evac_ready, evac_done = sem("evac_ready"), sem("evac_done")
        v_ready = sem("v_ready")
        var_ready, sd_ready = sem("var_ready"), sem("sd_ready")
        xn_ready, xn_read, lg_done, tanh_ready = sem("xn_ready"), sem("xn_read"), sem("lg_done"), sem("tanh_ready")
        xn_out0 = [sem("xn_out0a"), sem("xn_out0b")]
        xn_out1 = sem("xn_out1")
        chain = sem("dve_chain")
        e_arg, e_ready = sem("e_arg"), sem("e_ready")
        oh_ready, rank_done, map_ready, map_done = (sem(n) for n in ("oh_ready", "rank_done", "map_ready", "map_done"))
        rows_ready = sem("rows_ready")
        win_in, wout_in = [[sem(f"{n}{layer}") for layer in (0, 1)] for n in ("win_in", "wout_in")]
        win_hi, win_lo, wout_hi, wout_lo = [[sem(f"{n}{layer}") for layer in (0, 1)] for n in (
            "win_hi", "win_lo", "wout_hi", "wout_lo")]
        g0_in = [sem(f"g0_in{s}") for s in range(2 * CT)]
        s0_out = [sem(f"s0_out{s}") for s in range(2 * CT)]
        xt0_done, xt0_hi, xt0_lo, hid0_done, gelu_done, hid0_used, h0_hi, h0_lo = (sem(n) for n in (
            "xt0_done", "xt0_hi", "xt0_lo", "hid0_done", "gelu_done", "hid0_used", "h0_hi", "h0_lo"))
        y0_done, y0_evac, ys0_free = sem("y0_done"), sem("y0_evac"), sem("ys0_free")
        y_in = [sem(f"y_in{q}") for q in range(2)]
        yk_used = sem("yk_used")
        evac2_ready, evac2_done = sem("evac2_ready"), sem("evac2_done")
        sc_done, sc_ready, exp_done, pv_done, pv_used = (sem(n) for n in (
            "sc_done", "sc_ready", "exp_done", "pv_done", "pv_used"))
        tab_ready = sem("tab_ready")
        g1_in = [sem(f"g1_in{p}") for p in range(2)]
        s1_out = [sem(f"s1_out{p}") for p in range(2)]
        xt1_done, xt1_hi, xt1_lo, hid1_done, silu_done = (sem(n) for n in (
            "xt1_done", "xt1_hi", "xt1_lo", "hid1_done", "silu_done"))
        ht1_done, ht1_hi, ht1_lo, y1_done, y1_evac, ys1_free = (sem(n) for n in (
            "ht1_done", "ht1_hi", "ht1_lo", "y1_done", "y1_evac", "ys1_free"))
        fin_ready, fin_out = sem("fin_ready"), sem("fin_out")

        EV1 = {("xT", q): q + 1 for q in range(NQ)}
        for q in range(NQ):
            for n in ("ctxT", "kT", "v"):
                EV1[n, q] = len(EV1) + 1
        EV2 = {}
        for t in range(NQ + 4):
            for n, lag in (("xT4", 4), ("pT", 3), ("xT3", 1), ("qT", 1)):
                if 0 <= t - lag < NQ:
                    EV2[n, t - lag] = len(EV2) + 1
        SD = {}
        for t in range(NQ + 1):
            for n, lag in ((1, 1), (0, 0)):
                if 0 <= t - lag < NQ:
                    SD[n, t - lag] = len(SD) + 1
        for t in range(NQ + 3):
            for n, lag in ((3, 3), (2, 0)):
                if 0 <= t - lag < NQ:
                    SD[n, t - lag] = len(SD) + 1

        def tiles(dram, row0, n):
            return dram[row0:row0 + n * P, :].rearrange("(b p) d -> p b d", p=P)

        TAB_EXPERT, TAB_SPLIT, TAB_LANDED = range(3)
        w_in_v = w_in.rearrange("e (c p) f -> e p c f", p=P)
        w_out_v = w_out.rearrange("e (c p) d -> e p c d", p=P)
        w1_v = w1.rearrange("e (c p) f -> e p c f", p=P)
        w2_v = w2.rearrange("e (c p) d -> e p c d", p=P)

        def piece_in(n):
            at = (n % 2) * F1 + (n // 2) * 512
            return slice(at, at + 512)

        def piece_out(n):
            return slice(WIN + n * WOUT1 // PIECES, WIN + (n + 1) * WOUT1 // PIECES)

        block = ctx.enter_context(nc.Block())

        @block.sync
        def _(sp):
            sp.dma_start(cf[:, :], cf_d).then_inc(cf_in, 16)
            for q in range(NQ):
                sp.dma_start(cx[:, q * QB:(q + 1) * QB, :],
                             ctxt[q * QB:(q + 1) * QB].rearrange("b p d -> p b d")).then_inc(ctx_in[q], 16)
                sp.dma_start(xs[:, q * QB:(q + 1) * QB, :],
                             x[q * QB:(q + 1) * QB].rearrange("b p d -> p b d")).then_inc(x_in[q], 16)
                if q == 0:
                    sp.dma_start(gts[:, 0:2], g_xattn.partition_broadcast(P)).then_inc(g_in, 16)
                    sp.dma_start(gts[:, 2:4], g_ffn.partition_broadcast(P)).then_inc(g_in, 16)
                    for n, w in enumerate((wqT, wkT, wvT)):
                        sp.dma_start(wqkv[:, n, :, :], w.rearrange("(c p) d -> p c d", p=P)).then_inc(small_in, 16)
                    for n, b in enumerate((bq, bk)):
                        sp.dma_start(bqk[:, n, :], b).then_inc(small_in, 16)
                    sp.dma_start(bvb[:, :], bv.partition_broadcast(P)).then_inc(small_in, 16)
                    for n, w in enumerate((wg0, wg1T)):
                        sp.dma_start(wg[:, n, :, :], w.rearrange("(c p) e -> p c e", p=P)).then_inc(small_in, 16)
            sp.dma_start(mask8[:, :], mask.rearrange("b o s -> (b o s)").partition_broadcast(P)).then_inc(mask_in, 16)

            def load(layer, wanted, first):
                src, n = ((w_in_v, w_out_v), (w1_v, w2_v))[layer][1 - first], (DC, (FB0, FB1)[layer])[1 - first]
                dst = raw[:, 0:WIN] if first else raw[:, WIN:WIN + (WOUT0, WOUT1)[layer]]
                sp.dma_start(dst.rearrange("p (c f) -> p c f", c=n), src[wanted])\
                    .then_inc((win_in if first else wout_in)[layer], 16)

            load(0, 0, False)
            sp.wait_ge(zero_ready, 1)
            for n in range(K * NQ):
                sp.dma_start(tiles(y_rows[0], n * QN, QB), ys[:, 0:QB, :]).then_inc(zero_out, 16)
            for q in range(NQ):
                sp.wait_ge(xn_ready, q + 1)
                sp.dma_start(tiles(xn_rows[0], q * QN, QB), xn[:, q % 2]).then_inc(xn_out0[q % 2], 16)
            sp.wait_ge(ret_done, NQ)
            load(0, 0, True)
            for e in range(1, E):
                for hi, lo, first in ((win_hi[0], win_lo[0], True), (wout_hi[0], wout_lo[0], False)):
                    parts = DC if first else 1
                    sp.wait_ge(hi, parts * e)
                    sp.wait_ge(lo, parts * e)
                    load(0, e, first)

            def fetch(layer, q):
                for k in range(K):
                    sp.dma_start(yk(q, k), tiles(y_rows[layer], k * T + q * QN, QB)).then_inc(y_in[q % 2], 16)

            for s in range(2 * CT):
                sp.wait_ge(s0_out[s], 16 * E // 2)
            for hi, lo, first in ((win_hi[0], win_lo[0], True), (wout_hi[0], wout_lo[0], False)):
                sp.wait_ge(hi, (DC if first else 1) * E)
                sp.wait_ge(lo, (DC if first else 1) * E)
                load(1, 0, first)
            for t in range(NQ + 4):
                if 0 <= t - 4 < NQ:
                    sp.wait_ge(xn_ready, NQ + SDX[3, t - 4])
                    sp.dma_start(tiles(xn_rows[1], (t - 4) * QN, QB), xn[:, 1]).then_inc(xn_out1, 16)
                if t < NQ:
                    if t >= 2:
                        sp.wait_ge(yk_used, t - 1)
                    fetch(0, t)
            sp.wait_ge(tab_ready, 1)
            with sp.Fori(0, TILES1) as j:
                changes = sp.value_load(tabi[0:1, TAB_LANDED, bass.ds(j, 1)], min_val=0, max_val=16 * (E + 1))
                with sp.If(changes > 0):
                    e = sp.value_load(tabi[0:1, TAB_EXPERT, bass.ds(j, 1)], min_val=0, max_val=E - 1)
                    need = sp.value_load(tabi[0:1, TAB_SPLIT, bass.ds(j, 1)], min_val=1,
                                         max_val=PIECES * (TILES1 + 1))
                    for hi, lo, first in ((win_hi[1], win_lo[1], True), (wout_hi[1], wout_lo[1], False)):
                        sp.wait_ge(hi, need)
                        sp.wait_ge(lo, need)
                        load(1, e, first)
            for p in range(2):
                sp.wait_ge(s1_out[p], 16 * ((TILES1 + 1 - p) // 2))
            for q in range(NQ):
                if q >= 2:
                    sp.wait_ge(yk_used, NQ + q - 1)
                fetch(1, q)
            for q in range(NQ):
                sp.wait_ge(fin_ready, q + 1)
                sp.dma_start(out[q * QB:(q + 1) * QB].rearrange("b p d -> p b d"),
                             xs[:, q * QB:(q + 1) * QB, :]).then_inc(fin_out, 16)
            sp.wait_ge(fin_out, 16 * NQ)

        @block.gpsimd
        def _(pool):
            pool.memset(ys[:, 0:QB, :], 0.0).then_inc(zero_ready, 1)
            for t in range(NQ):
                pool.wait_ge(ctx_in[t], 16)
                if t >= 2:
                    pool.wait_ge(ret_done, t - 1)
                pool.tensor_tensor(cx2[:, t % 2], cx[:, t * QB:(t + 1) * QB, :], cx[:, t * QB:(t + 1) * QB, :],
                                   ALU.mult).then_inc(sq_ready, 1)

            def gather0(e):
                for t in range(CT):
                    s = (e % 2) * CT + t
                    pool.indirect_dma_start(xg[:, s, :], None, xn_rows[0].ap(), bass.IndirectOffsetOnAxis(
                        ap=row_x[:, e * CT + t:e * CT + t + 1], axis=0)).then_inc(g0_in[s], 16)

            def scatter0(e):
                for t in range(CT):
                    s = (e % 2) * CT + t
                    pool.wait_ge(y0_evac, 2 + e * CT + t + 1)
                    pool.indirect_dma_start(y_rows[0].ap(), bass.IndirectOffsetOnAxis(
                        ap=row_y[:, e * CT + t:e * CT + t + 1], axis=0), ys[:, s, :], None).then_inc(s0_out[s], 16)
                    if e >= 1:
                        pool.wait_ge(s0_out[s - CT if s >= CT else s + CT], 16 * ((e + 1) // 2))
                        pool.sem_inc(ys0_free, 1)

            pool.wait_ge(rows_ready, 1)
            for n in range(2):
                pool.wait_ge(xn_out0[n], 16 * NQ // 2)
            pool.wait_ge(zero_out, 16 * K * NQ)
            gather0(0)
            gather0(1)
            pool.wait_ge(small_in, 16 * 8)
            for q in range(NQ):
                pool.wait_ge(evac_done, EV1["v", q])
                v = vv[:, q * QB:(q + 1) * QB, :]
                pool.tensor_tensor(v, v, bvb[:, :].unsqueeze(1).broadcast_to([P, QB, D]), ALU.add)\
                    .then_inc(v_ready, 1)
            for e in range(E):
                if e + 2 < E:
                    pool.wait_ge(xt0_done, (e + 1) * CT)
                    gather0(e + 2)
                scatter0(e)

            def gather1(j):
                pool.indirect_dma_start(xg[:, j % 2, :], None, xn_rows[1].ap(), bass.IndirectOffsetOnAxis(
                    ap=row_x[:, j:j + 1], axis=0)).then_inc(g1_in[j % 2], 16)

            pool.wait_ge(rows_ready, 2)
            pool.wait_ge(xn_out1, 16 * NQ)
            gather1(0)
            gather1(1)
            for j in range(-1, TILES1):
                if j + 3 < TILES1:
                    pool.wait_ge(xt1_done, j + 2)
                    gather1(j + 3)
                if j < 0:
                    continue
                pool.wait_ge(y1_evac, 2 + j + 1)
                pool.indirect_dma_start(y_rows[1].ap(), bass.IndirectOffsetOnAxis(ap=row_y[:, j:j + 1], axis=0),
                                        ys[:, j % 2, :], None).then_inc(s1_out[j % 2], 16)
                if j >= 1:
                    pool.wait_ge(s1_out[(j - 1) % 2], 16 * ((j + 1) // 2))
                    pool.sem_inc(ys1_free, 1)

        @block.scalar
        def _(act):
            act.wait_ge(g_in, 32)
            act.activation(tg[:, :], gts[:, :], ACT.Tanh).then_inc(tanh_ready, 1)
            act.wait_ge(cf_in, 16)

            def root(n, q):
                act.wait_ge(var_ready, SD[n, q])
                act.activation(sd[:, n, :], mv[:, n, :, 1], ACT.Sqrt, bias=c("eps")).then_inc(sd_ready, 1)

            for t in range(NQ + 2):
                if 0 <= t - 1 < NQ:
                    root(1, t - 1)
                if t < NQ:
                    root(0, t)
                if 0 <= t - 2 < NQ:
                    act.wait_ge(evac_ready, EV1["xT", t - 2])
                    act.activation(xT[:, :, :], PB[:, :, :], ACT.Copy).then_inc(evac_done, 1)
            act.wait_ge(e_arg, 1)
            act.activation(pr[:, :, :], lg[:, :, :], ACT.Exp).then_inc(e_ready, 1)
            act.wait_ge(small_in, 16 * 8)
            for q in range(NQ):
                act.wait_ge(evac_ready, EV1["ctxT", q])
                act.activation(xT[:, :, :], PB[:, :, :], ACT.Copy).then_inc(evac_done, 1)
                act.wait_ge(evac_ready, EV1["kT", q])
                for k in range(DC):
                    ins = act.activation(kT[:, k, q * QN:(q + 1) * QN], PC[:, k, :], ACT.Identity,
                                         bias=bqk[:, 1, k:k + 1])
                ins.then_inc(evac_done, 1)
                act.wait_ge(evac_ready, EV1["v", q])
                act.activation(flat(vv[:, q * QB:(q + 1) * QB, :]), flat(PC[:, :, :]), ACT.Copy)\
                    .then_inc(evac_done, 1)

            def win0(e, k):
                act.wait_ge(win_in[0], e * 16 + 16)
                act.activation(whi[:, k * 2 * F0:(k + 1) * 2 * F0], raw[:, k * 2 * F0:(k + 1) * 2 * F0], ACT.Copy)\
                    .then_inc(win_hi[0], 1)

            def wout0(e):
                act.wait_ge(wout_in[0], e * 16 + 16)
                act.activation(whi[:, WIN:WIN + WOUT0], raw[:, WIN:WIN + WOUT0], ACT.Copy).then_inc(wout_hi[0], 1)

            def xt0(par, e):
                for t in range(CT):
                    act.wait_ge(xt0_done, e * CT + t + 1)
                    act.activation(xhi[:, :, t * P:(t + 1) * P], bank0(par, t), ACT.Copy).then_inc(xt0_hi, 1)

            def hid0(e, first=False):
                for s in range(STEPS0 + 1):
                    if s < STEPS0:
                        act.wait_ge(hid0_done, e * STEPS0 + s + 1)
                        act.wait_ge(h0_lo, e * STEPS0 + s + 1)
                        act.activation(ga[:, s % 4, :], (PA, PC)[s % 2][:, 0, 0:HALF], ACT.Gelu)\
                            .then_inc(gelu_done, 1)
                    if s >= 1:
                        act.wait_ge(hid0_used, e * STEPS0 + s + 2)
                        act.activation(hid_at(hhi, s - 1), ga[:, (s - 1) % 4, :], ACT.Copy).then_inc(h0_hi, 1)
                    if s == 1 and not first:
                        wout0(e)

            def out0(par, e, last=False):
                for t in range(CT):
                    if t < DC and not last:
                        win0(e + 1, t)
                    act.wait_ge(y0_done, e * CT + t + 1)
                    act.wait_ge(ys0_free, e * CT + t + 1)
                    act.activation(ys[:, par * CT + t, :], PD[:, (par * CT + t) % 2, 0:D], ACT.Copy)\
                        .then_inc(y0_evac, 1)

            act.sem_inc(y0_evac, 2)
            for k in range(DC):
                win0(0, k)
            wout0(0)
            xt0(0, 0)
            hid0(0, first=True)
            xt0(1, 1)
            out0(0, 0)
            with act.Fori(0, E // 2 - 1) as i:
                for par in (1, 0):
                    e = i * 2 + 2 - par
                    hid0(e)
                    xt0(1 - par, e + 1)
                    out0(par, e)
            hid0(E - 1)
            out0(1, E - 1, last=True)

            for t in range(NQ + 4):
                if 0 <= t - 4 < NQ:
                    act.wait_ge(evac2_ready, EV2["xT4", t - 4])
                    act.activation(xT[:, :, :], PB[:, :, :], ACT.Copy).then_inc(evac2_done, 1)
                if 0 <= t - 3 < NQ:
                    act.wait_ge(evac2_ready, EV2["pT", t - 3])
                    act.activation(pT[:, :, :], PA[:, 1, :].rearrange("p (b s) -> p b s", b=QB), ACT.Copy)\
                        .then_inc(evac2_done, 1)
                    root(3, t - 3)
                if 0 <= t - 2 < NQ:
                    q = t - 2
                    act.wait_ge(sc_ready, q + 1)
                    if q >= 1:
                        act.wait_ge(evac2_ready, EV2["pT", q - 1])
                        act.wait_ge(pv_used, q)
                    for b in range(QB):
                        ins = act.activation(prb[:, b, :], sc[:, b, :], ACT.Exp, bias=att[:, 1, b:b + 1], scale=SCALE,
                                             accum_out=att[:, 2, b:b + 1])
                    ins.then_inc(exp_done, 1)
                if 0 <= t - 1 < NQ:
                    q = t - 1
                    act.wait_ge(evac2_ready, EV2["xT3", q])
                    act.activation(xT[:, :, :], PB[:, :, :], ACT.Copy).then_inc(evac2_done, 1)
                    act.wait_ge(evac2_ready, EV2["qT", q])
                    for k in range(DC):
                        ins = act.activation(qT[:, k, :], PC[:, k, :], ACT.Identity, bias=bqk[:, 0, k:k + 1])
                    ins.then_inc(evac2_done, 1)
                if t < NQ:
                    root(2, t)
            act.wait_ge(e_arg, 2)
            act.activation(rr[:, 1, :], rr[:, 0, :], ACT.Exp).then_inc(e_ready, 1)

            def landed(j):
                return act.value_load(tabi[0:1, TAB_LANDED, bass.ds(j, 1)], min_val=0, max_val=16 * (E + 1))

            def split1(arrived, count, done, pieces):
                act.wait_ge(arrived, count)
                for n in range(PIECES):
                    act.activation(whi[:, pieces(n)], raw[:, pieces(n)], ACT.Copy).then_inc(done, 1)

            def win1(j, count):
                with act.If(count > 0):
                    act.wait_ge(hid1_done, j * 2 + 1)
                    split1(win_in[1], count, win_hi[1], piece_in)
                with act.Else():
                    act.drain().then_inc(win_hi[1], PIECES)

            def wout1(j, count):
                with act.If(count > 0):
                    act.wait_ge(y1_done, j + 1)
                    split1(wout_in[1], count, wout_hi[1], piece_out)
                with act.Else():
                    act.drain().then_inc(wout_hi[1], PIECES)

            def xt1(par, j):
                act.wait_ge(xt1_done, j + 1)
                act.activation(xhi[:, par, 0:D], PB[:, par, 0:D], ACT.Copy).then_inc(xt1_hi, 1)

            def silu1(j):
                for f in range(2):
                    act.wait_ge(hid1_done, j * 2 + f + 2)
                    act.activation(h1[:, f * 512:(f + 1) * 512], PA[:, f, :], ACT.Silu).then_inc(silu_done, 1)

            def turn1(j):
                for n in range(2):
                    act.wait_ge(ht1_done, j * 2 + n + 1)
                    act.activation(hhi[:, n * 512:(n + 1) * 512], PC[:, n, :], ACT.Copy).then_inc(ht1_hi, 1)

            def step(par, j, more=2):
                of_j = landed(j)
                of_next = landed(j + 2) if more == 2 else None
                turn1(j)
                wout1(j, of_j)
                if more >= 1:
                    silu1(j + 1)
                if more >= 2:
                    win1(j + 2, of_next)
                    xt1(par, j + 2)

            act.wait_ge(y0_done, TILES0)
            split1(win_in[1], 16, win_hi[1], piece_in)
            split1(wout_in[1], 16, wout_hi[1], piece_out)
            act.sem_inc(silu_done, 2)
            act.wait_ge(tab_ready, 1)
            win1(0, landed(0))
            xt1(0, 0)
            xt1(1, 1)
            silu1(0)
            win1(1, landed(1))
            with act.Fori(0, (TILES1 - 3) // 2) as i:
                for par in range(2):
                    j = i * 2 + par
                    step(par, j)
            for j in range(TILES1 - 3, TILES1):
                step(j % 2, j, more=min(2, TILES1 - 1 - j))

        @block.vector
        def _(dve):
            links = [0]

            def link(ins):
                links[0] += 1
                ins.then_inc(chain, 1)
                dve.wait_ge(chain, links[0])

            def norm_stats(n, q):
                for b in range(QB):
                    ins = dve.bn_stats(stats[:, b, :], xs[:, q * QB + b, :])
                link(ins)
                for b in range(QB):
                    ins = dve.bn_aggr(mv[:, n, b, :], stats[:, b, :])
                link(ins)
                dve.sem_inc(var_ready, 1)

            def normalise(n, q, dst):
                dve.wait_ge(sd_ready, SD[n, q])
                link(dve.reciprocal(rstd[:, n, :], sd[:, n, :]))
                for b in range(QB):
                    ins = dve.tensor_scalar(dst[:, b, :], xs[:, q * QB + b, :], mv[:, n, b, 0:1], rstd[:, n, b:b + 1],
                                            ALU.subtract, ALU.mult)
                return ins

            dve.wait_ge(tanh_ready, 1)
            for t in range(NQ + 2):
                if 0 <= t - 2 < NQ:
                    q = t - 2
                    if q >= 2:
                        dve.wait_ge(xn_out0[q % 2], 16 * (q // 2))
                        dve.wait_ge(xn_read, q - 1)
                    link(normalise(1, q, xn[:, q % 2]))
                    dve.sem_inc(xn_ready, 1)
                if 0 <= t - 1 < NQ:
                    q = t - 1
                    link(normalise(0, q, qT_rows(qT)))
                    dve.wait_ge(ret_done, q + 1)
                    link(dve.scalar_tensor_tensor(qT_flat(qT), qT_flat(qT), tg[:, 0:1], flat(PA[:, :, :]),
                                                  ALU.mult, ALU.mult))
                    dve.sem_inc(ret_used, 1)
                    xq = flat(xs[:, q * QB:(q + 1) * QB, :])
                    link(dve.tensor_tensor(xq, xq, qT_flat(qT), ALU.add))
                    norm_stats(1, q)
                if t < NQ:
                    dve.wait_ge(x_in[t], 16)
                    norm_stats(0, t)

            link(dve.tensor_copy(cb[:, :], cf[:, CF["before"][0]:CF["iota"][1]]))
            dve.sem_inc(cb_ready, 1)

            def best_two(src):
                for b in range(NB):
                    ins = dve.max(top[:, b, :], src[:, b, :])
                link(ins)
                for b in range(NB):
                    ins = dve.max_index(topi[:, b, :], top[:, b, :], src[:, b, :])
                link(ins)
                link(dve.tensor_copy(eidx[:, :].rearrange("p (k b) -> p k b", k=K),
                                     topi[:, :, 0:K].rearrange("p b k -> p k b")))
                link(dve.tensor_tensor(oh[:, :, :], eidx[:, :].unsqueeze(1).broadcast_to([P, E, NG]),
                                       c("iota_e").unsqueeze(2).broadcast_to([P, E, NG]), ALU.is_equal))
                dve.sem_inc(oh_ready, 1)

            def ranks(layer):
                dve.wait_ge(rank_done, layer + 1)
                totals = PD[:, 1, E * NG:2 * E * NG]
                link(dve.tensor_tensor_scan(flat(incl[:, :, :]), c("reset"), totals, 0.0, ALU.mult, ALU.add))
                link(dve.tensor_tensor(flat(loc[:, :, :]), flat(incl[:, :, :]), totals, ALU.subtract))
                link(dve.tensor_tensor(flat(loc[:, :, :]), flat(loc[:, :, :]), PD[:, 1, 0:E * NG], ALU.add))

            def pick(dst):
                link(dve.tensor_tensor(flat(loc[:, :, :]), flat(loc[:, :, :]), flat(oh[:, :, :]), ALU.mult))
                link(dve.tensor_reduce(dst, loc[:, :, :].rearrange("p e g -> p g e"), AX.X, ALU.add))

            def invert(layer, slot):
                link(dve.tensor_copy(smi[:, 0, :], slot))
                link(dve.tensor_scalar(smi[:, 1, :], smi[:, 0, :], P - 1, None, ALU.bitwise_and))
                link(dve.tensor_scalar(smi[:, 2, :], smi[:, 0, :], 7, None, ALU.arith_shift_right))
                link(dve.tensor_copy(sm[:, 6, :], smi[:, 1, :]))
                link(dve.tensor_copy(sm[:, 7, :], smi[:, 2, :]))
                link(dve.tensor_tensor(oha[:, :, :], sm[:, 7, :].unsqueeze(2).broadcast_to([P, NG, NA]),
                                       c("iota_a").unsqueeze(1).broadcast_to([P, NG, NA]), ALU.is_equal))
                dve.tensor_scalar(rhs_a[:, :, 0:NA], oha[:, :, :], c("part"), None, ALU.mult)
                dve.tensor_tensor(rhs_a[:, :, NA:2 * NA], oha[:, :, :],
                                  c("group1").unsqueeze(2).broadcast_to([P, NG, NA]), ALU.mult)
                for g in range(NG):
                    ins = dve.tensor_scalar(ohb[:, g, :], iota_b, sm[:, 6, g:g + 1], None, ALU.is_equal)
                link(ins)
                dve.sem_inc(map_ready, 1)
                dve.wait_ge(map_done, layer + 1)
                part, group = PD[:, 0, 128:128 + NA], PD[:, 0, 128 + NA:128 + 2 * NA]
                link(dve.tensor_copy(inv[:, 0, :], group))
                link(dve.scalar_tensor_tensor(inv[:, 1, :], inv[:, 0, :], float(P), part, ALU.mult, ALU.add))
                link(dve.scalar_tensor_tensor(inv[:, 2, :], inv[:, 1, :], float(-P), c("trash"), ALU.add,
                                              ALU.subtract))
                link(dve.scalar_tensor_tensor(inv[:, 3, :], inv[:, 0, :], 1.0, inv[:, 2, :], ALU.min, ALU.mult))
                link(dve.tensor_tensor(row_y[:, :], inv[:, 3, :], c("trash"), ALU.add))
                link(dve.tensor_scalar(row_x[:, :], row_y[:, :], T - 1, None, ALU.bitwise_and))
                dve.sem_inc(rows_ready, 1)

            def over_e(ap):
                return ap.unsqueeze(2).broadcast_to([P, NB, E])

            dve.wait_ge(lg_done, 1)
            logits = PD[:, 0, 0:NB * E].rearrange("p (b e) -> p b e", e=E)
            link(dve.tensor_reduce(rr[:, 0, :], logits, AX.X, ALU.max))
            link(dve.tensor_tensor(lg[:, :, :], logits, over_e(rr[:, 0, :]), ALU.subtract))
            dve.sem_inc(e_arg, 1)
            dve.wait_ge(e_ready, 1)
            link(dve.tensor_reduce(rr[:, 2, :], pr[:, :, :], AX.X, ALU.add))
            link(dve.reciprocal(rr[:, 3, :], rr[:, 2, :]))
            link(dve.tensor_tensor(pr[:, :, :], pr[:, :, :], over_e(rr[:, 3, :]), ALU.mult))
            best_two(pr)
            ranks(0)
            pick(sm[:, 0, :])
            link(dve.tensor_scalar(sm[:, 1, :], sm[:, 0, :], float(CAP), float(64 * P), ALU.is_ge, ALU.mult))
            link(dve.tensor_tensor(sm[:, 2, :], sm[:, 1, :], sm[:, 0, :], ALU.add))
            link(dve.scalar_tensor_tensor(sm[:, 3, :], eidx[:, :], float(CAP), sm[:, 2, :], ALU.mult, ALU.add))
            dve.wait_ge(zero_out, 16 * K * NQ)
            invert(0, sm[:, 3, :])
            link(dve.tensor_scalar(sm[:, 4, :], sm[:, 0, :], float(CAP), None, ALU.is_lt))
            link(dve.tensor_tensor(sm[:, 5, :].rearrange("p (k b) -> p k b", k=K),
                                   top[:, :, 0:K].rearrange("p b k -> p k b"),
                                   sm[:, 4, :].rearrange("p (k b) -> p k b", k=K), ALU.mult))
            link(dve.tensor_tensor(rr[:, 0, :], sm[:, 5, 0:NB], sm[:, 5, NB:NG], ALU.add))
            link(dve.tensor_scalar(rr[:, 2, :], rr[:, 0, :], 1e-9, None, ALU.max))
            link(dve.reciprocal(rr[:, 3, :], rr[:, 2, :]))
            link(dve.tensor_scalar(rr[:, 3, :], rr[:, 3, :], tg[:, 2:3], None, ALU.mult))
            for k in range(K):
                ins = dve.tensor_tensor(gates[0][:, k * NB:(k + 1) * NB], sm[:, 5, k * NB:(k + 1) * NB], rr[:, 3, :],
                                        ALU.mult)
            link(ins)

            def win0(e, k):
                dve.wait_ge(win_hi[0], e * DC + k + 1)
                at = slice(k * 2 * F0, (k + 1) * 2 * F0)
                dve.tensor_tensor(wlo[:, at], raw[:, at], whi[:, at].bitcast(F32), ALU.subtract)\
                    .then_inc(win_lo[0], 1)

            def wout0(e):
                dve.wait_ge(wout_hi[0], e + 1)
                at = slice(WIN, WIN + WOUT0)
                dve.tensor_tensor(wlo[:, at], raw[:, at], whi[:, at].bitcast(F32), ALU.subtract)\
                    .then_inc(wout_lo[0], 1)

            def xt0(par, e):
                for t in range(CT):
                    dve.wait_ge(xt0_hi, e * CT + t + 1)
                    at = xlo[:, :, t * P:(t + 1) * P]
                    dve.tensor_tensor(at, bank0(par, t), xhi[:, :, t * P:(t + 1) * P].bitcast(F32), ALU.subtract)\
                        .then_inc(xt0_lo, 1)

            def hid0(e, first=False):
                for s in range(STEPS0 + 1):
                    if s < STEPS0:
                        dve.wait_ge(gelu_done, e * STEPS0 + s + 1)
                        dve.tensor_tensor(ga[:, s % 4, :], ga[:, s % 4, :], (PA, PC)[s % 2][:, 1, 0:HALF],
                                          ALU.mult).then_inc(hid0_used, 1)
                    if s >= 1:
                        dve.wait_ge(h0_hi, e * STEPS0 + s)
                        dve.tensor_tensor(hid_at(hlo, s - 1), ga[:, (s - 1) % 4, :],
                                          hid_at(hhi, s - 1).bitcast(F32), ALU.subtract).then_inc(h0_lo, 1)
                    if s == 2 and not first:
                        wout0(e)

            def out0(e):
                for k in range(DC):
                    win0(e + 1, k)

            dve.sem_inc(xt0_lo, 2)
            dve.sem_inc(hid0_used, 2)
            dve.sem_inc(h0_lo, 4)
            dve.sem_inc(ys0_free, 2 * CT)
            for k in range(DC):
                win0(0, k)
            wout0(0)
            xt0(0, 0)
            hid0(0, first=True)
            xt0(1, 1)
            out0(0)
            with dve.Fori(0, E // 2 - 1) as i:
                for par in (1, 0):
                    e = i * 2 + 2 - par
                    hid0(e)
                    xt0(1 - par, e + 1)
                    out0(e)
            hid0(E - 1)

            def combine(layer, q):
                dve.wait_ge(y_in[q % 2], 32 * (2 * layer + q // 2 + 1))
                for k in range(K):
                    for b in range(QB):
                        n = q * QB + b
                        ins = dve.scalar_tensor_tensor(xs[:, n, :], yk(q, k)[:, b, :],
                                                       gates[layer][:, k * NB + n:k * NB + n + 1], xs[:, n, :],
                                                       ALU.mult, ALU.add)
                    link(ins)
                dve.sem_inc(yk_used, 1)

            for t in range(NQ + 4):
                if 0 <= t - 4 < NQ:
                    q = t - 4
                    if q >= 1:
                        dve.wait_ge(xn_out1, 16 * q)
                        dve.wait_ge(xn_read, NQ + SDX[3, q - 1])
                    link(normalise(3, q, xn[:, 1]))
                    dve.sem_inc(xn_ready, 1)
                if 0 <= t - 3 < NQ:
                    q = t - 3
                    dve.wait_ge(exp_done, q + 1)
                    link(dve.reciprocal(att[:, 3, :], att[:, 2, :]))
                    link(dve.tensor_scalar(att[:, 3, :], att[:, 3, :], tg[:, 1:2], None, ALU.mult))
                    dve.wait_ge(pv_done, q + 1)
                    for b in range(QB):
                        xb = xs[:, q * QB + b, :]
                        ins = dve.scalar_tensor_tensor(xb, PC[:, b // 2, (b % 2) * D:(b % 2 + 1) * D],
                                                       att[:, 3, b:b + 1], xb, ALU.mult, ALU.add)
                    link(ins)
                    dve.sem_inc(pv_used, 1)
                    norm_stats(3, q)
                if 0 <= t - 2 < NQ:
                    q = t - 2
                    dve.wait_ge(sc_done, q + 1)
                    if q >= 1:
                        dve.wait_ge(exp_done, q)
                    link(dve.scalar_tensor_tensor(flat(sc[:, :, :]), mask8[:, q * QN:(q + 1) * QN], NEG, PA[:, 0, :],
                                                  ALU.mult, ALU.add))
                    link(dve.tensor_reduce(att[:, 0, :], sc[:, :, :], AX.X, ALU.max))
                    link(dve.tensor_scalar(att[:, 1, :], att[:, 0, :], -SCALE, None, ALU.mult))
                    dve.sem_inc(sc_ready, 1)
                if 0 <= t - 1 < NQ:
                    q = t - 1
                    if q >= 1:
                        dve.wait_ge(xn_read, NQ + SDX[2, q - 1])
                    link(normalise(2, q, xn[:, 0]))
                    dve.sem_inc(xn_ready, 1)
                if t < NQ:
                    combine(0, t)
                    norm_stats(2, t)

            dve.wait_ge(lg_done, 2)
            link(dve.tensor_copy(lg[:, :, :], logits))
            best_two(lg)
            ranks(1)
            link(dve.tensor_scalar(tei[:, 0, :], incl[:, :, NG - 1], float(P - 1), None, ALU.add))
            link(dve.tensor_scalar(tei[:, 1, :], tei[:, 0, :], 7, None, ALU.arith_shift_right))
            link(dve.tensor_copy(te[:, 0, :], tei[:, 1, :]))
            link(dve.tensor_tensor_scan(te[:, 1, :], c("ones")[:, 0:E], te[:, 0, :], 0.0, ALU.mult, ALU.add))
            link(dve.tensor_tensor(te[:, 2, :], te[:, 1, :], te[:, 0, :], ALU.subtract))
            link(dve.tensor_scalar(te[:, 3, :], te[:, 2, :], float(P), None, ALU.mult))
            link(dve.tensor_tensor(loc[:, :, :], loc[:, :, :], te[:, 3, :].unsqueeze(2).broadcast_to([P, E, NG]),
                                   ALU.add))
            pick(sm[:, 0, :])
            invert(1, sm[:, 0, :])
            over_a = c("iota_a").unsqueeze(2).broadcast_to([P, NA, E])
            ends, starts = (te[:, n, :].unsqueeze(1).broadcast_to([P, NA, E]) for n in (1, 2))
            link(dve.tensor_tensor(tab, over_a, ends, ALU.is_ge))
            link(dve.tensor_reduce(tabf[:, 0, :], tab, AX.X, ALU.add))
            link(dve.tensor_scalar(tabi[:, TAB_EXPERT, :], tabf[:, 0, :], float(E - 1), None, ALU.min))
            link(dve.tensor_tensor(tab, over_a, starts, ALU.is_ge))
            link(dve.tensor_tensor(tab, tab, starts, ALU.mult))
            link(dve.tensor_reduce(tabf[:, 1, :], tab, AX.X, ALU.max))
            link(dve.tensor_tensor(tabf[:, 2, :], tabf[:, 1, :], c("iota_a"), ALU.is_equal))
            link(dve.tensor_scalar(tabf[:, 2, 0:1], te[:, 1, 0:1], 0.0, None, ALU.is_equal))
            dve.memset(tabf[:, 3, 0:1], 1.0)
            link(dve.tensor_scalar(tabf[:, 3, 1:NA], tabf[:, 1, 0:NA - 1], 2.0, None, ALU.add))
            link(dve.tensor_scalar(tabi[:, TAB_SPLIT, :], tabf[:, 3, :], float(PIECES), None, ALU.mult))
            link(dve.tensor_tensor_scan(tabf[:, 4, :], c("ones")[:, 0:NA], tabf[:, 2, :], 1.0, ALU.mult, ALU.add))
            link(dve.scalar_tensor_tensor(tabi[:, TAB_LANDED, :], tabf[:, 4, :], 16.0, tabf[:, 2, :], ALU.mult,
                                          ALU.mult))
            dve.sem_inc(tab_ready, 1)
            link(dve.tensor_tensor(rr[:, 0, :], top[:, :, 1], top[:, :, 0], ALU.subtract))
            dve.sem_inc(e_arg, 1)
            dve.wait_ge(e_ready, 2)
            link(dve.tensor_scalar(rr[:, 2, :], rr[:, 1, :], 1.0, None, ALU.add))
            link(dve.reciprocal(rr[:, 3, :], rr[:, 2, :]))
            link(dve.tensor_scalar(gates[1][:, 0:NB], rr[:, 3, :], tg[:, 3:4], None, ALU.mult))
            link(dve.tensor_tensor(gates[1][:, NB:NG], gates[1][:, 0:NB], rr[:, 1, :], ALU.mult))

            def low(dst, src, hi):
                return dve.tensor_tensor(dst, src, hi.bitcast(F32), ALU.subtract)

            def landed(j):
                return dve.value_load(tabi[0:1, TAB_LANDED, bass.ds(j, 1)], min_val=0, max_val=16 * (E + 1))

            def split1(before_it, hi_done, done, pieces):
                for n in range(PIECES):
                    dve.wait_ge(hi_done, before_it + n + 1)
                    low(wlo[:, pieces(n)], raw[:, pieces(n)], whi[:, pieces(n)]).then_inc(done, 1)

            def win1(j, new):
                with dve.If(new > 0):
                    split1(j * PIECES + PIECES, win_hi[1], win_lo[1], piece_in)
                with dve.Else():
                    dve.drain().then_inc(win_lo[1], PIECES)

            def wout1(j, new):
                with dve.If(new > 0):
                    split1(j * PIECES + PIECES, wout_hi[1], wout_lo[1], piece_out)
                with dve.Else():
                    dve.drain().then_inc(wout_lo[1], PIECES)

            def xt1(par, j):
                dve.wait_ge(xt1_hi, j + 1)
                low(xlo[:, par, 0:D], PB[:, par, 0:D], xhi[:, par, 0:D]).then_inc(xt1_lo, 1)

            def evac1(par, j):
                dve.wait_ge(y1_done, j + 2)
                dve.wait_ge(ys1_free, j + 1)
                dve.tensor_copy(ys[:, par, :], PD[:, par, 0:D]).then_inc(y1_evac, 1)

            def step(par, j, more=True, last=True):
                of_j = landed(j)
                of_next = landed(j + 2) if more else None
                if last:
                    evac1(1 - par, j - 1)
                for n in range(2):
                    dve.wait_ge(ht1_hi, j * 2 + n + 1)
                    at = slice(n * 512, (n + 1) * 512)
                    low(hlo[:, at], PC[:, n, :], hhi[:, at]).then_inc(ht1_lo, 1)
                wout1(j, of_j)
                if more:
                    win1(j + 2, of_next)
                    xt1(par, j + 2)

            dve.sem_inc(xt1_lo, 2)
            dve.sem_inc(ht1_lo, 2)
            dve.sem_inc(y1_evac, 2)
            dve.sem_inc(ys1_free, 2)
            split1(0, win_hi[1], win_lo[1], piece_in)
            split1(0, wout_hi[1], wout_lo[1], piece_out)
            win1(0, landed(0))
            xt1(0, 0)
            xt1(1, 1)
            win1(1, landed(1))
            step(0, 0, last=False)
            with dve.Fori(0, (TILES1 - 3) // 2) as i:
                for par in (1, 0):
                    step(par, i * 2 + 2 - par)
            for j in range(TILES1 - 2, TILES1):
                step(j % 2, j, more=False)
            evac1((TILES1 - 1) % 2, TILES1 - 1)

            for q in range(NQ):
                combine(1, q)
                dve.sem_inc(fin_ready, 1)

        @block.tensor
        def _(pe):
            def turn(src):
                for k in range(DC):
                    for b in range(QB):
                        mm = pe.transpose(PB[:, k, b * P:(b + 1) * P], src[:, b, k * P:(k + 1) * P], ident)
                return mm

            def product(dst, lhs, rhs):
                for k, (a, b) in enumerate(zip(lhs, rhs)):
                    mm = pe.matmul(dst, a, b, start=(k == 0), stop=(k == len(lhs) - 1))
                return mm

            def router(layer, q):
                for b in range(QB):
                    mm = product(PD[:, 0, (q * QB + b) * E:(q * QB + b + 1) * E],
                                 [xT[:, k, b * P:(b + 1) * P] for k in range(DC)],
                                 [wg[:, layer, k, :] for k in range(DC)])
                if q == NQ - 1:
                    mm.then_inc(lg_done, 1)

            pe.wait_ge(cf_in, 16)
            for t in range(NQ + 2):
                if t < NQ:
                    pe.wait_ge(sq_ready, t + 1)
                    if t >= 1:
                        pe.wait_ge(ret_used, t)
                    for n in range(2):
                        mm = pe.matmul(PA[:, n, :], decay, flat(cx2[:, t % 2, 2 * n:2 * n + 2, :]),
                                       start=True, stop=True)
                    mm.then_inc(ret_done, 1)
                if 0 <= t - 2 < NQ:
                    q = t - 2
                    pe.wait_ge(xn_ready, q + 1)
                    if q >= 1:
                        pe.wait_ge(evac_done, EV1["xT", q - 1])
                    turn(xn[:, q % 2]).then_inc(evac_ready, 1)
                    pe.wait_ge(evac_done, EV1["xT", q])
                    pe.sem_inc(xn_read, 1)
                    router(0, q)

            def keys(q):
                pe.wait_ge(evac_done, EV1["ctxT", q] - 1)
                turn(cx[:, q * QB:(q + 1) * QB, :]).then_inc(evac_ready, 1)
                pe.wait_ge(small_in, 16 * 8)
                pe.wait_ge(evac_done, EV1["ctxT", q])
                for m in range(DC):
                    mm = product(PC[:, m, :], [wqkv[:, 1, k, m * P:(m + 1) * P] for k in range(DC)],
                                 [xT[:, k, :] for k in range(DC)])
                mm.then_inc(evac_ready, 1)
                pe.wait_ge(evac_done, EV1["kT", q])
                for b in range(QB):
                    mm = product(PC[:, b // 2, (b % 2) * D:(b % 2 + 1) * D],
                                 [xT[:, k, b * P:(b + 1) * P] for k in range(DC)],
                                 [wqkv[:, 2, k, :] for k in range(DC)])
                mm.then_inc(evac_ready, 1)

            def ranks(layer):
                pe.wait_ge(oh_ready, layer + 1)
                pe.matmul(PD[:, 1, 0:E * NG], before, flat(oh[:, :, :]), start=True, stop=True)
                pe.matmul(PD[:, 1, E * NG:2 * E * NG], ones_b, flat(oh[:, :, :]), start=True, stop=True)\
                    .then_inc(rank_done, 1)

            def invert(layer):
                pe.wait_ge(map_ready, layer + 1)
                for g in range(NG):
                    mm = pe.matmul(PD[:, 0, 128:128 + 2 * NA], ohb[:, g, :], rhs_a[:, g, :], start=(g == 0),
                                   stop=(g == NG - 1))
                mm.then_inc(map_done, 1)

            keys(0)
            pe.wait_ge(cb_ready, 1)
            ranks(0)
            keys(1)
            invert(0)
            keys(2)
            keys(3)

            def exact(dst, lhs_hi, lhs_lo, rhs_hi, rhs_lo, first=True, last=True):
                n = len(lhs_hi)
                for k in range(n):
                    for a, b in ((lhs_hi, rhs_hi), (lhs_hi, rhs_lo), (lhs_lo, rhs_hi)):
                        mm = pe.matmul(dst, a[k], b[k], start=(first and k == 0 and a is lhs_hi and b is rhs_hi),
                                       stop=(last and k == n - 1 and a is lhs_lo))
                return mm

            def xt0(i, par, e):
                for t in range(CT):
                    s = par * CT + t
                    pe.wait_ge(g0_in[s], i * 16 + 16)
                    pe.wait_ge(xt0_lo, e * CT + t + 1)
                    for k in range(DC):
                        mm = pe.transpose(PB[:, s % 2, k * P:(k + 1) * P], xg[:, s, k * P:(k + 1) * P], ident)
                    mm.then_inc(xt0_done, 1)

            def hid0(i, par, e):
                pe.wait_ge(win_lo[0], e * DC + DC)
                pe.wait_ge(xt0_lo, e * CT + CT + 2)
                for s in range(STEPS0):
                    half, fb = divmod(s, FB0)
                    pe.wait_ge(hid0_used, e * STEPS0 + s + 1)
                    for n in range(2):
                        col = n * F0 + fb * P
                        mm = exact((PA, PC)[s % 2][:, n, 0:HALF],
                                   *([w[:, col + k * 2 * F0:col + k * 2 * F0 + P] for k in range(DC)]
                                     for w in (whi, wlo)),
                                   *([v[:, k, half * HALF:(half + 1) * HALF] for k in range(DC)] for v in (xhi, xlo)))
                    mm.then_inc(hid0_done, 1)

            def out0(i, par, e):
                pe.wait_ge(wout_lo[0], e + 1)
                pe.wait_ge(h0_lo, e * STEPS0 + STEPS0 + 4)
                for t in range(CT):
                    pe.wait_ge(y0_evac, e * CT + t + 1)
                    exact(PD[:, (par * CT + t) % 2, 0:D],
                          *([h[:, f * CAP + t * P:f * CAP + (t + 1) * P] for f in range(FB0)] for h in (hhi, hlo)),
                          *([w[:, WIN + f * D:WIN + (f + 1) * D] for f in range(FB0)] for w in (whi, wlo)))\
                        .then_inc(y0_done, 1)

            pe.wait_ge(evac_done, len(EV1))
            xt0(0, 0, 0)
            with pe.Fori(0, E // 2 - 1) as i:
                for par in range(2):
                    e = i * 2 + par
                    hid0(i, par, e)
                    xt0(i + par, 1 - par, e + 1)
                    out0(i, par, e)
            i = E // 2 - 1
            hid0(i, 0, E - 2)
            xt0(i, 1, E - 1)
            out0(i, 0, E - 2)
            hid0(i, 1, E - 1)
            out0(i, 1, E - 1)

            for t in range(NQ + 4):
                if 0 <= t - 4 < NQ:
                    q = t - 4
                    pe.wait_ge(xn_ready, NQ + SDX[3, q])
                    pe.wait_ge(evac2_done, EV2["xT4", q] - 1)
                    turn(xn[:, 1]).then_inc(evac2_ready, 1)
                    pe.wait_ge(evac2_done, EV2["xT4", q])
                    pe.sem_inc(xn_read, 1)
                    router(1, q)
                if 0 <= t - 3 < NQ:
                    q = t - 3
                    pe.wait_ge(exp_done, q + 1)
                    pe.wait_ge(evac2_done, EV2["pT", q] - 1)
                    for b in range(QB):
                        mm = pe.transpose(PA[:, 1, b * S:(b + 1) * S], prb[:, b, :], ident)
                    mm.then_inc(evac2_ready, 1)
                    pe.wait_ge(evac2_done, EV2["pT", q])
                    pe.wait_ge(v_ready, NQ)
                    for b in range(QB):
                        mm = pe.matmul(PC[:, b // 2, (b % 2) * D:(b % 2 + 1) * D], pT[:, b, :], vv[:, q * QB + b, :],
                                       start=True, stop=True)
                    mm.then_inc(pv_done, 1)
                if 0 <= t - 2 < NQ:
                    q = t - 2
                    pe.wait_ge(evac2_done, EV2["qT", q])
                    if q >= 1:
                        pe.wait_ge(sc_ready, q)
                    for b in range(QB):
                        n = (q * QB + b) * S
                        mm = product(PA[:, 0, b * S:(b + 1) * S],
                                     [qT[:, k, b * P:(b + 1) * P] for k in range(DC)] + [ident],
                                     [kT[:, k, n:n + S] for k in range(DC)] + [c("causal")])
                    mm.then_inc(sc_done, 1)
                if 0 <= t - 1 < NQ:
                    q = t - 1
                    pe.wait_ge(xn_ready, NQ + SDX[2, q])
                    if EV2["xT3", q] > 1:
                        pe.wait_ge(evac2_done, EV2["xT3", q] - 1)
                    turn(xn[:, 0]).then_inc(evac2_ready, 1)
                    pe.wait_ge(evac2_done, EV2["xT3", q])
                    pe.sem_inc(xn_read, 1)
                    if q >= 2:
                        pe.wait_ge(pv_used, q - 1)
                    for m in range(DC):
                        mm = product(PC[:, m, :], [wqkv[:, 0, k, m * P:(m + 1) * P] for k in range(DC)],
                                     [xT[:, k, :] for k in range(DC)])
                    mm.then_inc(evac2_ready, 1)
            ranks(1)
            invert(1)

            def xt1(i, par, j):
                pe.wait_ge(g1_in[par], i * 16 + 16)
                pe.wait_ge(xt1_lo, j + 1)
                for k in range(DC):
                    mm = pe.transpose(PB[:, par, k * P:(k + 1) * P], xg[:, par, k * P:(k + 1) * P], ident)
                mm.then_inc(xt1_done, 1)

            def hid1(par, j):
                pe.wait_ge(xt1_lo, j + 3)
                for f in range(2):
                    pe.wait_ge(win_lo[1], (j + 1) * PIECES + 2 * f + 2)
                    pe.wait_ge(silu_done, j * 2 + f + 1)
                    exact(PA[:, f, :], *([v[:, par, k * P:(k + 1) * P] for k in range(DC)] for v in (xhi, xlo)),
                          *([w[:, k * F1 + f * 512:k * F1 + (f + 1) * 512] for k in range(DC)] for w in (whi, wlo)))\
                        .then_inc(hid1_done, 1)

            def turn1(j):
                for n in range(2):
                    pe.wait_ge(silu_done, j * 2 + n + 3)
                    pe.wait_ge(ht1_lo, j * 2 + n + 1)
                    for b in range(4):
                        f = n * 4 + b
                        mm = pe.transpose(PC[:, n, b * P:(b + 1) * P], h1[:, f * P:(f + 1) * P], ident)
                    mm.then_inc(ht1_done, 1)

            def out1(par, j):
                pe.wait_ge(ht1_lo, j * 2 + 4)
                pe.wait_ge(y1_evac, j + 1)
                per = FB1 // PIECES
                for n in range(PIECES):
                    pe.wait_ge(wout_lo[1], (j + 1) * PIECES + n + 1)
                    mm = exact(PD[:, par, 0:D], *([h[:, f * P:(f + 1) * P] for f in range(n * per, (n + 1) * per)]
                                                  for h in (hhi, hlo)),
                               *([w[:, WIN + f * D:WIN + (f + 1) * D] for f in range(n * per, (n + 1) * per)]
                                 for w in (whi, wlo)), first=n == 0, last=n == PIECES - 1)
                mm.then_inc(y1_done, 1)

            pe.sem_inc(y1_done, 1)
            pe.sem_inc(hid1_done, 1)
            xt1(0, 0, 0)
            xt1(0, 1, 1)
            hid1(0, 0)
            with pe.Fori(0, (TILES1 - 3) // 2) as i:
                for par in range(2):
                    j = i * 2 + par
                    turn1(j)
                    hid1(1 - par, j + 1)
                    xt1(i + 1, par, j + 2)
                    out1(par, j)
            for j in range(TILES1 - 3, TILES1):
                turn1(j)
                if j + 1 < TILES1:
                    hid1((j + 1) % 2, j + 1)
                if j + 2 < TILES1:
                    xt1(j // 2 + 1, j % 2, j + 2)
                out1(j % 2, j)


def flat(ap):
    return ap.rearrange("p a b -> p (a b)")


def qT_flat(t):
    return flat(t[:, :, :])


def qT_rows(t):
    return qT_flat(t).rearrange("p (b d) -> p b d", d=D)


SDX = {}
for _t in range(NQ + 4):
    for _n, _lag in ((3, 4), (2, 1)):
        if 0 <= _t - _lag < NQ:
            SDX[_n, _t - _lag] = len(SDX) + 1


def kernel(**inputs):
    import concourse.bacc as bacc
    from concourse.bass_utils import run_bass_kernel_spmd

    nc = bacc.Bacc("TRN2", target_bir_lowering=False, num_devices=1)
    arrays, args = {}, []

    def give(name, a):
        a = np.ascontiguousarray(a)
        arrays[name] = a
        args.append(nc.dram_tensor(name, a.shape, mybir.dt.from_np(a.dtype), kind="ExternalInput").ap())

    for name in ("x", "ctx_1024", "mask_Bx1xS2_bk0", "g_xattn", "g_ffn", "L0_ffn_Wg", "L0_ffn_W_in", "L0_ffn_W_out"):
        give(name, inputs[name])
    for m in "qkv":
        give(f"w{m}T", np.asarray(inputs[f"L1_xattn_W{m}"]).T)
        b = np.asarray(inputs[f"L1_xattn_b{m}"])
        give(f"b{m}", b if m == "v" else b.reshape(DC, P).T)
    give("gate_wT", np.asarray(inputs["L1_ffn_gate_w"]).T)
    give("w1", inputs["L1_ffn_w1"])
    give("w2", inputs["L1_ffn_w2"])
    give("tables", constants())
    out = nc.dram_tensor("out", (NB, S, D), F32, kind="ExternalOutput").ap()
    build(nc, *args, out)
    r = run_bass_kernel_spmd(nc, [arrays], core_ids=[0])
    return r.results[0]["out"]
```

```python
import math
from contextlib import ExitStack

import numpy as np

import concourse.bass as bass
from concourse import mybir

ALU = mybir.AluOpType
ACT = mybir.ActivationFunctionType
AX = mybir.AxisListType
F32 = mybir.dt.float32
F32R = mybir.dt.float32r
BF16 = mybir.dt.bfloat16
I32 = mybir.dt.int32
U32 = mybir.dt.uint32
U8 = mybir.dt.uint8

P = 128
NB, S, D = 16, 128, 256
T = NB * S
DC = D // P
E, K = 8, 2
QB = 4
NQ = NB // QB
QN = QB * P
NG = K * NB
F0 = 512
F1 = 1024
CAP = math.ceil(K * T / E * 1.25)
CT = CAP // P
TILES0 = E * CT
PAIRS = (CT + 1) // 2
FULL1 = K * T // P
TILES1 = FULL1 + E - 1
NA = max(TILES0, TILES1 + 1)
HALF = CAP // 2
FB0 = F0 // P
FB1 = F1 // P
PIECES = 4
STEPS0 = 2 * FB0
LN_EPS = 1e-5
NEG = -1.0e30
WIN = DC * 2 * F0
WOUT0 = F0 // P * D
WOUT1 = F1 // P * D
SCALE = 1.0 / math.sqrt(D)

_at, CF = 0, {}
for _n, _w in (("ident", P), ("decay", P), ("causal", P), ("reset", E * NG), ("iota_e", E), ("iota_a", NA),
               ("trash", NA), ("part", 1), ("eps", 1), ("group1", NG),
               ("before", P), ("ones", P), ("iota", P)):
    CF[_n] = (_at, _at + _w)
    _at += _w
CF_W = _at
CB = {"before": (0, P), "ones": (P, 2 * P)}


def constants():
    f = np.zeros((P, CF_W), np.float32)
    r = np.arange(P)

    def put(name, value):
        f[:, slice(*CF[name])] = value

    put("ident", np.eye(P))
    lag = r[None, :] - r[:, None]
    put("decay", np.where(lag >= 0, np.float64(np.float32(0.9)) ** np.maximum(lag, 0), 0.0))
    put("causal", np.where(r[None, :] <= r[:, None], 0.0, NEG))
    put("reset", np.tile(np.arange(NG) > 0, E)[None, :])
    put("iota_e", np.arange(E)[None, :])
    put("iota_a", np.arange(NA)[None, :])
    put("trash", K * T + P * np.arange(NA)[None, :] + r[:, None])
    put("part", r[:, None])
    put("eps", LN_EPS)
    put("group1", np.arange(1, NG + 1)[None, :])
    put("ones", 1.0)
    put("before", r[:, None] < r[None, :])
    put("iota", r[None, :])
    return f


def build(nc, x, ctxt, mask, g_xattn, g_ffn, wg0, w_in, w_out, wq, bq, wk, bk, wvT, bv, wg1T, w1, w2, cf_d, out):
    with ExitStack() as ctx:
        def sb(name, shape, dt=F32):
            return ctx.enter_context(nc.sbuf_tensor(name, shape, dt))

        def sem(name):
            return ctx.enter_context(nc.semaphore(name))

        xn_rows = [nc.dram_tensor(f"xn_rows{layer}", [T, D], F32) for layer in (0, 1)]
        y_rows = [nc.dram_tensor(f"y_rows{layer}", [K * T + NA * P, D], F32) for layer in (0, 1)]

        cf = sb("cf", [P, CF_W])
        cb = sb("cb", [P, 2 * P], BF16)
        xs = sb("xs", [P, NB, D])
        cx = sb("cx", [P, NB, D])
        gT = sb("gT", [P, DC, T])
        vv = sb("vv", [P, NB, D])
        xn = sb("xn", [P, 2, QB, D])
        xT = sb("xT", [P, DC, QN])
        h1 = flat(xT[:, :, :])
        raw = sb("raw", [P, WIN + WOUT1])
        cx2 = raw[:, 0:2 * QB * D].rearrange("p (n b d) -> p n b d", n=2, b=QB)
        whi, wlo = (sb(n, [P, WIN + WOUT1], F32R) for n in ("whi", "wlo"))
        xhi, xlo = (sb(n, [P, DC, CAP], F32R) for n in ("xhi", "xlo"))
        hhi, hlo = (sb(n, [P, FB0 * CAP], F32R) for n in ("hhi", "hlo"))
        bias_at = flat(cx[:, 0:NB // 2, :])
        xg = sb("xg", [P, 2 * CT, D])
        ys = sb("ys", [P, 2 * CT, D])
        mask8 = sb("mask8", [P, NB * S], U8)
        wqkv = sb("wqkv", [P, 3, DC, D])
        bqk = sb("bqk", [P, 2, DC])
        bvb = sb("bvb", [P, D])
        wg = sb("wg", [P, 2, DC, E])
        gts = sb("gts", [P, 4])
        tg = sb("tg", [P, 4])
        stats = sb("stats", [P, QB, 6])
        mv = sb("mv", [P, 3 + NQ, QB, 2])
        sd = sb("sd", [P, 3 + NQ, QB])
        rstd = sb("rstd", [P, 3 + NQ, QB])
        nmr = sb("nmr", [P, 3 + NQ, QB])
        gbias = sb("gbias", [P, DC])
        lg = sb("lg", [P, NB, E])
        pr = sb("pr", [P, NB, E])
        top = sb("top", [P, NB, 8])
        topi = sb("topi", [P, NB, 8], U32)
        eidx = sb("eidx", [P, NG])
        oh = sb("oh", [P, E, NG], BF16)
        incl = sb("incl", [P, E, NG])
        loc = sb("loc", [P, E, NG])
        sm = sb("sm", [P, 8, NG])
        smi = sb("smi", [P, 4, NG], I32)
        rr = sb("rr", [P, 4, NB])
        xflat = flat(xg[:, :, :])
        oha = xflat[:, 0:NG * NA].rearrange("p (g a) -> p g a", g=NG)
        ring = sb("ring", [P, NG * NA])
        rhs_a = ring[:, :].bitcast(BF16).rearrange("p (g a) -> p g a", g=NG)
        ga = ring[:, 0:4 * HALF].rearrange("p (n c) -> p n c", n=4)
        ohb = flat(ys[:, :, :])[:, 0:NG * P // 2].bitcast(BF16).rearrange("p (g n) -> p g n", g=NG)
        inv = sb("inv", [P, 4, NA])
        row_y = sb("row_y", [P, NA], I32)
        row_x = sb("row_x", [P, NA], I32)
        gates = [sb(f"gates{layer}", [P, NG]) for layer in (0, 1)]
        te = sb("te", [P, 4, E])
        tei = sb("tei", [P, 4, E], I32)
        tab = ring[:, 0:NA * E].rearrange("p (a e) -> p a e", e=E)
        tabf = sb("tabf", [P, 6, NA])
        full = sb("full", [P, E], I32)
        tabi = sb("tabi", [P, 4, NA], I32)
        def context_at(name, q):
            at = {"cT": (raw[:, WIN + WOUT0:WIN + WOUT0 + DC * QN], flat(ys[:, QB:2 * QB, :]))[q % 2],
                  "cT again": (raw[:, WIN + WOUT0:WIN + WOUT0 + DC * QN], flat(xT[:, :, :]),
                               flat(xn[:, 1]), flat(xT[:, :, :]))[q]}[name]
            return at.rearrange("p (c n) -> p c n", c=DC)

        u_wide = wqkv[:, 0, 0, :].rearrange("p (c n) -> p c n", c=DC)
        wkqT = wqkv[:, 1]
        bq_wide, bk_wide = (ys[:, 2 * QB + n, :].rearrange("p (c n) -> p c n", c=DC) for n in range(2))
        xn0 = [at[:, 0:QB * D].rearrange("p (b d) -> p b d", b=QB) for at in (xflat, ring)]
        prb, pT = (xflat[:, n * QN:(n + 1) * QN].rearrange("p (b s) -> p b s", b=QB) for n in range(2))
        att = sb("att", [P, 2, 4, QB])

        def psum(name):
            return ctx.enter_context(nc.psum_tensor(name, [P, 2, 512], F32))

        PA, PB, PC, PD = psum("PA"), psum("PB"), psum("PC"), psum("PD")

        def c(name):
            return cf[:, CF[name][0]:CF[name][1]]

        ident, decay = c("ident"), c("decay")
        before, ones_b = (cb[:, a:b] for a, b in (CB["before"], CB["ones"]))

        def wout_half(k):
            return slice(WIN + k * WOUT0 // 2, WIN + (k + 1) * WOUT0 // 2)

        def tiles_of(pair):
            return range(2 * pair, min(2 * pair + 2, CT))

        def bank0(pair):
            return PB[:, pair % 2, 0:len(tiles_of(pair)) * D].rearrange("p (t c n) -> p t c n", c=DC, n=P)

        def pair_at(x, pair):
            at = tiles_of(pair)
            return x[:, :, at[0] * P:(at[-1] + 1) * P].rearrange("p c (t n) -> p t c n", n=P)

        def hid_at(h, s):
            half, fb = divmod(s, FB0)
            return h[:, fb * CAP + half * HALF:fb * CAP + (half + 1) * HALF]

        def place(n, q):
            return n + (q if n == 3 else 0)

        def xn3(q):
            return 0 if q == NQ - 2 else 1

        def yk(layer, q, k):
            if layer == 0:
                return ((ys[:, 0:QB, :], ys[:, QB:2 * QB, :]),
                        (xg[:, 2 * CT - QB:2 * CT, :], ring[:, 0:QB * D].rearrange("p (b d) -> p b d", b=QB)))[q % 2][k]
            rows = cx[:, :, :] if q < 2 else gT[:, :, :].rearrange("p c (b d) -> p (c b) d", d=D)
            return rows[:, (2 * (q % 2) + k) * QB:(2 * (q % 2) + k + 1) * QB, :]

        cf_in, cb_ready, g_in, small_in, mask_in = (sem(n) for n in (
            "cf_in", "cb_ready", "g_in", "small_in", "mask_in"))
        x_in = [sem(f"x_in{q}") for q in range(NQ)]
        ctx_in = [sem(f"ctx_in{q}") for q in range(NQ)]
        zero_ready, zero_out = sem("zero_ready"), sem("zero_out")
        sq_ready, ret_done, ret_used = sem("sq_ready"), sem("ret_done"), sem("ret_used")
        evac_ready, evac_done = sem("evac_ready"), sem("evac_done")
        v_ready = sem("v_ready")
        var_ready, sd_ready = sem("var_ready"), sem("sd_ready")
        coef_ready, xn0_ready, wide_ready, pad_ready = (sem(n) for n in (
            "coef_ready", "xn0_ready", "wide_ready", "pad_ready"))
        xn_ready, lg_done, lg_used, tanh_ready = (sem(n) for n in (
            "xn_ready", "lg_done", "lg_used", "tanh_ready"))
        xn_out0 = [sem("xn_out0a"), sem("xn_out0b")]
        xn_out1 = [sem("xn_out1a"), sem("xn_out1b")]
        chain = sem("dve_chain")
        e_arg, e_ready = sem("e_arg"), sem("e_ready")
        oh_ready, rank_done, map_ready, map_done = (sem(n) for n in ("oh_ready", "rank_done", "map_ready", "map_done"))
        oha_ready, part_ready, group_ready = sem("oha_ready"), sem("part_ready"), sem("group_ready")
        rows_ready = sem("rows_ready")
        win_in, wout_in = [[sem(f"{n}{layer}") for layer in (0, 1)] for n in ("win_in", "wout_in")]
        win_hi, win_lo, wout_hi, wout_lo = [[sem(f"{n}{layer}") for layer in (0, 1)] for n in (
            "win_hi", "win_lo", "wout_hi", "wout_lo")]
        g0_in = [sem(f"g0_in{s}") for s in range(2 * CT)]
        s0_out = [sem(f"s0_out{s}") for s in range(2 * CT)]
        xt0_done, xt0_hi, xt0_lo, hid0_done, gelu_done, hid0_used, h0_hi, h0_lo = (sem(n) for n in (
            "xt0_done", "xt0_hi", "xt0_lo", "hid0_done", "gelu_done", "hid0_used", "h0_hi", "h0_lo"))
        y0_done, y0_evac, ys0_free = sem("y0_done"), sem("y0_evac"), sem("ys0_free")
        y_in = [sem(f"y_in{q}") for q in range(NQ)]
        yk_used, gates_ready, share_done, pool_chain = (sem(n) for n in (
            "yk_used", "gates_ready", "share_done", "pool_chain"))
        evac2_ready, evac2_done = sem("evac2_ready"), sem("evac2_done")
        sc_done, sc_ready, exp_done, pv_done, pv_used = (sem(n) for n in (
            "sc_done", "sc_ready", "exp_done", "pv_done", "pv_used"))
        tab_ready, rows1_back = sem("tab_ready"), sem("rows1_back")
        g1_in = [sem(f"g1_in{p}") for p in range(2)]
        s1_out = [sem(f"s1_out{p}") for p in range(2)]
        xt1_done, xt1_hi, xt1_lo, hid1_done, silu_done = (sem(n) for n in (
            "xt1_done", "xt1_hi", "xt1_lo", "hid1_done", "silu_done"))
        ht1_done, ht1_hi, ht1_lo, y1_done, y1_evac, ys1_free = (sem(n) for n in (
            "ht1_done", "ht1_hi", "ht1_lo", "y1_done", "y1_evac", "ys1_free"))
        fin_ready, fin_out = sem("fin_ready"), sem("fin_out")

        EV1 = {}
        for t in range(NQ + 2):
            for n, q in (("cT", t), ("w", t), ("xT", t - 2), ("gT", t)):
                if 0 <= q < NQ and (n != "w" or t == 0):
                    EV1[n, q] = len(EV1) + 1
        for q in range(NQ):
            for n in ("cT again", "v", "bias"):
                EV1[n, q] = len(EV1) + 1
        def early(t):
            return [t - 3] if 3 <= t < NQ else []

        def late(t):
            return {NQ: [NQ - 3, NQ - 2], NQ + 1: [NQ - 1]}.get(t, [])

        EV2 = {}
        for t in range(NQ + 2):
            for n, q in [("xT2", t), ("pT", t - 1)] + [("xT3", q) for q in early(t) + late(t)]:
                if 0 <= q < NQ:
                    EV2[n, q] = len(EV2) + 1
        VAR, COEF, XN = {}, {}, {}
        for t in range(NQ + 2):
            for order, norms in ((VAR, ((0, t), (1, t - 1))), (COEF, ((1, t - 2), (0, t))), (XN, ((1, t - 2),))):
                for n, q in norms:
                    if 0 <= q < NQ:
                        order[n, q] = len(order) + 1
        for t in range(NQ + 2):
            first, last = ([(3, q) for q in quads] for quads in (early(t), late(t)))
            for order, norms in ((VAR, ((2, t), (3, t - 2))), (COEF, first + [(2, t)] + last),
                                 (XN, [(2, t)] + first + last)):
                for n, q in norms:
                    if 0 <= q < NQ:
                        order[n, q] = len(order) + 1

        def tiles(dram, row0, n):
            return dram[row0:row0 + n * P, :].rearrange("(b p) d -> p b d", p=P)

        TAB_EXPERT, TAB_SPLIT, TAB_LANDED, TAB_NUMBER = range(4)
        w_in_v = w_in.rearrange("e (c p) f -> e p c f", p=P)
        w_out_v = w_out.rearrange("e (c p) d -> e p c d", p=P)
        w1_v = w1.rearrange("e (c p) f -> e p c f", p=P)
        w2_v = w2.rearrange("e (c p) d -> e p c d", p=P)

        def scores_at(q):
            return (PA[:, 0, :], PD[:, 1, :])[q % 2]

        def piece_in(n):
            at = (n % 2) * F1 + (n // 2) * 512
            return slice(at, at + 512)

        def piece_out(n):
            return slice(WIN + n * WOUT1 // PIECES, WIN + (n + 1) * WOUT1 // PIECES)

        def number(engine):
            return engine.value_load(tabi[0:1, TAB_NUMBER, 0:1], min_val=FULL1, max_val=TILES1)

        block = ctx.enter_context(nc.Block())

        @block.sync
        def _(sp):
            for q in range(NQ):
                sp.dma_start(xs[:, q * QB:(q + 1) * QB, :],
                             x[q * QB:(q + 1) * QB].rearrange("b p d -> p b d")).then_inc(x_in[q], 16)
                if q == 0:
                    sp.dma_start(cf[:, :], cf_d).then_inc(cf_in, 16)
                sp.dma_start(cx[:, q * QB:(q + 1) * QB, :],
                             ctxt[q * QB:(q + 1) * QB].rearrange("b p d -> p b d")).then_inc(ctx_in[q], 16)
                if q == 0:
                    sp.dma_start(gts[:, 0:2], g_xattn.partition_broadcast(P)).then_inc(g_in, 16)
                    sp.dma_start(gts[:, 2:4], g_ffn.partition_broadcast(P)).then_inc(g_in, 16)
                    for n, w in enumerate((wq, wk, wvT)):
                        sp.dma_start(wqkv[:, n, :, :], w.rearrange("(c p) d -> p c d", p=P)).then_inc(small_in, 16)
                    for n, b in enumerate((bq, bk)):
                        sp.dma_start(bqk[:, n, :], b).then_inc(small_in, 16)
                    sp.dma_start(bvb[:, :], bv.partition_broadcast(P)).then_inc(small_in, 16)
                    for n, w in enumerate((wg0, wg1T)):
                        sp.dma_start(wg[:, n, :, :], w.rearrange("(c p) e -> p c e", p=P)).then_inc(small_in, 16)
            sp.dma_start(mask8[:, :], mask.rearrange("b o s -> (b o s)").partition_broadcast(P)).then_inc(mask_in, 16)

            def load(layer, wanted, first):
                src, n = ((w_in_v, w_out_v), (w1_v, w2_v))[layer][1 - first], (DC, (FB0, FB1)[layer])[1 - first]
                dst = raw[:, 0:WIN] if first else raw[:, WIN:WIN + (WOUT0, WOUT1)[layer]]
                sp.dma_start(dst.rearrange("p (c f) -> p c f", c=n), src[wanted])\
                    .then_inc((win_in if first else wout_in)[layer], 16)

            load(0, 0, False)
            sp.wait_ge(zero_ready, 1)
            for n in range(K * NQ):
                sp.dma_start(tiles(y_rows[0], n * QN, QB), ys[:, 0:QB, :]).then_inc(zero_out, 16)
            for q in range(NQ):
                sp.wait_ge(xn_ready, XN[1, q])
                sp.dma_start(tiles(xn_rows[0], q * QN, QB), xn[:, q % 2]).then_inc(xn_out0[q % 2], 16)
            sp.wait_ge(ret_done, NQ)
            load(0, 0, True)
            for e in range(1, E):
                for hi, lo, first in ((win_hi[0], win_lo[0], True), (wout_hi[0], wout_lo[0], False)):
                    sp.wait_ge(hi, 2 * e)
                    sp.wait_ge(lo, 2 * e)
                    load(0, e, first)

            def fetch(layer, q):
                for k in range(K):
                    sp.dma_start(yk(layer, q, k), tiles(y_rows[layer], k * T + q * QN, QB)).then_inc(y_in[q], 16)

            for hi, lo, first in ((win_hi[0], win_lo[0], True), (wout_hi[0], wout_lo[0], False)):
                sp.wait_ge(hi, 2 * E)
                sp.wait_ge(lo, 2 * E)
                load(1, 0, first)
            for s in range(2 * CT):
                sp.wait_ge(s0_out[s], 16 * E // 2)
            for q in range(NQ):
                if q >= 2:
                    sp.wait_ge(yk_used, q - 1)
                fetch(0, q)
            for q in range(NQ):
                sp.wait_ge(xn_ready, XN[3, q])
                sp.dma_start(tiles(xn_rows[1], q * QN, QB), xn[:, xn3(q)]).then_inc(xn_out1[xn3(q)], 16)
            sp.wait_ge(tab_ready, 1)
            with sp.Fori(0, TILES1) as j:
                changes = sp.value_load(tabi[0:1, TAB_LANDED, bass.ds(j, 1)], min_val=0, max_val=16 * (E + 1))
                with sp.If(changes > 0):
                    e = sp.value_load(tabi[0:1, TAB_EXPERT, bass.ds(j, 1)], min_val=0, max_val=E - 1)
                    need = sp.value_load(tabi[0:1, TAB_SPLIT, bass.ds(j, 1)], min_val=1,
                                         max_val=PIECES * (TILES1 + 1))
                    for hi, lo, first in ((win_hi[1], win_lo[1], True), (wout_hi[1], wout_lo[1], False)):
                        sp.wait_ge(hi, need)
                        sp.wait_ge(lo, need)
                        load(1, e, first)
            sp.wait_ge(rows1_back, 1)
            for q in range(NQ):
                fetch(1, q)
            for q in range(NQ):
                sp.wait_ge(fin_ready, q + 1)
                sp.dma_start(out[q * QB:(q + 1) * QB].rearrange("b p d -> p b d"),
                             xs[:, q * QB:(q + 1) * QB, :]).then_inc(fin_out, 16)
            sp.wait_ge(fin_out, 16 * NQ)

        @block.gpsimd
        def _(pool):
            pool.memset(ys[:, 0:QB, :], 0.0).then_inc(zero_ready, 1)
            for t in range(NQ):
                pool.wait_ge(ctx_in[t], 16)
                if t >= 2:
                    pool.wait_ge(ret_done, t - 1)
                pool.tensor_tensor(cx2[:, t % 2], cx[:, t * QB:(t + 1) * QB, :], cx[:, t * QB:(t + 1) * QB, :],
                                   ALU.mult).then_inc(sq_ready, 1)
                if t == 0:
                    pool.wait_ge(cf_in, 16)
                    pool.wait_ge(small_in, 16 * 8)
                    for n, wide in enumerate((bq_wide, bk_wide)):
                        for k in range(DC):
                            ins = pool.tensor_tensor(wide[:, k, :], c("ones"),
                                                     bqk[:, n, k:k + 1].broadcast_to([P, P]), ALU.mult)
                    ins.then_inc(wide_ready, 1)

            def gather0(e):
                for t in range(CT):
                    s = (e % 2) * CT + t
                    pool.indirect_dma_start(xg[:, s, :], None, xn_rows[0].ap(), bass.IndirectOffsetOnAxis(
                        ap=row_x[:, e * CT + t:e * CT + t + 1], axis=0)).then_inc(g0_in[s], 16)

            def scatter0(e):
                for t in range(CT):
                    s = (e % 2) * CT + t
                    pool.wait_ge(y0_evac, 2 + e * CT + t + 1)
                    pool.indirect_dma_start(y_rows[0].ap(), bass.IndirectOffsetOnAxis(
                        ap=row_y[:, e * CT + t:e * CT + t + 1], axis=0), ys[:, s, :], None).then_inc(s0_out[s], 16)
                    if e >= 1:
                        pool.wait_ge(s0_out[s - CT if s >= CT else s + CT], 16 * ((e + 1) // 2))
                        pool.sem_inc(ys0_free, 1)

            def group_part(layer):
                pool.wait_ge(oha_ready, layer + 1)
                pool.tensor_tensor(rhs_a[:, :, NA:2 * NA], oha[:, :, :],
                                   c("group1").unsqueeze(2).broadcast_to([P, NG, NA]), ALU.mult)\
                    .then_inc(group_ready, 1)

            def value_bias(q):
                pool.wait_ge(evac_done, EV1["v", q])
                v = vv[:, q * QB:(q + 1) * QB, :]
                pool.tensor_tensor(v, v, bvb[:, :].unsqueeze(1).broadcast_to([P, QB, D]), ALU.add)\
                    .then_inc(v_ready, 1)

            group_part(0)
            pool.wait_ge(rows_ready, 1)
            for n in range(2):
                pool.wait_ge(xn_out0[n], 16 * NQ // 2)
            pool.wait_ge(zero_out, 16 * K * NQ)
            gather0(0)
            gather0(1)
            for q in range(2):
                value_bias(q)
            for e in range(E):
                if e + 2 < E:
                    pool.wait_ge(xt0_done, (e + 1) * PAIRS)
                    gather0(e + 2)
                scatter0(e)

            def share(layer, q):
                pool.wait_ge(y_in[q], 32 * (layer + 1))
                n = q * QB + QB - 1
                rows = [yk(layer, q, k)[:, QB - 1, :] for k in range(K)]
                for k in range(K):
                    ins = pool.tensor_tensor(rows[k], rows[k], gates[layer][:, k * NB + n:k * NB + n + 1]
                                             .broadcast_to([P, D]), ALU.mult)
                for k in range(K):
                    ins.then_inc(pool_chain, 1)
                    pool.wait_ge(pool_chain, (layer * NQ + q) * K + k + 1)
                    ins = pool.tensor_tensor(xs[:, n, :], xs[:, n, :], rows[k], ALU.add)
                ins.then_inc(share_done, 1)

            pool.wait_ge(gates_ready, 1)
            for q in range(NQ):
                share(0, q)
                if q + 2 < NQ:
                    value_bias(q + 2)
            group_part(1)

            def gather1(j):
                pool.indirect_dma_start(xg[:, j % 2, :], None, xn_rows[1].ap(), bass.IndirectOffsetOnAxis(
                    ap=row_x[:, j:j + 1], axis=0)).then_inc(g1_in[j % 2], 16)

            pool.wait_ge(rows_ready, 2)
            for n, parts in ((0, 1), (1, NQ - 1)):
                pool.wait_ge(xn_out1[n], 16 * parts)
            gather1(0)
            gather1(1)

            def scatter1(j):
                pool.wait_ge(y1_evac, 2 + j + 1)
                pool.indirect_dma_start(y_rows[1].ap(), bass.IndirectOffsetOnAxis(ap=row_y[:, j:j + 1], axis=0),
                                        ys[:, j % 2, :], None).then_inc(s1_out[j % 2], 16)

            def free1(j):
                pool.wait_ge(s1_out[j % 2], 16 * (j // 2 + 1))
                pool.sem_inc(ys1_free, 1)

            def ahead1(j):
                if j + 3 < TILES1:
                    pool.wait_ge(xt1_done, j + 2)
                    gather1(j + 3)

            ahead1(-1)
            for j in range(FULL1):
                ahead1(j)
                scatter1(j)
                if j >= 1:
                    free1(j - 1)
            free1(FULL1 - 1)
            pool.wait_ge(tab_ready, 1)
            needed = number(pool)
            for j in range(FULL1, TILES1):
                with pool.If(needed > j):
                    ahead1(j)
                    scatter1(j)
                    free1(j)
            pool.sem_inc(rows1_back, 1)
            pool.wait_ge(gates_ready, 2)
            for q in range(NQ):
                share(1, q)

        @block.scalar
        def _(act):
            act.wait_ge(g_in, 32)
            act.activation(tg[:, :], gts[:, :], ACT.Tanh).then_inc(tanh_ready, 1)
            act.wait_ge(cf_in, 16)

            def root(n, q):
                act.wait_ge(var_ready, VAR[n, q])
                m = place(n, q)
                act.activation(sd[:, m, :], mv[:, m, :, 1], ACT.Sqrt, bias=c("eps")).then_inc(sd_ready, 1)

            def normalise(n, q, dst):
                act.wait_ge(coef_ready, COEF[n, q])
                for b in range(QB):
                    ins = act.activation(dst[:, b, :], xs[:, q * QB + b, :], ACT.Identity,
                                         scale=rstd[:, place(n, q), b:b + 1], bias=nmr[:, place(n, q), b:b + 1])
                ins.then_inc(xn_ready if n else xn0_ready, 1)

            def keys_out(q):
                act.wait_ge(evac_ready, EV1["gT", q])
                for k in range(DC):
                    ins = act.activation(gT[:, k, q * QN:(q + 1) * QN], PC[:, k, :], ACT.Identity,
                                         bias=gbias[:, k:k + 1])
                ins.then_inc(evac_done, 1)

            def context_out(n, q):
                act.wait_ge(evac_ready, EV1[n, q])
                act.activation(context_at(n, q), PB[:, :, :], ACT.Copy).then_inc(evac_done, 1)

            for t in range(NQ + 2):
                if t < NQ and t != 1:
                    root(0, t)
                if t >= 2:
                    q = t - 2
                    if q >= 2:
                        act.wait_ge(xn_out0[q % 2], 16 * (q // 2))
                    normalise(1, q, xn[:, q % 2])
                if 0 <= t - 1 < NQ:
                    keys_out(t - 1)
                if t < NQ:
                    context_out("cT", t)
                if t == 0:
                    normalise(0, 0, xn0[0])
                    root(0, 1)
                    normalise(0, 1, xn0[1])
                    act.wait_ge(evac_ready, EV1["w", 0])
                    act.activation(wkqT, PC[:, :, 0:D], ACT.Copy)
                    act.activation(u_wide, PD[:, 1, 0:DC * P].rearrange("p (c n) -> p c n", c=DC), ACT.Copy)
                    act.activation(c("causal"), PD[:, 1, DC * P:DC * P + P], ACT.Copy)
                    act.activation(gbias[:, :], PD[:, 1, DC * P + P:DC * P + P + DC], ACT.Copy)\
                        .then_inc(evac_done, 1)
                if 1 < t < NQ:
                    normalise(0, t, xn0[t % 2])
                if t >= 2:
                    act.wait_ge(evac_ready, EV1["xT", t - 2])
                    act.activation(xT[:, :, :], PB[:, :, :], ACT.Copy).then_inc(evac_done, 1)
                if 0 <= t - 1 < NQ:
                    root(1, t - 1)
            act.wait_ge(e_arg, 1)
            act.activation(pr[:, :, :], lg[:, :, :], ACT.Exp).then_inc(e_ready, 1)

            def values_out(q):
                act.wait_ge(evac_ready, EV1["v", q])
                act.activation(flat(vv[:, q * QB:(q + 1) * QB, :]), flat(PC[:, :, :]), ACT.Copy)\
                    .then_inc(evac_done, 1)
                act.wait_ge(evac_ready, EV1["bias", q])
                act.activation(bias_at[:, q * QN:(q + 1) * QN], PA[:, q % 2, :], ACT.Copy).then_inc(evac_done, 1)

            def part_part(layer):
                act.wait_ge(oha_ready, layer + 1)
                act.activation(rhs_a[:, :, 0:NA], oha[:, :, :], ACT.Copy, scale=c("part")).then_inc(part_ready, 1)

            context_out("cT again", 0)
            values_out(0)
            context_out("cT again", 1)
            part_part(0)
            values_out(1)

            def win0(e, k):
                act.wait_ge(win_in[0], e * 16 + 16)
                act.activation(whi[:, k * 2 * F0:(k + 1) * 2 * F0], raw[:, k * 2 * F0:(k + 1) * 2 * F0], ACT.Copy)\
                    .then_inc(win_hi[0], 1)

            def wout0(e, k):
                act.wait_ge(wout_in[0], e * 16 + 16)
                act.activation(whi[:, wout_half(k)], raw[:, wout_half(k)], ACT.Copy).then_inc(wout_hi[0], 1)

            def xt0(e, pair):
                act.wait_ge(xt0_done, e * PAIRS + pair + 1)
                act.activation(pair_at(xhi, pair), bank0(pair), ACT.Copy).then_inc(xt0_hi, 1)

            def hid0(e, first=False):
                for s in range(STEPS0 + 1):
                    if s < STEPS0:
                        act.wait_ge(hid0_done, e * STEPS0 + s + 1)
                        act.wait_ge(h0_lo, e * STEPS0 + s + 1)
                        act.activation(ga[:, s % 4, :], (PA, PC)[s % 2][:, 0, 0:HALF], ACT.Gelu)\
                            .then_inc(gelu_done, 1)
                    if s >= 1:
                        act.wait_ge(hid0_used, e * STEPS0 + s + 2)
                        act.activation(hid_at(hhi, s - 1), ga[:, (s - 1) % 4, :], ACT.Copy).then_inc(h0_hi, 1)
                    if s in (1, 3) and not first:
                        wout0(e, s // 2)

            def evac0(par, e, tiles_now):
                for t in tiles_now:
                    act.wait_ge(y0_done, e * CT + t + 1)
                    act.wait_ge(ys0_free, e * CT + t + 1)
                    act.activation(ys[:, par * CT + t, :], PD[:, (par * CT + t) % 2, 0:D], ACT.Copy)\
                        .then_inc(y0_evac, 1)

            def out0(par, e):
                evac0(par, e, [0])
                win0(e + 1, 0)
                xt0(e + 1, 0)
                xt0(e + 1, 1)
                evac0(par, e, [1])
                win0(e + 1, 1)
                evac0(par, e, [2])
                xt0(e + 1, 2)
                evac0(par, e, range(3, CT))

            act.sem_inc(y0_evac, 2)
            for k in range(DC):
                win0(0, k)
            for k in range(2):
                wout0(0, k)
            for pair in range(PAIRS):
                xt0(0, pair)
            hid0(0, first=True)
            out0(0, 0)
            with act.Fori(0, E // 2 - 1) as i:
                for par in (1, 0):
                    e = i * 2 + 2 - par
                    hid0(e)
                    out0(par, e)
            hid0(E - 1)
            evac0(1, E - 1, range(CT))

            def split1(arrived, count, done, pieces):
                act.wait_ge(arrived, count)
                for n in range(PIECES):
                    act.activation(whi[:, pieces(n)], raw[:, pieces(n)], ACT.Copy).then_inc(done, 1)

            context_out("cT again", 2)
            split1(win_in[1], 16, win_hi[1], piece_in)
            values_out(2)
            context_out("cT again", 3)

            def rows_turned(n, q):
                act.wait_ge(evac2_ready, EV2[n, q])
                act.activation(xT[:, :, :], PB[:, :, :], ACT.Copy).then_inc(evac2_done, 1)

            def last_norm(q):
                if q >= 1:
                    act.wait_ge(xn_out1[1], 16 if q < NQ - 1 else 16 * (NQ - 2))
                normalise(3, q, xn[:, xn3(q)])

            for t in range(NQ + 2):
                if t < NQ:
                    root(2, t)
                    normalise(2, t, xn[:, 0])
                if t == 0:
                    values_out(3)
                if 0 <= t - 1 < NQ:
                    q = t - 1
                    act.wait_ge(sc_ready, q + 1)
                    if q >= 2:
                        act.wait_ge(pv_used, q - 1)
                    for b in range(QB):
                        ins = act.activation(prb[:, b, :], scores_at(q)[:, b * S:(b + 1) * S], ACT.Exp,
                                             bias=att[:, q % 2, 1, b:b + 1], scale=SCALE,
                                             accum_out=att[:, q % 2, 2, b:b + 1])
                    ins.then_inc(exp_done, 1)
                if t < NQ:
                    rows_turned("xT2", t)
                if 0 <= t - 1 < NQ:
                    act.wait_ge(evac2_ready, EV2["pT", t - 1])
                    act.activation(pT[:, :, :], PA[:, 1, :].rearrange("p (b s) -> p b s", b=QB), ACT.Copy)\
                        .then_inc(evac2_done, 1)
                for q in late(t):
                    root(3, q)
                for q in early(t) + late(t):
                    last_norm(q)
                for q in early(t + 1):
                    root(3, q)
                for q in (early(t) + late(t))[0:1] if t <= NQ else (NQ - 2, NQ - 1):
                    rows_turned("xT3", q)
            split1(wout_in[1], 16, wout_hi[1], piece_out)
            part_part(1)
            act.wait_ge(e_arg, 2)
            act.activation(rr[:, 1, :], rr[:, 0, :], ACT.Exp).then_inc(e_ready, 1)

            def landed(j):
                return act.value_load(tabi[0:1, TAB_LANDED, bass.ds(j, 1)], min_val=0, max_val=16 * (E + 1))

            def win1(j, count):
                with act.If(count > 0):
                    act.wait_ge(hid1_done, j * 2 + 1)
                    split1(win_in[1], count, win_hi[1], piece_in)
                with act.Else():
                    act.drain().then_inc(win_hi[1], PIECES)

            def wout1(j, count):
                with act.If(count > 0):
                    act.wait_ge(y1_done, j + 1)
                    split1(wout_in[1], count, wout_hi[1], piece_out)
                with act.Else():
                    act.drain().then_inc(wout_hi[1], PIECES)

            def xt1(par, j):
                act.wait_ge(xt1_done, j + 1)
                act.activation(xhi[:, par, 0:D], PB[:, par, 0:D], ACT.Copy).then_inc(xt1_hi, 1)

            def silu1(j):
                for f in range(2):
                    act.wait_ge(hid1_done, j * 2 + f + 2)
                    act.activation(h1[:, f * 512:(f + 1) * 512], PA[:, f, :], ACT.Silu).then_inc(silu_done, 1)

            def turn1(j):
                for n in range(2):
                    act.wait_ge(ht1_done, j * 2 + n + 1)
                    act.activation(hhi[:, n * 512:(n + 1) * 512], PC[:, n, :], ACT.Copy).then_inc(ht1_hi, 1)

            def step(par, j, more=2):
                of_j = landed(j)
                of_next = landed(j + 2) if more == 2 else None
                turn1(j)
                wout1(j, of_j)
                if more >= 1:
                    silu1(j + 1)
                if more >= 2:
                    win1(j + 2, of_next)
                    xt1(par, j + 2)

            act.sem_inc(silu_done, 2)
            act.wait_ge(tab_ready, 1)
            needed = number(act)
            win1(0, landed(0))
            xt1(0, 0)
            xt1(1, 1)
            silu1(0)
            win1(1, landed(1))
            with act.Fori(0, FULL1 // 2) as i:
                for par in range(2):
                    step(par, i * 2 + par)
            for j in range(FULL1, TILES1):
                with act.If(needed > j):
                    step(j % 2, j, more=min(2, TILES1 - 1 - j))

        @block.vector
        def _(dve):
            links = [0]

            def link(ins):
                links[0] += 1
                ins.then_inc(chain, 1)
                dve.wait_ge(chain, links[0])

            def norm_stats(n, q):
                for b in range(QB):
                    ins = dve.bn_stats(stats[:, b, :], xs[:, q * QB + b, :])
                link(ins)
                for b in range(QB):
                    ins = dve.bn_aggr(mv[:, place(n, q), b, :], stats[:, b, :])
                link(ins)
                dve.sem_inc(var_ready, 1)

            def coefs(n, q):
                dve.wait_ge(sd_ready, VAR[n, q])
                m = place(n, q)
                link(dve.reciprocal(rstd[:, m, :], sd[:, m, :]))
                link(dve.scalar_tensor_tensor(nmr[:, m, :], mv[:, m, :, 0], -1.0, rstd[:, m, :], ALU.mult, ALU.mult))
                dve.sem_inc(coef_ready, 1)

            for t in range(NQ + 2):
                if t < NQ:
                    dve.wait_ge(x_in[t], 16)
                    norm_stats(0, t)
                if t >= 2:
                    coefs(1, t - 2)
                if t == 0:
                    coefs(0, 0)
                if 0 <= t - 1 < NQ:
                    q = t - 1
                    dve.wait_ge(xn0_ready, q + 1)
                    dve.wait_ge(ret_done, q + 1)
                    if q == 0:
                        dve.wait_ge(tanh_ready, 1)
                    rows = flat(xn0[q % 2])
                    link(dve.scalar_tensor_tensor(rows, rows, tg[:, 0:1], flat(PA[:, :, :]), ALU.mult, ALU.mult))
                    dve.sem_inc(ret_used, 1)
                    if t < NQ:
                        coefs(0, t)
                    xq = flat(xs[:, q * QB:(q + 1) * QB, :])
                    link(dve.tensor_tensor(xq, xq, rows, ALU.add))
                    norm_stats(1, q)

            link(dve.tensor_copy(cb[:, :], cf[:, CF["before"][0]:CF["ones"][1]]))
            dve.sem_inc(cb_ready, 1)

            def best_two(src, tiles):
                for b in tiles:
                    ins = dve.max(top[:, b, :], src[:, b, :])
                link(ins)
                for b in tiles:
                    ins = dve.max_index(topi[:, b, :], top[:, b, :], src[:, b, :])
                link(ins)

            def one_hots():
                link(dve.tensor_copy(eidx[:, :].rearrange("p (k b) -> p k b", k=K),
                                     topi[:, :, 0:K].rearrange("p b k -> p k b")))
                link(dve.tensor_tensor(oh[:, :, :], eidx[:, :].unsqueeze(1).broadcast_to([P, E, NG]),
                                       c("iota_e").unsqueeze(2).broadcast_to([P, E, NG]), ALU.is_equal))
                dve.sem_inc(oh_ready, 1)

            def ranks(layer):
                dve.wait_ge(rank_done, layer + 1)
                totals = PD[:, 1, E * NG:2 * E * NG]
                link(dve.tensor_tensor_scan(flat(incl[:, :, :]), c("reset"), totals, 0.0, ALU.mult, ALU.add))
                link(dve.tensor_tensor(flat(loc[:, :, :]), flat(incl[:, :, :]), totals, ALU.subtract))
                link(dve.tensor_tensor(flat(loc[:, :, :]), flat(loc[:, :, :]), PD[:, 1, 0:E * NG], ALU.add))

            def pick(dst):
                link(dve.tensor_tensor(flat(loc[:, :, :]), flat(loc[:, :, :]), flat(oh[:, :, :]), ALU.mult))
                link(dve.tensor_reduce(dst, loc[:, :, :].rearrange("p e g -> p g e"), AX.X, ALU.add))

            def invert(layer, slot):
                link(dve.tensor_copy(smi[:, 0, :], slot))
                link(dve.tensor_scalar(smi[:, 1, :], smi[:, 0, :], 7, None, ALU.arith_shift_right))
                link(dve.tensor_copy(sm[:, 7, :], smi[:, 1, :]))
                dve.scalar_tensor_tensor(sm[:, 6, :], sm[:, 7, :], float(-P), slot, ALU.mult, ALU.add)
                link(dve.tensor_tensor(oha[:, :, :], sm[:, 7, :].unsqueeze(2).broadcast_to([P, NG, NA]),
                                       c("iota_a").unsqueeze(1).broadcast_to([P, NG, NA]), ALU.is_equal))
                dve.sem_inc(oha_ready, 1)
                link(dve.tensor_tensor(ohb[:, :, :], sm[:, 6, :].unsqueeze(2).broadcast_to([P, NG, P]),
                                       c("iota").unsqueeze(1).broadcast_to([P, NG, P]), ALU.is_equal))
                dve.sem_inc(map_ready, 1)
                if layer == 1:
                    split1(0, wout_hi[1], wout_lo[1], piece_out)
                dve.wait_ge(map_done, layer + 1)
                part, group = PD[:, 0, 128:128 + NA], PD[:, 0, 128 + NA:128 + 2 * NA]
                link(dve.tensor_copy(inv[:, 0, :], group))
                link(dve.scalar_tensor_tensor(inv[:, 1, :], inv[:, 0, :], float(P), part, ALU.mult, ALU.add))
                link(dve.scalar_tensor_tensor(inv[:, 2, :], inv[:, 1, :], float(-P), c("trash"), ALU.add,
                                              ALU.subtract))
                link(dve.scalar_tensor_tensor(inv[:, 3, :], inv[:, 0, :], 1.0, inv[:, 2, :], ALU.min, ALU.mult))
                link(dve.tensor_tensor(row_y[:, :], inv[:, 3, :], c("trash"), ALU.add))
                link(dve.tensor_scalar(row_x[:, :], row_y[:, :], T - 1, None, ALU.bitwise_and))
                dve.sem_inc(rows_ready, 1)

            def over_e(ap):
                return ap.unsqueeze(2).broadcast_to([P, NB, E])

            dve.wait_ge(lg_done, 1)
            logits = PD[:, 0, 0:NB * E].rearrange("p (b e) -> p b e", e=E)
            link(dve.tensor_reduce(rr[:, 0, :], logits, AX.X, ALU.max))
            link(dve.tensor_tensor(lg[:, :, :], logits, over_e(rr[:, 0, :]), ALU.subtract))
            dve.sem_inc(e_arg, 1)
            dve.wait_ge(e_ready, 1)
            link(dve.tensor_reduce(rr[:, 2, :], pr[:, :, :], AX.X, ALU.add))
            link(dve.reciprocal(rr[:, 3, :], rr[:, 2, :]))
            link(dve.tensor_tensor(pr[:, :, :], pr[:, :, :], over_e(rr[:, 3, :]), ALU.mult))
            best_two(pr, range(NB))
            one_hots()
            ranks(0)
            pick(sm[:, 0, :])
            link(dve.tensor_scalar(sm[:, 1, :], sm[:, 0, :], float(CAP), float(64 * P), ALU.is_ge, ALU.mult))
            link(dve.tensor_tensor(sm[:, 2, :], sm[:, 1, :], sm[:, 0, :], ALU.add))
            link(dve.scalar_tensor_tensor(sm[:, 3, :], eidx[:, :], float(CAP), sm[:, 2, :], ALU.mult, ALU.add))
            link(dve.tensor_scalar(full[:, :], incl[:, :, NG - 1], float(CAP - P), None, ALU.is_gt))
            dve.wait_ge(zero_out, 16 * K * NQ)
            invert(0, sm[:, 3, :])
            link(dve.tensor_scalar(sm[:, 4, :], sm[:, 0, :], float(CAP), None, ALU.is_lt))
            link(dve.tensor_tensor(sm[:, 5, :].rearrange("p (k b) -> p k b", k=K),
                                   top[:, :, 0:K].rearrange("p b k -> p k b"),
                                   sm[:, 4, :].rearrange("p (k b) -> p k b", k=K), ALU.mult))
            link(dve.tensor_tensor(rr[:, 0, :], sm[:, 5, 0:NB], sm[:, 5, NB:NG], ALU.add))
            link(dve.tensor_scalar(rr[:, 2, :], rr[:, 0, :], 1e-9, None, ALU.max))
            link(dve.reciprocal(rr[:, 3, :], rr[:, 2, :]))
            link(dve.tensor_scalar(rr[:, 3, :], rr[:, 3, :], tg[:, 2:3], None, ALU.mult))
            for k in range(K):
                ins = dve.tensor_tensor(gates[0][:, k * NB:(k + 1) * NB], sm[:, 5, k * NB:(k + 1) * NB], rr[:, 3, :],
                                        ALU.mult)
            link(ins)
            dve.sem_inc(gates_ready, 1)
            def pad(q):
                dve.wait_ge(evac_done, EV1["bias", q])
                at = bias_at[:, q * QN:(q + 1) * QN]
                dve.scalar_tensor_tensor(at, mask8[:, q * QN:(q + 1) * QN], NEG, at, ALU.mult, ALU.add)\
                    .then_inc(pad_ready, 1)

            dve.wait_ge(mask_in, 16)
            for q in range(2):
                pad(q)

            def win0(e, k):
                dve.wait_ge(win_hi[0], e * DC + k + 1)
                at = slice(k * 2 * F0, (k + 1) * 2 * F0)
                dve.tensor_tensor(wlo[:, at], raw[:, at], whi[:, at].bitcast(F32), ALU.subtract)\
                    .then_inc(win_lo[0], 1)

            def wout0(e, k):
                dve.wait_ge(wout_hi[0], e * 2 + k + 1)
                at = wout_half(k)
                dve.tensor_tensor(wlo[:, at], raw[:, at], whi[:, at].bitcast(F32), ALU.subtract)\
                    .then_inc(wout_lo[0], 1)

            def xt0(e, pair):
                dve.wait_ge(xt0_hi, e * PAIRS + pair + 1)
                dve.tensor_tensor(pair_at(xlo, pair), bank0(pair), pair_at(xhi, pair).bitcast(F32), ALU.subtract)\
                    .then_inc(xt0_lo, 1)

            def hid0(e, first=False):
                for s in range(STEPS0 + 1):
                    if s < STEPS0:
                        dve.wait_ge(gelu_done, e * STEPS0 + s + 1)
                        dve.tensor_tensor(ga[:, s % 4, :], ga[:, s % 4, :], (PA, PC)[s % 2][:, 1, 0:HALF],
                                          ALU.mult).then_inc(hid0_used, 1)
                    if s >= 1:
                        dve.wait_ge(h0_hi, e * STEPS0 + s)
                        dve.tensor_tensor(hid_at(hlo, s - 1), ga[:, (s - 1) % 4, :],
                                          hid_at(hhi, s - 1).bitcast(F32), ALU.subtract).then_inc(h0_lo, 1)
                    if s in (2, 4) and not first:
                        wout0(e, s // 2 - 1)

            def out0(e):
                win0(e + 1, 0)
                xt0(e + 1, 0)
                xt0(e + 1, 1)
                win0(e + 1, 1)
                xt0(e + 1, 2)

            dve.sem_inc(hid0_used, 2)
            dve.sem_inc(h0_lo, 4)
            dve.sem_inc(ys0_free, 2 * CT)
            for k in range(DC):
                win0(0, k)
            for k in range(2):
                wout0(0, k)
            for pair in range(PAIRS):
                xt0(0, pair)
            hid0(0, first=True)
            out0(0)
            with dve.Fori(0, E - 2) as i:
                hid0(i + 1)
                out0(i + 1)
            hid0(E - 1)

            def low(dst, src, hi):
                return dve.tensor_tensor(dst, src, hi.bitcast(F32), ALU.subtract)

            def split1(before_it, hi_done, done, pieces):
                for n in range(PIECES):
                    dve.wait_ge(hi_done, before_it + n + 1)
                    low(wlo[:, pieces(n)], raw[:, pieces(n)], whi[:, pieces(n)]).then_inc(done, 1)

            def combine(layer, q):
                dve.wait_ge(y_in[q], 32 * (layer + 1))
                for k in range(K):
                    for b in range(QB - 1):
                        n = q * QB + b
                        ins = dve.scalar_tensor_tensor(xs[:, n, :], yk(layer, q, k)[:, b, :],
                                                       gates[layer][:, k * NB + n:k * NB + n + 1], xs[:, n, :],
                                                       ALU.mult, ALU.add)
                    link(ins)
                dve.wait_ge(share_done, layer * NQ + q + 1)

            split1(0, win_hi[1], win_lo[1], piece_in)
            def choose(q):
                dve.wait_ge(lg_done, q + 2)
                quad = slice(q * QB, (q + 1) * QB)
                link(dve.tensor_copy(lg[:, quad, :], logits[:, quad, :]))
                dve.sem_inc(lg_used, 1)
                best_two(lg, range(q * QB, (q + 1) * QB))

            for t in range(NQ + 2):
                if t == NQ + 1:
                    choose(0)
                if t < NQ:
                    combine(0, t)
                    dve.sem_inc(yk_used, 1)
                if t < NQ:
                    norm_stats(2, t)
                for q in early(t):
                    coefs(3, q)
                if t < NQ:
                    coefs(2, t)
                if 0 <= t - 1 < NQ:
                    q = t - 1
                    dve.wait_ge(sc_done, q + 1)
                    link(dve.tensor_reduce(att[:, q % 2, 0, :], scores_at(q).rearrange("p (b s) -> p b s", b=QB), AX.X,
                                           ALU.max))
                    link(dve.tensor_scalar(att[:, q % 2, 1, :], att[:, q % 2, 0, :], -SCALE, None, ALU.mult))
                    dve.sem_inc(sc_ready, 1)
                if 0 <= t - 2 < NQ:
                    q = t - 2
                    dve.wait_ge(exp_done, q + 1)
                    link(dve.reciprocal(att[:, q % 2, 3, :], att[:, q % 2, 2, :]))
                    link(dve.tensor_scalar(att[:, q % 2, 3, :], att[:, q % 2, 3, :], tg[:, 1:2], None, ALU.mult))
                    dve.wait_ge(pv_done, q + 1)
                    for b in range(QB):
                        xb = xs[:, q * QB + b, :]
                        ins = dve.scalar_tensor_tensor(xb, PC[:, b // 2, (b % 2) * D:(b % 2 + 1) * D],
                                                       att[:, q % 2, 3, b:b + 1], xb, ALU.mult, ALU.add)
                    link(ins)
                    dve.sem_inc(pv_used, 1)
                    norm_stats(3, q)
                for q in late(t):
                    coefs(3, q)
                if t + 2 in (2, 3):
                    pad(t + 2)

            for q in range(1, NQ):
                choose(q)
            one_hots()
            ranks(1)
            link(dve.tensor_scalar(tei[:, 0, :], incl[:, :, NG - 1], float(P - 1), None, ALU.add))
            link(dve.tensor_scalar(tei[:, 1, :], tei[:, 0, :], 7, None, ALU.arith_shift_right))
            link(dve.tensor_copy(te[:, 0, :], tei[:, 1, :]))
            link(dve.tensor_tensor_scan(te[:, 1, :], c("ones")[:, 0:E], te[:, 0, :], 0.0, ALU.mult, ALU.add))
            link(dve.tensor_tensor(te[:, 2, :], te[:, 1, :], te[:, 0, :], ALU.subtract))
            link(dve.tensor_scalar(te[:, 3, :], te[:, 2, :], float(P), None, ALU.mult))
            link(dve.tensor_tensor(loc[:, :, :], loc[:, :, :], te[:, 3, :].unsqueeze(2).broadcast_to([P, E, NG]),
                                   ALU.add))
            pick(sm[:, 0, :])
            invert(1, sm[:, 0, :])
            over_a = c("iota_a").unsqueeze(2).broadcast_to([P, NA, E])
            ends, starts = (te[:, n, :].unsqueeze(1).broadcast_to([P, NA, E]) for n in (1, 2))
            link(dve.tensor_tensor(tab, over_a, ends, ALU.is_ge))
            link(dve.tensor_reduce(tabf[:, 0, :], tab, AX.X, ALU.add))
            link(dve.tensor_scalar(tabi[:, TAB_EXPERT, :], tabf[:, 0, :], float(E - 1), None, ALU.min))
            link(dve.tensor_tensor(tab, over_a, starts, ALU.is_ge))
            link(dve.tensor_tensor(tab, tab, starts, ALU.mult))
            link(dve.tensor_reduce(tabf[:, 1, :], tab, AX.X, ALU.max))
            link(dve.tensor_tensor(tabf[:, 2, :], tabf[:, 1, :], c("iota_a"), ALU.is_equal))
            link(dve.tensor_scalar(tabf[:, 2, 0:1], te[:, 1, 0:1], 0.0, None, ALU.is_equal))
            dve.memset(tabf[:, 3, 0:1], 1.0)
            link(dve.tensor_scalar(tabf[:, 3, 1:NA], tabf[:, 1, 0:NA - 1], 2.0, None, ALU.add))
            link(dve.tensor_scalar(tabi[:, TAB_SPLIT, :], tabf[:, 3, :], float(PIECES), None, ALU.mult))
            link(dve.tensor_tensor_scan(tabf[:, 4, :], c("ones")[:, 0:NA], tabf[:, 2, :], 1.0, ALU.mult, ALU.add))
            link(dve.scalar_tensor_tensor(tabi[:, TAB_LANDED, :], tabf[:, 4, :], 16.0, tabf[:, 2, :], ALU.mult,
                                          ALU.mult))
            link(dve.tensor_copy(tabi[:, TAB_NUMBER, 0:1], te[:, 1, E - 1:E]))
            dve.sem_inc(tab_ready, 1)
            link(dve.tensor_tensor(rr[:, 0, :], top[:, :, 1], top[:, :, 0], ALU.subtract))
            dve.sem_inc(e_arg, 1)
            dve.wait_ge(e_ready, 2)
            link(dve.tensor_scalar(rr[:, 2, :], rr[:, 1, :], 1.0, None, ALU.add))
            link(dve.reciprocal(rr[:, 3, :], rr[:, 2, :]))
            link(dve.tensor_scalar(gates[1][:, 0:NB], rr[:, 3, :], tg[:, 3:4], None, ALU.mult))
            link(dve.tensor_tensor(gates[1][:, NB:NG], gates[1][:, 0:NB], rr[:, 1, :], ALU.mult))
            dve.sem_inc(gates_ready, 1)

            def landed(j):
                return dve.value_load(tabi[0:1, TAB_LANDED, bass.ds(j, 1)], min_val=0, max_val=16 * (E + 1))

            def win1(j, new):
                with dve.If(new > 0):
                    split1(j * PIECES + PIECES, win_hi[1], win_lo[1], piece_in)
                with dve.Else():
                    dve.drain().then_inc(win_lo[1], PIECES)

            def wout1(j, new):
                with dve.If(new > 0):
                    split1(j * PIECES + PIECES, wout_hi[1], wout_lo[1], piece_out)
                with dve.Else():
                    dve.drain().then_inc(wout_lo[1], PIECES)

            def xt1(par, j):
                dve.wait_ge(xt1_hi, j + 1)
                low(xlo[:, par, 0:D], PB[:, par, 0:D], xhi[:, par, 0:D]).then_inc(xt1_lo, 1)

            def evac1(par, j):
                dve.wait_ge(y1_done, j + 2)
                dve.wait_ge(ys1_free, j + 1)
                dve.tensor_copy(ys[:, par, :], PD[:, par, 0:D]).then_inc(y1_evac, 1)

            def step(par, j, more=True, last=True):
                of_j = landed(j)
                of_next = landed(j + 2) if more else None
                if last:
                    evac1(1 - par, j - 1)
                for n in range(2):
                    dve.wait_ge(ht1_hi, j * 2 + n + 1)
                    at = slice(n * 512, (n + 1) * 512)
                    low(hlo[:, at], PC[:, n, :], hhi[:, at]).then_inc(ht1_lo, 1)
                wout1(j, of_j)
                if more:
                    win1(j + 2, of_next)
                    xt1(par, j + 2)

            needed = number(dve)
            dve.sem_inc(xt1_lo, 2)
            dve.sem_inc(ht1_lo, 2)
            dve.sem_inc(y1_evac, 2)
            dve.sem_inc(ys1_free, 2)
            win1(0, landed(0))
            xt1(0, 0)
            xt1(1, 1)
            win1(1, landed(1))
            step(0, 0, last=False)
            with dve.Fori(0, FULL1 // 2 - 1) as i:
                for par in (1, 0):
                    step(par, i * 2 + 2 - par)
            step(1, FULL1 - 1)
            evac1(1, FULL1 - 1)
            for j in range(FULL1, TILES1):
                with dve.If(needed > j):
                    step(j % 2, j, more=j + 2 < TILES1, last=False)
                    evac1(j % 2, j)

            for q in range(NQ):
                combine(1, q)
                dve.sem_inc(fin_ready, 1)

        @block.tensor
        def _(pe):
            def turn(src):
                for k in range(DC):
                    for b in range(QB):
                        mm = pe.transpose(PB[:, k, b * P:(b + 1) * P], src[:, b, k * P:(k + 1) * P], ident)
                return mm

            def product(dst, lhs, rhs):
                for k, (a, b) in enumerate(zip(lhs, rhs)):
                    mm = pe.matmul(dst, a, b, start=(k == 0), stop=(k == len(lhs) - 1))
                return mm

            def router(layer, q):
                if layer == 1 and q >= 1:
                    pe.wait_ge(lg_used, q)
                for b in range(QB):
                    mm = product(PD[:, 0, (q * QB + b) * E:(q * QB + b + 1) * E],
                                 [xT[:, k, b * P:(b + 1) * P] for k in range(DC)],
                                 [wg[:, layer, k, :] for k in range(DC)])
                if layer == 1 or q == NQ - 1:
                    mm.then_inc(lg_done, 1)

            pe.wait_ge(cf_in, 16)
            def retention(q):
                pe.wait_ge(sq_ready, q + 1)
                if q >= 1:
                    pe.wait_ge(ret_used, q)
                for n in range(2):
                    mm = pe.matmul(PA[:, n, :], decay, flat(cx2[:, q % 2, 2 * n:2 * n + 2, :]), start=True, stop=True)
                mm.then_inc(ret_done, 1)

            def weights():
                pe.wait_ge(small_in, 16 * 8)
                pe.wait_ge(wide_ready, 1)
                w_q, w_k = wqkv[:, 0], wqkv[:, 1]
                at = [slice(k * P, (k + 1) * P) for k in range(DC)]
                for k in range(DC):
                    product(PC[:, k, 0:D], [w_k[:, m, at[k]] for m in range(DC)], [w_q[:, m, :] for m in range(DC)])
                    product(PD[:, 1, at[k]], [w_k[:, m, at[k]] for m in range(DC)],
                            [bq_wide[:, m, :] for m in range(DC)])
                product(PD[:, 1, DC * P:DC * P + P], [bq_wide[:, m, :] for m in range(DC)] + [ident],
                        [bk_wide[:, m, :] for m in range(DC)] + [c("causal")])
                for k in range(DC):
                    mm = product(PD[:, 1, DC * P + P + k:DC * P + P + k + 1], [w_q[:, m, at[k]] for m in range(DC)],
                                 [bqk[:, 1, m:m + 1] for m in range(DC)])
                mm.then_inc(evac_ready, 1)

            def context(n, q):
                pe.wait_ge(ctx_in[q], 16)
                if n == "cT" and q >= 1:
                    pe.wait_ge(evac_done, EV1["xT", q - 3] if q >= 3 else EV1["cT", q - 1])
                elif n == "cT again":
                    pe.wait_ge(evac_done, EV1[n, q] - 1)
                turn(cx[:, q * QB:(q + 1) * QB, :]).then_inc(evac_ready, 1)

            def keys(q):
                pe.wait_ge(evac_done, max(EV1["cT", q], EV1["w", 0], EV1.get(("gT", q - 1), 0)))
                cT = context_at("cT", q)
                for m in range(DC):
                    mm = product(PC[:, m, :], [wkqT[:, k, m * P:(m + 1) * P] for k in range(DC)],
                                 [cT[:, k, :] for k in range(DC)])
                mm.then_inc(evac_ready, 1)

            def values(q):
                pe.wait_ge(evac_done, EV1["cT again", q])
                cT = context_at("cT again", q)
                for b in range(QB):
                    mm = product(PC[:, b // 2, (b % 2) * D:(b % 2 + 1) * D],
                                 [cT[:, k, b * P:(b + 1) * P] for k in range(DC)],
                                 [wqkv[:, 2, k, :] for k in range(DC)])
                mm.then_inc(evac_ready, 1)
                if q == 0:
                    pe.wait_ge(ret_used, NQ)
                product(PA[:, q % 2, :], [u_wide[:, k, :] for k in range(DC)] + [ident],
                        [cT[:, k, :] for k in range(DC)] +
                        [c("causal").unsqueeze(1).broadcast_to([P, QB, S])]).then_inc(evac_ready, 1)

            for t in range(NQ + 2):
                if t < NQ:
                    context("cT", t)
                    retention(t)
                if t == 0:
                    weights()
                if t >= 2:
                    q = t - 2
                    pe.wait_ge(xn_ready, XN[1, q])
                    if t < NQ:
                        pe.wait_ge(evac_done, EV1["cT", t])
                    else:
                        pe.wait_ge(evac_done, EV1["xT", q - 1])
                    turn(xn[:, q % 2]).then_inc(evac_ready, 1)
                if t < NQ:
                    keys(t)
                if t >= 2:
                    pe.wait_ge(evac_done, EV1["xT", t - 2])
                    router(0, t - 2)

            def ranks(layer):
                pe.wait_ge(oh_ready, layer + 1)
                pe.matmul(PD[:, 1, 0:E * NG], before, flat(oh[:, :, :]), start=True, stop=True)
                pe.matmul(PD[:, 1, E * NG:2 * E * NG], ones_b, flat(oh[:, :, :]), start=True, stop=True)\
                    .then_inc(rank_done, 1)

            def invert(layer):
                for ready in (map_ready, part_ready, group_ready):
                    pe.wait_ge(ready, layer + 1)
                for g in range(NG):
                    mm = pe.matmul(PD[:, 0, 128:128 + 2 * NA], ohb[:, g, :], rhs_a[:, g, :], start=(g == 0),
                                   stop=(g == NG - 1))
                mm.then_inc(map_done, 1)

            context("cT again", 0)
            pe.wait_ge(cb_ready, 1)
            ranks(0)
            values(0)
            context("cT again", 1)
            invert(0)
            values(1)

            def exact(dst, lhs_hi, lhs_lo, rhs_hi, rhs_lo, first=True, last=True):
                n = len(lhs_hi)
                for k in range(n):
                    for a, b in ((lhs_hi, rhs_hi), (lhs_hi, rhs_lo), (lhs_lo, rhs_hi)):
                        mm = pe.matmul(dst, a[k], b[k], start=(first and k == 0 and a is lhs_hi and b is rhs_hi),
                                       stop=(last and k == n - 1 and a is lhs_lo))
                return mm

            def xt0(i, par, e, pair):
                if pair == 2:
                    pe.wait_ge(xt0_lo, e * PAIRS + 1)
                for t in tiles_of(pair):
                    s = par * CT + t
                    pe.wait_ge(g0_in[s], i * 16 + 16)
                    for k in range(DC):
                        mm = pe.transpose(bank0(pair)[:, t % 2, k, :], xg[:, s, k * P:(k + 1) * P], ident)
                mm.then_inc(xt0_done, 1)

            def hid0(e, width):
                for s in range(STEPS0):
                    half, fb = divmod(s, FB0)
                    pe.wait_ge(xt0_lo, e * PAIRS + PAIRS - 1 + half)
                    pe.wait_ge(hid0_used, e * STEPS0 + s + 1)
                    for n in range(2):
                        col = n * F0 + fb * P
                        for k in range(DC):
                            if s == 0 and n == 0:
                                pe.wait_ge(win_lo[0], e * DC + k + 1)
                            mm = exact((PA, PC)[s % 2][:, n, 0:width],
                                       *([w[:, col + k * 2 * F0:col + k * 2 * F0 + P]] for w in (whi, wlo)),
                                       *([v[:, k, half * width:(half + 1) * width]] for v in (xhi, xlo)),
                                       first=k == 0, last=k == DC - 1)
                    mm.then_inc(hid0_done, 1)

            def out0(par, e, width, tiles_now):
                for t in tiles_now:
                    pe.wait_ge(wout_lo[0], e * 2 + 2)
                    steps = FB0 if (t + 1) * P <= width else STEPS0
                    pe.wait_ge(h0_lo, e * STEPS0 + steps + 4)
                    pe.wait_ge(y0_evac, e * CT + t + 1)
                    bank = PD[:, (par * CT + t) % 2, 0:D]
                    if t * P < 2 * width:
                        at = t * P + (HALF - width) * (t * P // width)
                        exact(bank, *([h[:, f * CAP + at:f * CAP + at + P] for f in range(FB0)] for h in (hhi, hlo)),
                              *([w[:, WIN + f * D:WIN + (f + 1) * D] for f in range(FB0)] for w in (whi, wlo)))\
                            .then_inc(y0_done, 1)
                    else:
                        pe.matmul(bank, hhi[:, 0:P], whi[:, WIN:WIN + D], start=True, stop=True).then_inc(y0_done, 1)

            def expert0(i, par, e, more=True):
                def run(width):
                    hid0(e, width)
                    out0(par, e, width, [0])
                    if more:
                        xt0(i + par, 1 - par, e + 1, 0)
                        xt0(i + par, 1 - par, e + 1, 1)
                    out0(par, e, width, [1, 2])
                    if more:
                        xt0(i + par, 1 - par, e + 1, 2)
                    out0(par, e, width, range(3, CT))

                with pe.If(pe.value_load(full[0:1, bass.ds(e, 1)], min_val=0, max_val=1) > 0):
                    run(HALF)
                with pe.Else():
                    run((CAP - P) // 2)

            pe.wait_ge(evac_done, EV1["bias", 1])
            for pair in range(PAIRS):
                xt0(0, 0, 0, pair)
            with pe.Fori(0, E // 2 - 1) as i:
                for par in range(2):
                    expert0(i, par, i * 2 + par)
            for par in range(2):
                expert0(E // 2 - 1, par, E - 2 + par, more=par == 0)

            pe.wait_ge(hid0_used, E * STEPS0 + 2)
            for q in range(2, NQ):
                context("cT again", q)
                values(q)
            def last_turn(q):
                pe.wait_ge(xn_ready, XN[3, q])
                turn(xn[:, xn3(q)]).then_inc(evac2_ready, 1)

            def last_router(q):
                pe.wait_ge(evac2_done, EV2["xT3", q])
                router(1, q)

            for t in range(NQ + 2):
                if t <= NQ:
                    for q in early(t - 1):
                        last_router(q)
                if t < NQ:
                    pe.wait_ge(xn_ready, XN[2, t])
                    turn(xn[:, 0]).then_inc(evac2_ready, 1)
                if 0 <= t - 1 < NQ:
                    q = t - 1
                    pe.wait_ge(exp_done, q + 1)
                    if q >= 1:
                        pe.wait_ge(evac2_done, EV2["pT", q - 1])
                    for b in range(QB):
                        mm = pe.transpose(PA[:, 1, b * S:(b + 1) * S], prb[:, b, :], ident)
                    mm.then_inc(evac2_ready, 1)
                if t < NQ:
                    pe.wait_ge(evac2_done, EV2["xT2", t])
                    if t == 0:
                        pe.wait_ge(evac_done, EV1["bias", 3])
                    pe.wait_ge(pad_ready, t + 1)
                    if t >= 2:
                        pe.wait_ge(exp_done, t - 1)
                    for b in range(QB):
                        n = (t * QB + b) * S
                        mm = product(scores_at(t)[:, b * S:(b + 1) * S],
                                     [xT[:, k, b * P:(b + 1) * P] for k in range(DC)] + [ident],
                                     [gT[:, k, n:n + S] for k in range(DC)] + [bias_at[:, n:n + S]])
                    mm.then_inc(sc_done, 1)
                for q in early(t):
                    last_turn(q)
                if 0 <= t - 1 < NQ:
                    q = t - 1
                    pe.wait_ge(evac2_done, EV2["pT", q])
                    if q >= 1:
                        pe.wait_ge(pv_used, q)
                    pe.wait_ge(v_ready, q + 1)
                    for b in range(QB):
                        mm = pe.matmul(PC[:, b // 2, (b % 2) * D:(b % 2 + 1) * D], pT[:, b, :], vv[:, q * QB + b, :],
                                       start=True, stop=True)
                    mm.then_inc(pv_done, 1)
                for q in late(t):
                    last_turn(q)
                    last_router(q)
            ranks(1)
            invert(1)

            def xt1(i, par, j):
                pe.wait_ge(g1_in[par], i * 16 + 16)
                pe.wait_ge(xt1_lo, j + 1)
                for k in range(DC):
                    mm = pe.transpose(PB[:, par, k * P:(k + 1) * P], xg[:, par, k * P:(k + 1) * P], ident)
                mm.then_inc(xt1_done, 1)

            def hid1(par, j):
                pe.wait_ge(xt1_lo, j + 3)
                for f in range(2):
                    pe.wait_ge(win_lo[1], (j + 1) * PIECES + 2 * f + 2)
                    pe.wait_ge(silu_done, j * 2 + f + 1)
                    exact(PA[:, f, :], *([v[:, par, k * P:(k + 1) * P] for k in range(DC)] for v in (xhi, xlo)),
                          *([w[:, k * F1 + f * 512:k * F1 + (f + 1) * 512] for k in range(DC)] for w in (whi, wlo)))\
                        .then_inc(hid1_done, 1)

            def turn1(j):
                for n in range(2):
                    pe.wait_ge(silu_done, j * 2 + n + 3)
                    pe.wait_ge(ht1_lo, j * 2 + n + 1)
                    for b in range(4):
                        f = n * 4 + b
                        mm = pe.transpose(PC[:, n, b * P:(b + 1) * P], h1[:, f * P:(f + 1) * P], ident)
                    mm.then_inc(ht1_done, 1)

            def out1(par, j):
                pe.wait_ge(ht1_lo, j * 2 + 4)
                pe.wait_ge(y1_evac, j + 1)
                per = FB1 // PIECES
                for n in range(PIECES):
                    pe.wait_ge(wout_lo[1], (j + 1) * PIECES + n + 1)
                    mm = exact(PD[:, par, 0:D], *([h[:, f * P:(f + 1) * P] for f in range(n * per, (n + 1) * per)]
                                                  for h in (hhi, hlo)),
                               *([w[:, WIN + f * D:WIN + (f + 1) * D] for f in range(n * per, (n + 1) * per)]
                                 for w in (whi, wlo)), first=n == 0, last=n == PIECES - 1)
                mm.then_inc(y1_done, 1)

            pe.sem_inc(y1_done, 1)
            pe.sem_inc(hid1_done, 1)
            pe.wait_ge(tab_ready, 1)
            needed = number(pe)
            xt1(0, 0, 0)
            xt1(0, 1, 1)
            hid1(0, 0)
            with pe.Fori(0, FULL1 // 2) as i:
                for par in range(2):
                    j = i * 2 + par
                    turn1(j)
                    hid1(1 - par, j + 1)
                    xt1(i + 1, par, j + 2)
                    out1(par, j)
            for j in range(FULL1, TILES1):
                with pe.If(needed > j):
                    turn1(j)
                    if j + 1 < TILES1:
                        hid1((j + 1) % 2, j + 1)
                    if j + 2 < TILES1:
                        xt1(j // 2 + 1, j % 2, j + 2)
                    out1(j % 2, j)


def flat(ap):
    return ap.rearrange("p a b -> p (a b)")


def kernel(**inputs):
    import concourse.bacc as bacc
    from concourse.bass_utils import run_bass_kernel_spmd

    nc = bacc.Bacc("TRN2", target_bir_lowering=False, num_devices=1)
    arrays, args = {}, []

    def give(name, a):
        a = np.ascontiguousarray(a)
        arrays[name] = a
        args.append(nc.dram_tensor(name, a.shape, mybir.dt.from_np(a.dtype), kind="ExternalInput").ap())

    for name in ("x", "ctx_1024", "mask_Bx1xS2_bk0", "g_xattn", "g_ffn", "L0_ffn_Wg", "L0_ffn_W_in", "L0_ffn_W_out"):
        give(name, inputs[name])
    for m in "qkv":
        w = np.asarray(inputs[f"L1_xattn_W{m}"])
        give(f"w{m}", w.T if m == "v" else w)
        b = np.asarray(inputs[f"L1_xattn_b{m}"])
        give(f"b{m}", b if m == "v" else b.reshape(DC, P).T)
    give("gate_wT", np.asarray(inputs["L1_ffn_gate_w"]).T)
    give("w1", inputs["L1_ffn_w1"])
    give("w2", inputs["L1_ffn_w2"])
    give("tables", constants())
    out = nc.dram_tensor("out", (NB, S, D), F32, kind="ExternalOutput").ap()
    build(nc, *args, out)
    r = run_bass_kernel_spmd(nc, [arrays], core_ids=[0])
    return r.results[0]["out"]
```
